# Optimizing a Trainium2 kernel written in Bass

```python
import numpy as np
import jax
import jax.numpy as jnp

def _softmax(x, axis=-1):
    return jax.nn.softmax(x, axis=axis)

def _gelu(x):
    return jax.nn.gelu(x, approximate=True)

def _silu(x):
    return jax.nn.silu(x)

def _sigmoid(x):
    return jax.nn.sigmoid(x)

def _layernorm(x, axis=-1, eps=1e-05):
    m = jnp.mean(x, axis=axis, keepdims=True)
    v = jnp.var(x, axis=axis, keepdims=True)
    return (x - m) / jnp.sqrt(v + eps)

def _scatter_add(tgt, idx, src, axis=0):
    return tgt.at[idx].add(src)

def _segment_sum(src, seg, n):
    return jax.ops.segment_sum(src, seg, n)
kernel_name = 'mk_gnn_ffn_d2_gnn_r32_9950d2'

def setup_inputs(seed: int=0):
    np.random.seed(seed)
    _w = jnp.asarray

    def _rec_inputs():
        import jax
        import jax.numpy as jnp
        _gk = jax.random.key(seed)
        x = -0.0003713 + 1 * jax.random.normal(jax.random.fold_in(_gk, 1), (3125, 256), jnp.float32)
        src = jax.random.randint(jax.random.fold_in(_gk, 2), (50000,), 0, 3125, jnp.int32)
        dst = jnp.minimum((3125 * jax.random.uniform(jax.random.fold_in(_gk, 3), (50000,)) ** 2.0).astype(jnp.int32), 99999)
        _o = jnp.argsort(dst, stable=True)
        src = src[_o]
        dst = dst[_o]
        edge_type_8 = jax.random.randint(jax.random.fold_in(_gk, 13), (50000,), 0, 8, jnp.int32)
        edge_weight = jax.random.uniform(jax.random.fold_in(_gk, 14), (50000,), jnp.float32, 0.0, 1)
        return (x, src, dst, edge_type_8, edge_weight)
    x, src, dst, edge_type_8, edge_weight = _rec_inputs()

    def _L0_gnn_setup():
        import jax, jax.numpy as jnp
        import numpy as np
        N_NODES = 50000
        N_EDGES = 25000
        IN_FEAT = 256
        OUT_FEAT = 256
        NUM_RELS = 8
        NUM_BASES = 8
        SUBMAT_IN = IN_FEAT // NUM_BASES
        SUBMAT_OUT = OUT_FEAT // NUM_BASES
        key = jax.random.key(seed)
        k_h, k_w, k_src, k_dst, k_rel, k_norm = jax.random.split(key, 6)
        h = jax.random.normal(k_h, (N_NODES, IN_FEAT), dtype=jnp.float32)
        weight = jax.random.normal(k_w, (NUM_RELS, NUM_BASES * SUBMAT_IN * SUBMAT_OUT), dtype=jnp.float32) * 0.05
        edge_src = jax.random.randint(k_src, (N_EDGES,), 0, N_NODES, dtype=jnp.int32)
        edge_dst = jax.random.randint(k_dst, (N_EDGES,), 0, N_NODES, dtype=jnp.int32)
        edge_rel = jax.random.randint(k_rel, (N_EDGES,), 0, NUM_RELS, dtype=jnp.int32)
        edge_norm = jax.random.uniform(k_norm, (N_EDGES,), dtype=jnp.float32)
        return {'h': h, 'weight': weight, 'edge_src': edge_src, 'edge_dst': edge_dst, 'edge_rel': edge_rel, 'edge_norm': edge_norm}
    _L0_gnn_all = _L0_gnn_setup()
    _L0_gnn_in = {k: v for k, v in _L0_gnn_all.items() if k in ('weight',)}
    del _L0_gnn_all

    def _L0_ffn_setup():
        import jax, jax.numpy as jnp
        import numpy as np
        E = 8
        K = 2
        D = 256
        H = 512
        DOUT = 256
        EPS = 1e-05
        key = jax.random.key(seed)
        ks = jax.random.split(key, 9)
        s = 0.02
        return {'x': jax.random.normal(ks[0], (4, 256, D), jnp.float32), 'gamma': 1.0 + 0.05 * jax.random.normal(ks[1], (D,), jnp.float32), 'beta': 0.05 * jax.random.normal(ks[2], (D,), jnp.float32), 'Wr': 0.01 * jax.random.normal(ks[3], (D, E), jnp.float32), 'br': jnp.zeros((E,), jnp.float32), 'W1': s * jax.random.normal(ks[4], (E, D, H), jnp.float32), 'b1': s * jax.random.normal(ks[5], (E, H), jnp.float32), 'W2': s * jax.random.normal(ks[6], (E, H, DOUT), jnp.float32), 'b2': s * jax.random.normal(ks[7], (E, DOUT), jnp.float32)}
    _L0_ffn_all = _L0_ffn_setup()
    _L0_ffn_in = {k: v for k, v in _L0_ffn_all.items() if k in ('gamma', 'beta', 'Wr', 'br', 'W1', 'b1', 'W2', 'b2')}
    del _L0_ffn_all

    def _L1_gnn_setup():
        import jax, jax.numpy as jnp
        import numpy as np
        N = 50000
        E = 25000
        IN_F = 256
        OUT_F = 64
        NHEAD = 4
        ALPHA = 0.2

        def _gat_forward(x, W, a_l, a_r, edge):
            n = x.shape[0]
            row, col = (edge[0], edge[1])
            h = (x @ W).reshape(n, NHEAD, OUT_F)
            hl = jnp.sum(a_l * h, axis=-1)
            hr = jnp.sum(a_r * h, axis=-1)
            e = jax.nn.leaky_relu(hl[row] + hr[col], negative_slope=ALPHA)
            e_max = jax.ops.segment_max(e, row, num_segments=n)
            e_max = jnp.where(jnp.isfinite(e_max), e_max, 0.0)
            ee = jnp.exp(e - e_max[row])
            denom = jax.ops.segment_sum(ee, row, num_segments=n)
            att = ee / denom[row]
            msg = att[:, :, None] * h[col]
            out_h = jax.ops.segment_sum(msg, row, num_segments=n)
            return out_h.reshape(n, NHEAD * OUT_F)
        key = jax.random.key(seed)
        k1, k2, k3, k4, k5 = jax.random.split(key, 5)
        x = jax.random.normal(k1, (N, IN_F), dtype=jnp.float32)
        edge = jax.random.randint(k2, (2, E), 0, N, dtype=jnp.int32)
        stdv_W = float(np.sqrt(6.0 / (IN_F + OUT_F * NHEAD)))
        W = jax.random.uniform(k3, (IN_F, OUT_F * NHEAD), jnp.float32, -stdv_W, stdv_W)
        stdv_a = float(np.sqrt(6.0 / (NHEAD + OUT_F)))
        a_l = jax.random.uniform(k4, (1, NHEAD, OUT_F), jnp.float32, -stdv_a, stdv_a)
        a_r = jax.random.uniform(k5, (1, NHEAD, OUT_F), jnp.float32, -stdv_a, stdv_a)
        return {'x': x, 'edge': edge, 'W': W, 'a_l': a_l, 'a_r': a_r}
    _L1_gnn_all = _L1_gnn_setup()
    _L1_gnn_in = {k: v for k, v in _L1_gnn_all.items() if k in ('W', 'a_l', 'a_r')}
    del _L1_gnn_all

    def _L1_ffn_setup():
        import jax, jax.numpy as jnp
        import numpy as np
        BN_EPS = 0.001

        def _bn(h, g, b, m, v):
            return g * (h - m) * jax.lax.rsqrt(v + BN_EPS) + b
        key = jax.random.key(seed)
        ks = jax.random.split(key, 8)
        B, F, Df = (256, 64, 256)
        E, H, D = (8, 256, 256)
        s1 = 1.0 / np.sqrt(Df)
        s2 = 1.0 / np.sqrt(H)
        return {'x': jax.random.normal(ks[0], (B, F, Df), jnp.float32), 'Wr': jax.random.normal(ks[1], (Df, E), jnp.float32) * s1, 'br': jnp.zeros((E,), jnp.float32), 'W1': jax.random.normal(ks[2], (E, Df, H), jnp.float32) * s1, 'b1': jnp.zeros((E, H), jnp.float32), 'g1': jnp.ones((E, H), jnp.float32), 'be1': jnp.zeros((E, H), jnp.float32), 'm1': jnp.zeros((E, H), jnp.float32), 'v1': jnp.ones((E, H), jnp.float32), 'W2': jax.random.normal(ks[3], (E, H, H), jnp.float32) * s2, 'b2': jnp.zeros((E, H), jnp.float32), 'g2': jnp.ones((E, H), jnp.float32), 'be2': jnp.zeros((E, H), jnp.float32), 'm2': jnp.zeros((E, H), jnp.float32), 'v2': jnp.ones((E, H), jnp.float32), 'Wo': jax.random.normal(ks[4], (E, H, D), jnp.float32) * s2, 'bo': jnp.zeros((E, D), jnp.float32)}
    _L1_ffn_all = _L1_ffn_setup()
    _L1_ffn_in = {k: v for k, v in _L1_ffn_all.items() if k in ('Wr', 'br', 'W1', 'b1', 'g1', 'be1', 'm1', 'v1', 'W2', 'b2', 'g2', 'be2', 'm2', 'v2', 'Wo', 'bo')}
    del _L1_ffn_all
    return {'x': x, 'src': src, 'dst': dst, 'edge_type_8': edge_type_8, 'edge_weight': edge_weight, 'L0_gnn_weight': _L0_gnn_in['weight'], 'L0_ffn_gamma': _L0_ffn_in['gamma'], 'L0_ffn_beta': _L0_ffn_in['beta'], 'L0_ffn_Wr': _L0_ffn_in['Wr'], 'L0_ffn_br': _L0_ffn_in['br'], 'L0_ffn_W1': _L0_ffn_in['W1'], 'L0_ffn_b1': _L0_ffn_in['b1'], 'L0_ffn_W2': _L0_ffn_in['W2'], 'L0_ffn_b2': _L0_ffn_in['b2'], 'L1_gnn_W': _L1_gnn_in['W'], 'L1_gnn_a_l': _L1_gnn_in['a_l'], 'L1_gnn_a_r': _L1_gnn_in['a_r'], 'L1_ffn_Wr': _L1_ffn_in['Wr'], 'L1_ffn_br': _L1_ffn_in['br'], 'L1_ffn_W1': _L1_ffn_in['W1'], 'L1_ffn_b1': _L1_ffn_in['b1'], 'L1_ffn_g1': _L1_ffn_in['g1'], 'L1_ffn_be1': _L1_ffn_in['be1'], 'L1_ffn_m1': _L1_ffn_in['m1'], 'L1_ffn_v1': _L1_ffn_in['v1'], 'L1_ffn_W2': _L1_ffn_in['W2'], 'L1_ffn_b2': _L1_ffn_in['b2'], 'L1_ffn_g2': _L1_ffn_in['g2'], 'L1_ffn_be2': _L1_ffn_in['be2'], 'L1_ffn_m2': _L1_ffn_in['m2'], 'L1_ffn_v2': _L1_ffn_in['v2'], 'L1_ffn_Wo': _L1_ffn_in['Wo'], 'L1_ffn_bo': _L1_ffn_in['bo']}

def reference(x, src, dst, edge_type_8, edge_weight, L0_gnn_weight, L0_ffn_gamma, L0_ffn_beta, L0_ffn_Wr, L0_ffn_br, L0_ffn_W1, L0_ffn_b1, L0_ffn_W2, L0_ffn_b2, L1_gnn_W, L1_gnn_a_l, L1_gnn_a_r, L1_ffn_Wr, L1_ffn_br, L1_ffn_W1, L1_ffn_b1, L1_ffn_g1, L1_ffn_be1, L1_ffn_m1, L1_ffn_v1, L1_ffn_W2, L1_ffn_b2, L1_ffn_g2, L1_ffn_be2, L1_ffn_m2, L1_ffn_v2, L1_ffn_Wo, L1_ffn_bo):
    import jax
    import jax.numpy as jnp

    def _L0_gnn_ref(h, weight, edge_src, edge_dst, edge_rel, edge_norm):
        import jax, jax.numpy as jnp
        import numpy as np
        N_NODES = 50000
        N_EDGES = 25000
        IN_FEAT = 256
        OUT_FEAT = 256
        NUM_RELS = 8
        NUM_BASES = 8
        SUBMAT_IN = IN_FEAT // NUM_BASES
        SUBMAT_OUT = OUT_FEAT // NUM_BASES
        'RGCNBlockLayer forward (self_loop=False, bias=None, activation=None).\n\n            Per relation r: agg_r[v] = sum_{(u->v) in rel r} norm_e * h[u]\n            then block-diagonal matmul out_r = blockmm(agg_r, W_r); output = sum_r out_r.\n            '
        N, in_feat = h.shape
        R = weight.shape[0]
        msg = h[edge_src] * edge_norm[:, None]
        seg = edge_rel * N + edge_dst
        agg = jax.ops.segment_sum(msg, seg, num_segments=R * N)
        agg = agg.reshape(R, N, NUM_BASES, SUBMAT_IN)
        W = weight.reshape(R, NUM_BASES, SUBMAT_IN, SUBMAT_OUT)
        out = jnp.einsum('rnbi,rbio->nbo', agg, W)
        return out.reshape(N, NUM_BASES * SUBMAT_OUT)

    def _L0_ffn_ref(x, gamma, beta, Wr, br, W1, b1, W2, b2):
        import jax, jax.numpy as jnp
        import numpy as np
        E = 8
        K = 2
        D = 256
        H = 512
        DOUT = 256
        EPS = 1e-05
        mu = jnp.mean(x, axis=-1, keepdims=True)
        var = jnp.mean(jnp.square(x - mu), axis=-1, keepdims=True)
        xn = (x - mu) * jax.lax.rsqrt(var + EPS) * gamma + beta
        logits = jnp.einsum('bsd,de->bse', xn, Wr) + br
        top_vals, top_idx = jax.lax.top_k(logits, K)
        w = jax.nn.softmax(top_vals, axis=-1)
        w_full = jnp.einsum('bsk,bske->bse', w, jax.nn.one_hot(top_idx, E, dtype=w.dtype))
        y = jnp.zeros(x.shape[:-1] + (DOUT,), x.dtype)
        for e in range(E):
            h = jax.nn.gelu(jnp.einsum('bsd,dh->bsh', xn, W1[e]) + b1[e], approximate=False)
            y_e = jnp.einsum('bsh,hd->bsd', h, W2[e]) + b2[e]
            y = y + y_e * w_full[..., e, None]
        return y

    def _L1_gnn_ref(x, edge, W, a_l, a_r):
        import jax, jax.numpy as jnp
        import numpy as np
        N = 50000
        E = 25000
        IN_F = 256
        OUT_F = 64
        NHEAD = 4
        ALPHA = 0.2

        def _gat_forward(x, W, a_l, a_r, edge):
            n = x.shape[0]
            row, col = (edge[0], edge[1])
            h = (x @ W).reshape(n, NHEAD, OUT_F)
            hl = jnp.sum(a_l * h, axis=-1)
            hr = jnp.sum(a_r * h, axis=-1)
            e = jax.nn.leaky_relu(hl[row] + hr[col], negative_slope=ALPHA)
            e_max = jax.ops.segment_max(e, row, num_segments=n)
            e_max = jnp.where(jnp.isfinite(e_max), e_max, 0.0)
            ee = jnp.exp(e - e_max[row])
            denom = jax.ops.segment_sum(ee, row, num_segments=n)
            att = ee / denom[row]
            msg = att[:, :, None] * h[col]
            out_h = jax.ops.segment_sum(msg, row, num_segments=n)
            return out_h.reshape(n, NHEAD * OUT_F)
        return _gat_forward(x, W, a_l, a_r, edge)

    def _L1_ffn_ref(x, Wr, br, W1, b1, g1, be1, m1, v1, W2, b2, g2, be2, m2, v2, Wo, bo):
        import jax, jax.numpy as jnp
        import numpy as np
        BN_EPS = 0.001

        def _bn(h, g, b, m, v):
            return g * (h - m) * jax.lax.rsqrt(v + BN_EPS) + b
        feat = jnp.mean(x, axis=0)
        w = jax.nn.softmax(feat @ Wr + br, axis=-1)
        h = jnp.einsum('bfd,edh->bfeh', x, W1) + b1
        h = jax.nn.relu(_bn(h, g1, be1, m1, v1))
        h = jnp.einsum('bfeh,ehk->bfek', h, W2) + b2
        h = jax.nn.relu(_bn(h, g2, be2, m2, v2))
        y = jnp.einsum('bfeh,ehd->bfed', h, Wo) + bo
        return jnp.einsum('bfed,fe->bfd', y, w)
    edge_index = jnp.stack([src, dst])
    x = x + _L0_gnn_ref(_layernorm(x, axis=-1), L0_gnn_weight, src, dst, edge_type_8, edge_weight)
    x = x + _L0_ffn_ref(_layernorm(x, axis=-1)[None], L0_ffn_gamma, L0_ffn_beta, L0_ffn_Wr, L0_ffn_br, L0_ffn_W1, L0_ffn_b1, L0_ffn_W2, L0_ffn_b2)[0]
    x = x + _L1_gnn_ref(_layernorm(x, axis=-1), edge_index, L1_gnn_W, L1_gnn_a_l, L1_gnn_a_r)
    x = x + _L1_ffn_ref(_layernorm(x, axis=-1)[None], L1_ffn_Wr, L1_ffn_br, L1_ffn_W1, L1_ffn_b1, L1_ffn_g1, L1_ffn_be1, L1_ffn_m1, L1_ffn_v1, L1_ffn_W2, L1_ffn_b2, L1_ffn_g2, L1_ffn_be2, L1_ffn_m2, L1_ffn_v2, L1_ffn_Wo, L1_ffn_bo)[0]
    return x

_drawn_inputs = setup_inputs


def setup_inputs(seed=0):
    import zlib

    import numpy as np

    out = dict(_drawn_inputs(seed))
    spreads = {'L0_ffn_br': (0.0, 0.1),
     'L1_ffn_br': (0.0, 0.616),
     'L1_ffn_b1': (0.0, 0.386),
     'L1_ffn_g1': (1.0, 0.2),
     'L1_ffn_be1': (0.0, 0.415),
     'L1_ffn_m1': (0.0, 0.393),
     'L1_ffn_v1': (1.0, 0.6),
     'L1_ffn_b2': (0.0, 0.285),
     'L1_ffn_g2': (1.0, 0.2),
     'L1_ffn_be2': (0.0, 0.313),
     'L1_ffn_m2': (0.0, 0.281),
     'L1_ffn_v2': (1.0, 0.6),
     'L1_ffn_bo': (0.0, 0.1)}
    factors = {'L0_ffn_gamma': 6.805, 'L0_ffn_beta': 5.415, 'L0_ffn_b1': 8.0, 'L0_ffn_b2': 4.496}
    for name, (base, spread) in spreads.items():
        noise = np.random.default_rng([zlib.crc32(name.encode()), seed]).standard_normal(out[name].shape)
        drawn = base * np.exp(spread * noise) if base else spread * noise
        out[name] = jnp.asarray(drawn.astype(out[name].dtype))
    for name, factor in factors.items():
        out[name] = (out[name] * factor).astype(out[name].dtype)
    return out
```

```python
from contextlib import ExitStack

import concourse.bass as bass
from concourse import mybir

ALU = mybir.AluOpType
ACT = mybir.ActivationFunctionType
AX = mybir.AxisListType.X
F32 = mybir.dt.float32
F16 = mybir.dt.float16
I32 = mybir.dt.int32
RMAX = bass.bass_isa.ReduceOp.max
ds = bass.ds

P = 128
UG = 4
LN_EPS = 1e-5
BN_EPS = 1e-3
SLOPE = 0.2
PIECE = 11


class Steps:

    def __init__(self, eng, sem):
        self.eng, self.sem, self.n = eng, sem, 0

    def done(self, ins):
        ins.then_inc(self.sem, 1)
        self.n = self.n + 1
        return ins

    def settle(self):
        self.eng.wait_ge(self.sem, self.n)

    def enter(self, i, per):
        self.start, self.per = self.n, per
        self.n = i * per + self.start
        self.at = 0

    def leave(self, rounds):
        self.n = self.start + self.per * rounds


def program(nc, x, src, dst, rel, wgt, w_rgcn, gamma, beta, Wr0, br0, W10, b10, W20, b20,
            Wg, a_l, a_r, Wr1, br1, W11, b11, g1, be1, m1, v1, W21, b21, g2, be2, m2, v2, Wo, bo, out):
    N, D = x.shape
    E = src.shape[0]
    NR = w_rgcn.shape[0]
    NX = W10.shape[0]
    H0 = W10.shape[2]
    NH, DH = a_l.shape[1], a_l.shape[2]
    SB = 32
    KD = D // P
    NT = -(-N // P)
    EC = 4 * -(-E // (4 * P))
    T = 2 * UG * -(-(E + NT * (P - 1)) // (2 * UG * P))
    TX = T + UG
    HC = H0 // P
    GT = 5
    NG = NT // GT
    GC = GT * P
    HG = GC // 2
    AGG = D + NH
    ROW = AGG
    WG = D + 2 * NH
    NB = NT
    UNITS = [(0, 1), (2, 3), (4,)]
    YM = len(UNITS) * (NX + 1)
    YT = GT * (NX + 1)
    assert NT % GT == 0 and NR * D == 4 * 512 and D == NH * DH and NX == 8

    table0 = nc.dram_tensor("relation_table", (NT * P * NR, D), F32, kind="Internal").ap()
    table1 = nc.dram_tensor("gat_table", (NT * P, ROW), F32, kind="Internal").ap()
    table_hr = nc.dram_tensor("hr_table", (NT * P, NH), F32, kind="Internal").ap()

    with ExitStack() as ctx:
        def sb(name, shape, dt=F32):
            return ctx.enter_context(nc.sbuf_tensor(name, shape, dt))

        def sem(name):
            return ctx.enter_context(nc.semaphore(name))

        bank = [ctx.enter_context(nc.psum_tensor(f"bank{i}", [P, 512], F32)) for i in range(8)]

        X = sb("X", [P, (NT + 2) * D])
        X3 = X[:, :].rearrange("p (t d) -> p t d", d=D)
        arena = sb("arena", [P, 20480])
        work = sb("work", [P, 11584])
        W_rel = sb("W_rel", [P, KD, NR, P])
        vals = sb("vals", [P, 7, EC])
        slot_f = sb("slot_f", [P, 2, EC])
        tile_f = sb("tile_f", [P, 2, EC])

        ident = sb("ident", [P, P])
        ones = sb("ones", [P, P])
        lower = sb("lower", [P, P])
        iota_p = sb("iota_p", [P, P])
        iota_slot = sb("iota_slot", [P, P], F16)
        iota_tile = sb("iota_tile", [P, T], F16)
        iota_b = sb("iota_b", [P, NB])
        iota_x = sb("iota_x", [P, NX])
        eps_ln = sb("eps_ln", [P, 1])
        eps_bn = sb("eps_bn", [P, 1])

        idx0 = sb("idx0", [P, TX], I32)
        loc0 = sb("loc0", [P, TX])
        wgt0 = sb("wgt0", [P, TX], I32)
        idx1 = sb("idx1", [P, TX], I32)
        loc1 = sb("loc1", [P, TX])
        bucket_row = [sb(f"bucket_row{w}", [1, TX], I32) for w in range(2)]
        stage = sb("stage", [P, 2, UG], I32)
        pause = sb("pause", [P, 2])

        totals = sb("totals", [P, 6, NB])
        tiles_i = sb("tiles_i", [P, 2, NB], I32)
        bc = sb("bc", [P, 4 * D + 2 * NX])
        gamma_b = bc[:, 0:D]
        beta_b = bc[:, D:2 * D]
        al_b = bc[:, 2 * D:3 * D]
        ar_b = bc[:, 3 * D:4 * D]
        br_b = [bc[:, 4 * D:4 * D + NX], bc[:, 4 * D + NX:4 * D + 2 * NX]]
        par = sb("par", [P, 192])
        bn_s = sb("bn_s", [P, 2, 2 * NX])
        bn_t = sb("bn_t", [P, 2, 2 * NX])
        Wr_sb = sb("Wr_sb", [P, 2, KD, NX])
        b2_sb = sb("b2_sb", [NX, 2, D])

        stats = sb("stats", [P, NT, 6])
        mv = sb("mv", [P, NT, 2])
        rstd = sb("rstd", [P, NT + 2])
        nbias = sb("nbias", [P, NT + 2])
        lg = sb("lg", [P, GT, NX])
        top = sb("top", [P, GT, 8])
        topi = sb("topi", [P, GT, 8], mybir.dt.uint32)
        topf = sb("topf", [P, GT, 8])
        gsm = sb("gsm", [P, 4, GT])
        wf = sb("wf", [P, GT, NX])
        wf2 = sb("wf2", [P, GT, NX])
        wT = sb("wT", [NX, GC])

        HRL = sb("HRL", [P, NT, 2 * NH])
        HR = sb("HR", [P, NT * NH])
        shift = sb("shift", [P, 2, NH])
        M = sb("M", [P, (NT) * NH])
        R = sb("R", [P, NT * 2 * NH])
        hre = sb("hre", [P, 2, UG * NH])
        tmx = sb("tmx", [P, 2, UG, NH])
        ez = sb("ez", [P, 4, UG, NH])

        def wk(a, n):
            return work[:, a:a + n]
        tbl = wk(0, NR * D)
        h_t = wk(2048, D)
        hT_t = wk(2304, D)
        ints = [wk(2560 + k * EC, EC).bitcast(I32) for k in range(6)]
        bucket_f = wk(2560 + 6 * EC, EC)
        oh0 = 5312
        tile_oh = [wk(oh0 + u * 528, 208).bitcast(F16) for u in range(4)]
        slot_oh = [wk(oh0 + u * 528 + 208, 320).bitcast(F16) for u in range(4)]
        G = [[wk(7424 + (b * UG + u) * ROW, ROW) for u in range(UG)] for b in range(2)]
        G4 = [wk(7424 + b * UG * ROW, UG * ROW).rearrange("p (u r) -> p u r", r=ROW) for b in range(2)]
        S = [wk(9536 + b * 512, 512).rearrange("p (u r) -> p u r", r=P) for b in range(2)]
        words = wk(9536, 2 * T).bitcast(I32).rearrange("p (a t) -> p a t", a=2)
        wordf = [wk(9536 + 2 * T, T)]
        row_a = work[0:1, 7424:7424 + 4 * D + 2 * NX]
        par_a = wk(8480, P)
        par_b = work[0:64, 8608:8608 + P]
        ST = [wk(10560 + b * 512, 512) for b in range(2)]
        hid = wk(0, 2 * HC * GC).rearrange("p (b c n) -> p b c n", b=2, c=HC)
        xn = wk(5120, GT * D).rearrange("p (t d) -> p t d", d=D)
        xnT = wk(6400, KD * GC)
        Dm = [[wk((b * UG + u) * 512, 512) for u in range(UG)] for b in range(2)]
        ACC = wk(0, NT * AGG)
        tb1 = wk(7424, WG)
        prod = wk(7936, D)

        onehot_b = arena[:, 0:NB * EC]
        onehot_b3 = onehot_b.rearrange("p (b c) -> p b c", c=EC)
        count_b = arena[:, NB * EC:2 * NB * EC]
        count_b3 = count_b.rearrange("p (b c) -> p b c", c=EC)
        W10_sb = arena[:, 0:NX * KD * H0].rearrange("p (e k h) -> p e k h", e=NX, k=KD)
        W20_sb = arena[:, NX * KD * H0:NX * KD * H0 + NX * HC * D].rearrange("p (e k h) -> p e k h", e=NX, k=HC)
        W1_sb = [arena[:, j * NX * KD * D:(j + 1) * NX * KD * D].rearrange("p (e k h) -> p e k h", e=NX, k=KD)
                 for j in range(3)]
        Wg_sb = arena[:, 16384:16384 + KD * WG].rearrange("p (k h) -> p k h", k=KD)

        const_set = sem("const_set")
        pool_step = sem("pool_step")
        vec_step = sem("vec_step")
        act_step = sem("act_step")
        x_in = sem("x_in")
        edges_in = sem("edges_in")
        par_in = sem("par_in")
        wg_in = sem("wg_in")
        w0_in = sem("w0_in")
        w1_in = sem("w1_in")
        par_T = sem("par_T")
        par_ok = sem("par_ok")
        bn_sq = sem("bn_sq")
        bn_v = sem("bn_v")
        t_stats = sem("t_stats")
        t_sqrt = sem("t_sqrt")
        t_rstd = sem("t_rstd")
        t_h = sem("t_h")
        t_tr = sem("t_tr")
        t_hT = sem("t_hT")
        t_mm = sem("t_mm")
        t_ev = [sem(f"t_ev{k}") for k in range(4)]
        t_out = sem("t_out")
        tot_in = sem("tot_in")
        tot_ok = sem("tot_ok")
        oh_ready = [sem(f"oh_ready{u}") for u in range(4)]
        oh_used = [sem(f"oh_used{u}") for u in range(4)]
        order_ok = sem("order_ok")
        staged = sem("staged")
        g_in = [sem(f"g_in{b}") for b in range(2)]
        g_used = [sem(f"g_used{b}") for b in range(2)]
        s_ready = [sem(f"s_ready{b}") for b in range(2)]
        acc_ok = [sem(f"acc_ok{b}") for b in range(2)]
        agg_ok = sem("agg_ok")
        ln_var = sem("ln_var")
        ln_sd = sem("ln_sd")
        xn_ok = sem("xn_ok")
        xn_tr = sem("xn_tr")
        xnT_ok = sem("xnT_ok")
        logit_ok = sem("logit_ok")
        gate_in = sem("gate_in")
        gate_exp = sem("gate_exp")
        gate_ok = sem("gate_ok")
        wT_tr = sem("wT_tr")
        wT_ok = sem("wT_ok")
        hid_mm = sem("hid_mm")
        hid_ok = sem("hid_ok")
        y_mm = sem("y_mm")
        y_ok = sem("y_ok")
        ffn_ok = sem("ffn_ok")
        hrl_ok = sem("hrl_ok")
        wa_ok = sem("wa_ok")
        low_ok = sem("low_ok")
        shift_ok = sem("shift_ok")
        hrt_ok = sem("hrt_ok")
        hrt_out = sem("hrt_out")
        d_ready = [sem(f"d_ready{b}") for b in range(2)]
        m_mm = [sem(f"m_mm{b}") for b in range(2)]
        m_red = [sem(f"m_red{b}") for b in range(2)]
        m_ok = [sem(f"m_ok{b}") for b in range(2)]
        r_ready = sem("r_ready")
        st_tr = [sem(f"st_tr{b}") for b in range(2)]
        st_ok = [sem(f"st_ok{b}") for b in range(2)]
        re_mm = [sem(f"re_mm{b}") for b in range(2)]
        e_in = [sem(f"e_in{b}") for b in range(2)]
        e_exp = [sem(f"e_exp{b}") for b in range(2)]
        msg_ok = [sem(f"msg_ok{b}") for b in range(2)]
        acc2_mm = [sem(f"acc2_mm{b}") for b in range(2)]
        acc2_ok = [sem(f"acc2_ok{b}") for b in range(2)]
        stored = sem("stored")

        LEAD = 1
        led = [hid_ok, y_ok, y_mm, hrl_ok, *t_ev, *oh_used, *g_used, *acc_ok, *m_mm, *m_red, *m_ok, *d_ready,
               *acc2_mm, *acc2_ok, *e_exp, *st_ok, *e_in]
        tails = (idx0, loc0, wgt0, idx1, loc1, *bucket_row)
        NCONST = 14 + 5 + len(tails)
        RB = 16 * (D // SB)
        NPAR = 8 + 2 + 1 + 4 + 2 + 2 + 2
        rounds = T // (2 * UG)
        block = ctx.enter_context(nc.Block())

        @block.sync
        def _(sp):
            full = (NT - 1) * P
            sp.wait_ge(const_set, NCONST)
            sp.dma_start(X3[:, 0:NT - 1, :], x[0:full, :].rearrange("(t p) d -> p t d", p=P)).then_inc(x_in, 16)
            sp.dma_start(X3[0:N - full, NT - 1, :], x[full:N, :]).then_inc(x_in, 16)
            lastp = E // EC
            for k, a in enumerate((dst, src, rel, wgt.bitcast(I32))):
                sp.dma_start(ints[k][0:lastp, :], a[0:lastp * EC].rearrange("(p c) -> p c", c=EC)).then_inc(edges_in, 16)
                sp.dma_start(ints[k][lastp:lastp + 1, 0:E - lastp * EC],
                             a[lastp * EC:E].rearrange("(p c) -> p c", p=1)).then_inc(edges_in, 16)
            for b in range(D // SB):
                q = b % (P // SB)
                sp.dma_start(W_rel[q * SB:(q + 1) * SB, b // (P // SB), :, q * SB:(q + 1) * SB],
                             w_rgcn[:, b * SB * SB:(b + 1) * SB * SB].rearrange("r (i o) -> i r o", o=SB)
                             ).then_inc(t_out, 16)
            for k, a in enumerate((b11, g1, be1, m1, v1, b21, g2, be2)):
                sp.dma_start(par_a[16 * k:16 * k + 16, :], a.rearrange("e (c p) -> (e c) p", p=P)).then_inc(par_in, 16)
            for k, a in enumerate((m2, v2)):
                sp.dma_start(par_b[16 * k:16 * k + 16, :], a.rearrange("e (c p) -> (e c) p", p=P)).then_inc(par_in, 16)
            sp.dma_start(par_b[32:64, :], b10.rearrange("e (c p) -> (e c) p", p=P)).then_inc(par_in, 16)
            for a, o, n in ((gamma, 0, D), (beta, D, D), (br0, 4 * D, NX), (br1, 4 * D + NX, NX)):
                sp.dma_start(row_a[0:1, o:o + n], a.rearrange("(a n) -> a n", a=1)).then_inc(par_in, 16)
            for a, o in ((a_l, 2 * D), (a_r, 3 * D)):
                sp.dma_start(row_a[0:1, o:o + D], a.rearrange("a h d -> a (h d)")).then_inc(par_in, 16)
            for j, a in enumerate((Wr0, Wr1)):
                sp.dma_start(Wr_sb[:, j, :, :], a.rearrange("(k p) e -> p k e", p=P)).then_inc(par_in, 16)
            for j, a in enumerate((b20, bo)):
                sp.dma_start(b2_sb[:, j, :], a).then_inc(par_in, 16)

            with sp.Fori(0, NT) as i:
                for k in range(4):
                    sp.wait_ge(t_ev[k], LEAD + i + 1)
                sp.dma_start(table0[ds(i * (P * NR), P * NR), :].rearrange("(p r) d -> p (r d)", r=NR),
                             tbl).then_inc(t_out, 16)
            sp.wait_ge(tot_ok, 2)
            sp.wait_ge(order_ok, 2)
            for e in range(NX):
                sp.dma_start(W10_sb[:, e], W10[e].rearrange("(k p) h -> p k h", p=P)).then_inc(w0_in, 16)
                sp.dma_start(W20_sb[:, e], W20[e].rearrange("(k p) h -> p k h", p=P)).then_inc(w0_in, 16)
            sp.dma_start(Wg_sb[:, :, 0:D], Wg.rearrange("(k p) h -> p k h", p=P)).then_inc(wg_in, 16)
            sp.wait_ge(y_mm, LEAD + NG * YM)
            for e in range(NX):
                for j, a in enumerate((W11, W21, Wo)):
                    sp.dma_start(W1_sb[j][:, e], a[e].rearrange("(k p) h -> p k h", p=P)).then_inc(w1_in, 16)
            with sp.Fori(0, NT) as i:
                sp.wait_ge(t_ev[0], LEAD + i + (NT + 1))
                sp.dma_start(table1[ds(i * P, P), :], tb1[:, 0:ROW]).then_inc(t_out, 16)
            sp.wait_ge(hrt_ok, 1)
            sp.dma_start(table_hr[:, :].rearrange("(t p) h -> p t h", p=P),
                         HR[:, :].rearrange("p (t h) -> p t h", h=NH)).then_inc(hrt_out, 16)
            with sp.Fori(0, NG - 1) as g:
                sp.wait_ge(y_ok, LEAD + g * YT + (NG + 1) * YT)
                sp.dma_start(out[ds(g * GC, GC), :].rearrange("(t p) d -> p t d", p=P),
                             X3[:, ds(g * GT, GT), :]).then_inc(stored, 16)
            sp.wait_ge(y_ok, LEAD + 2 * NG * YT)
            sp.dma_start(out[(NG - 1) * GC:full, :].rearrange("(t p) d -> p t d", p=P),
                         X3[:, (NG - 1) * GT:NT - 1, :]).then_inc(stored, 16)
            sp.dma_start(out[full:N, :], X3[0:N - full, NT - 1, :]).then_inc(stored, 16)
            sp.wait_ge(stored, 16 * (NG + 1))

        @block.gpsimd
        def _(pool):
            step = Steps(pool, pool_step)
            step.done(pool.memset(ident[:, :], 0.0))
            step.done(pool.memset(lower[:, :], 1.0))
            step.done(pool.memset(pause[:, 0:1], 0.0))
            for s in led:
                pool.sem_inc(s, LEAD)
            pool.memset(ones[:, :], 1.0).then_inc(const_set, 1)
            pool.memset(X[:, (NT - 1) * D:(NT + 2) * D], 0.0).then_inc(const_set, 1)
            pool.memset(ints[0][:, :], -1).then_inc(const_set, 1)
            pool.memset(ints[1][:, :], -1).then_inc(const_set, 1)
            pool.memset(ints[2][:, :], 0).then_inc(const_set, 1)
            pool.memset(ints[3][:, :], 0).then_inc(const_set, 1)
            pool.memset(W_rel[:, :, :, :], 0.0).then_inc(const_set, 1)
            pool.memset(eps_ln[:, :], LN_EPS).then_inc(const_set, 1)
            pool.memset(eps_bn[:, :], BN_EPS).then_inc(const_set, 1)
            for a in (rstd[:, NT:NT + 2], nbias[:, NT:NT + 2], M[:, :], *(a[:, T:TX] for a in tails)):
                pool.memset(a, 0).then_inc(const_set, 1)
            step.settle()
            pool.affine_select(out=ident[:, :], in_=ident[:, :], compare_op=ALU.not_equal, fill=1.0, base=0,
                               pattern=[[-1, P]], channel_multiplier=1).then_inc(const_set, 1)
            pool.affine_select(out=lower[:, :], in_=lower[:, :], compare_op=ALU.is_gt, fill=0.0, base=0,
                               pattern=[[1, P]], channel_multiplier=-1).then_inc(const_set, 1)
            for t, n in ((iota_p, P), (iota_slot, P), (iota_tile, T), (iota_b, NB), (iota_x, NX)):
                pool.iota(t[:, :], pattern=[[1, n]], base=0, channel_multiplier=0,
                          allow_small_or_imprecise_dtypes=True).then_inc(const_set, 1)

            def gathers(idx, table, dest, width, used, used_at, k, b):
                pool.wait_ge(used, LEAD + used_at)
                step.done(pool.tensor_copy(stage[:, b, :], idx[:, ds(k * UG, UG)]))
                step.settle()
                pool.tensor_tensor(pause[:, 0:1], pause[:, 0:1], pause[:, 0:1], ALU.add)
                for u in range(UG):
                    pool.indirect_dma_start(dest[b][u][:, 0:width], None, table,
                                            bass.IndirectOffsetOnAxis(ap=stage[:, b, u:u + 1], axis=0)
                                            ).then_inc(g_in[b], 16)

            pool.wait_ge(t_out, RB + 16 * NT)
            pool.wait_ge(order_ok, 1)
            with pool.Fori(0, rounds) as i:
                step.enter(i, 2)
                for b in range(2):
                    gathers(idx0, table0, G, D, g_used[b], i, i * 2 + b, b)
            step.leave(rounds)
            for b in range(2):
                pool.wait_ge(g_used[b], LEAD + rounds)
            pool.wait_ge(low_ok, 1)
            pool.partition_all_reduce(shift[:, 1, :], shift[:, 0, :], P, RMAX).then_inc(shift_ok, 1)
            pool.wait_ge(hrt_out, 16)
            hre_t = [[hre[:, b, u * NH:(u + 1) * NH] for u in range(UG)] for b in range(2)]
            with pool.Fori(0, rounds) as i:
                step.enter(i, 2)
                for b in range(2):
                    gathers(idx1, table_hr, hre_t, NH, d_ready[b], i, i * 2 + b, b)
            step.leave(rounds)
            for b in range(2):
                pool.wait_ge(d_ready[b], LEAD + rounds)
            pool.wait_ge(t_out, RB + 16 * 2 * NT)
            with pool.Fori(0, rounds) as i:
                step.enter(i, 2)
                for b in range(2):
                    gathers(idx1, table1, G, ROW, acc2_mm[b], i * UG, i * 2 + b, b)
            step.leave(rounds)

        @block.tensor
        def _(pe):
            pe.wait_ge(const_set, NCONST)
            pe.wait_ge(par_in, 16 * NPAR)
            pe.transpose(bank[0][:, 0:P], par_a[:, :], ident[:, :])
            pe.transpose(bank[0][:, P:P + 64], par_b[:, :], ident[0:64, 0:64])
            nrow = 4 * D + 2 * NX
            for k in range(3):
                a, b = 512 * k, min(512 * k + 512, nrow)
                mm = pe.matmul(bank[1 + k][:, 0:b - a], ones[0:1, :], row_a[0:1, a:b], start=True, stop=True)
            mm.then_inc(par_T, 1)

            def turn(tr, h_ready, free):
                pe.wait_ge(h_ready[0], h_ready[1])
                pe.wait_ge(free[0], free[1])
                for k in range(KD):
                    t = pe.transpose(bank[7][:, k * P:(k + 1) * P], h_t[:, k * P:(k + 1) * P], ident[:, :])
                t.then_inc(tr, 1)

            pe.wait_ge(t_h, 1)
            for k in range(KD):
                t = pe.transpose(bank[7][:, k * P:(k + 1) * P], h_t[:, k * P:(k + 1) * P], ident[:, :])
            t.then_inc(t_tr, 1)
            pe.wait_ge(t_out, RB)
            pe.wait_ge(par_ok, 1)
            with pe.Fori(0, NT) as i:
                pe.wait_ge(t_hT, i + 1)
                for k in range(4):
                    pe.wait_ge(t_ev[k], LEAD + i)
                    half, c = k // 2, k % 2
                    pe.matmul(bank[k][:, :], hT_t[:, half * P:(half + 1) * P],
                              W_rel[:, half, 4 * c:4 * c + 4, :].rearrange("p r o -> p (r o)"),
                              start=True, stop=True).then_inc(t_mm, 1)
                turn(t_tr, (t_h, i + 2), (t_hT, i + 1))

            def totals_mm(w):
                pe.wait_ge(tot_in, w + 1)
                pe.matmul(bank[6][:, 0:NB], lower[:, :], totals[:, 0, :], start=True, stop=True)
                pe.matmul(bank[6][:, 32:32 + NB], ones[:, :], totals[:, 0, :], start=True, stop=True
                          ).then_inc(tot_ok, 1)

            def sort_group(w, j, first, last):
                nf = (5, 2)[w]
                for u in range(4):
                    pe.wait_ge(oh_ready[u], j + 1 + w * (EC // 4))
                    for f in range(nf):
                        mm = pe.matmul(bank[f][:, 0:T], slot_oh[u][:, f * P:(f + 1) * P], tile_oh[u],
                                       start=(first and u == 0), stop=(last and u == 3))
                    mm.then_inc(oh_used[u], 1)
                return mm

            for w in range(2):
                totals_mm(w)
                if w == 0:
                    for k in range(4):
                        pe.wait_ge(t_ev[k], LEAD + NT)
                else:
                    pe.wait_ge(order_ok, 1)
                sort_group(w, 0, True, False)
                with pe.Fori(1, EC // 4 - 1) as j:
                    sort_group(w, j, False, False)
                sort_group(w, EC // 4 - 1, False, True)

            pe.wait_ge(order_ok, 2)
            with pe.Fori(0, rounds) as i:
                for b in range(2):
                    pe.wait_ge(g_in[b], i * 64 + 64)
                    pe.wait_ge(s_ready[b], i + 1)
                    pe.wait_ge(acc_ok[b], LEAD + i * UG)
                    for u in range(UG):
                        mm = pe.matmul(bank[2 * b + u // 2][:, (u % 2) * D:(u % 2 + 1) * D], S[b][:, u, :],
                                       G[b][u][:, 0:D], start=True, stop=True)
                    mm.then_inc(g_used[b], 1)

            def experts(layer):
                hn = 2 * 4 * NX
                yb, mb, hb = layer * NG * YT, layer * NG * YM, layer * NG * hn
                yslot = [bank[4 + t // 2][:, (t % 2) * D:(t % 2 + 1) * D] for t in range(GT)]

                def group(g):
                    gg = g + layer * NG
                    pe.wait_ge(xn_ok, gg + 1)
                    pe.wait_ge(hid_ok, LEAD + g * hn + hb)
                    for k in range(KD):
                        for t in range(GT):
                            q = k * GT + t
                            tr = pe.transpose(bank[q // 4][:, (q % 4) * P:(q % 4 + 1) * P],
                                              xn[:, t, k * P:(k + 1) * P], ident[:, :])
                    tr.then_inc(xn_tr, 1)
                    pe.wait_ge(xnT_ok, gg + 1)
                    for t in range(GT):
                        for k in range(KD):
                            mm = pe.matmul(bank[7][:, t * NX:(t + 1) * NX],
                                           xnT[:, k * GC + t * P:k * GC + (t + 1) * P], Wr_sb[:, layer, k, :],
                                           start=(k == 0), stop=(k == KD - 1))
                    mm.then_inc(logit_ok, 1)

                    def hidden(e, c, weights, source):
                        r = 4 * e + c
                        pe.wait_ge(hid_ok, LEAD + g * hn + (hb + max(0, 2 * r - 2)))
                        n = len(weights)
                        for j in range(2):
                            for k in range(n):
                                mm = pe.matmul(bank[2 * (r % 2) + j][:, 0:HG], weights[k], source(k, j),
                                               start=(k == 0), stop=(k == n - 1))
                            mm.then_inc(hid_mm, 1)

                    def x_in_cols(k, j):
                        return xnT[:, k * GC + j * HG:k * GC + (j + 1) * HG]

                    def first(e):
                        if layer == 0:
                            for c in range(HC):
                                hidden(e, c, [W10_sb[:, e, k, c * P:(c + 1) * P] for k in range(KD)], x_in_cols)
                        else:
                            for c in range(KD):
                                hidden(e, c, [W1_sb[0][:, e, k, c * P:(c + 1) * P] for k in range(KD)], x_in_cols)

                    def second(e):
                        pe.wait_ge(hid_ok, LEAD + g * hn + (hb + 8 * e + 4))
                        for c in range(KD):
                            hidden(e, 2 + c, [W1_sb[1][:, e, k, c * P:(c + 1) * P] for k in range(KD)],
                                   lambda k, j: hid[:, e % 2, k, j * HG:(j + 1) * HG])

                    def outs(e):
                        pe.wait_ge(hid_ok, LEAD + g * hn + (hb + 8 * e + 8))
                        ks = range(HC) if layer == 0 else range(2, 4)
                        for q, tiles in enumerate(UNITS):
                            pe.wait_ge(y_ok, LEAD + g * YT + (yb + (GT * (e - 1) + tiles[-1] + 1 if e else 0)))
                            if e == 1 and q == 2:
                                pe.wait_ge(wT_ok, gg + 1)
                            for t in tiles:
                                for k in ks:
                                    w = W20_sb[:, e, k, :] if layer == 0 else W1_sb[2][:, e, k - 2, :]
                                    mm = pe.matmul(yslot[t], hid[:, e % 2, k, t * P:(t + 1) * P], w,
                                                   start=(k == ks[0]), stop=(k == ks[-1]))
                            mm.then_inc(y_mm, 1)

                    first(0)
                    if layer == 1:
                        second(0)
                    for e in range(NX):
                        if e + 1 < NX:
                            first(e + 1)
                        if e == 1:
                            pe.wait_ge(gate_ok, gg + 1)
                            pe.wait_ge(y_ok, LEAD + g * YT + (yb + GT))
                            for t in range(GT):
                                o = bank[7][0:NX, t * P:(t + 1) * P] if t < 4 else bank[6][0:NX, 256:384]
                                tr = pe.transpose(o, wf[:, t, :], ident[:, :])
                            tr.then_inc(wT_tr, 1)
                        outs(e)
                        if layer == 1 and e + 1 < NX:
                            second(e + 1)
                    for q, tiles in enumerate(UNITS):
                        pe.wait_ge(y_ok, LEAD + g * YT + (yb + GT * (NX - 1) + tiles[-1] + 1))
                        for t in tiles:
                            mm = pe.matmul(yslot[t], wT[:, t * P:(t + 1) * P], b2_sb[:, layer, :],
                                           start=True, stop=True)
                        mm.then_inc(y_mm, 1)

                with pe.Fori(0, NG) as g:
                    group(g)

            pe.wait_ge(w0_in, 16 * 2 * NX)
            experts(0)

            pe.wait_ge(wa_ok, 1)
            pe.wait_ge(t_h, NT + 3)
            for k in range(KD):
                tr = pe.transpose(bank[7][:, k * P:(k + 1) * P], h_t[:, k * P:(k + 1) * P], ident[:, :])
            tr.then_inc(t_tr, 1)
            with pe.Fori(0, NT) as i:
                pe.wait_ge(t_hT, i + (NT + 2))
                pe.wait_ge(t_ev[0], LEAD + i + NT)
                for k in range(KD):
                    mm = pe.matmul(bank[0][:, 0:WG], hT_t[:, k * P:(k + 1) * P], Wg_sb[:, k, :],
                                   start=(k == 0), stop=(k == KD - 1))
                mm.then_inc(t_mm, 1)
                turn(t_tr, (t_h, i + (NT + 4)), (t_hT, i + (NT + 2)))

            with pe.Fori(0, rounds) as i:
                for b in range(2):
                    pe.wait_ge(d_ready[b], LEAD + i + 1)
                    pe.wait_ge(s_ready[b], i + (rounds + 2 - b))
                    pe.wait_ge(m_red[b], LEAD + i * UG)
                    for u in range(UG):
                        mm = pe.matmul(bank[4 * b + u][:, :], S[b][:, u, :], Dm[b][u], start=True, stop=True)
                    mm.then_inc(m_mm[b], 1)

            pe.wait_ge(r_ready, 1)
            regs = [pe.alloc_register(f"pe_b{k}") for k in range(2 * UG)]
            with pe.Fori(0, rounds) as i:
                pe.load(regs, bucket_row[1][0:1, ds(i * (2 * UG), 2 * UG)])
                bs = [pe.snap(r, min_val=0, max_val=NB - 1) for r in regs]
                for b in range(2):
                    pe.wait_ge(s_ready[b], i + (2 * (rounds + 1 - b) + 1))
                    pe.wait_ge(st_ok[b], LEAD + i)
                    for u in range(UG):
                        tr = pe.transpose(bank[4 + b][:, u * P:(u + 1) * P], S[b][:, u, :], ident[:, :])
                    tr.then_inc(st_tr[b], 1)
                    pe.wait_ge(st_ok[b], LEAD + i + 1)
                    pe.wait_ge(e_in[b], LEAD + i)
                    for u in range(UG):
                        mm = pe.matmul(bank[6 + b][:, u * 2 * NH:(u + 1) * 2 * NH], ST[b][:, u * P:(u + 1) * P],
                                       R[:, ds(bs[b * UG + u] * (2 * NH), 2 * NH)], start=True, stop=True)
                    mm.then_inc(re_mm[b], 1)
                for b in range(2):
                    pe.wait_ge(msg_ok[b], i + 1)
                    for u in range(UG):
                        pe.wait_ge(acc2_ok[1 - b], LEAD + i * UG + (u + 1 if b else 0))
                        pe.matmul(bank[u][:, 0:AGG], S[b][:, u, :], G[b][u][:, 0:AGG],
                                  start=True, stop=True).then_inc(acc2_mm[b], 1)

            pe.wait_ge(w1_in, 16 * 3 * NX)
            experts(1)


        @block.scalar
        def _(act):
            act.wait_ge(const_set, NCONST)
            act.wait_ge(par_T, 1)
            act.activation(par[:, 0:P + 64], bank[0][:, 0:P + 64], ACT.Copy)
            nrow = 4 * D + 2 * NX
            for k in range(3):
                a, b = 512 * k, min(512 * k + 512, nrow)
                cp = act.activation(bc[:, a:b], bank[1 + k][:, 0:b - a], ACT.Copy)
            cp.then_inc(par_ok, 1)
            act.wait_ge(par_ok, 1)
            for j, c in enumerate((64, 144)):
                act.activation(bn_s[:, j, :], par[:, c:c + 16], ACT.Sqrt, bias=eps_bn[:, 0:1]).then_inc(bn_sq, 1)

            def norm(i):
                act.activation(h_t, X[:, ds(i * D, D)], ACT.Identity, bias=nbias[:, ds(i, 1)],
                               scale=rstd[:, ds(i, 1)]).then_inc(t_h, 1)

            def table(layer):
                tb, hb, nb = layer * (NT + 1), layer * (NT + 1), (4, 1)[layer]

                def turned(i):
                    act.wait_ge(t_tr, i + (tb + 1))
                    act.activation(hT_t, bank[7][:, 0:D], ACT.Copy).then_inc(t_hT, 1)

                def evacuate(i, k):
                    if layer == 0:
                        act.wait_ge(t_mm, i * 4 + (k + 1))
                        o = tbl.rearrange("p (r d) -> p r d", d=D)[:, 4 * (k % 2):4 * (k % 2) + 4,
                                                                   (k // 2) * P:(k // 2 + 1) * P]
                        act.activation(o, bank[k][:, :].rearrange("p (r o) -> p r o", o=P), ACT.Copy).then_inc(t_ev[k], 1)
                    else:
                        act.wait_ge(t_mm, i + (4 * NT + 1))
                        act.wait_ge(hrl_ok, LEAD + i)
                        act.activation(tb1, bank[0][:, 0:WG], ACT.Copy).then_inc(t_ev[0], 1)

                act.wait_ge(t_stats, layer + 1)
                act.activation(rstd[:, 0:NT], mv[:, :, 1], ACT.Sqrt, bias=eps_ln[:, 0:1]).then_inc(t_sqrt, 1)
                act.wait_ge(t_rstd, layer + 1)
                norm(0)
                turned(0)
                act.wait_ge(t_tr, tb + 1)
                norm(1)
                with act.Fori(0, NT) as i:
                    act.wait_ge(t_out, i * 16 + (RB + layer * 16 * NT))
                    for k in range(nb - 1):
                        evacuate(i, k)
                    turned(i + 1)
                    act.wait_ge(t_out, i * 16 + (RB + layer * 16 * NT))
                    norm(i + 2)
                    evacuate(i, nb - 1)

            table(0)

            def experts(layer):
                hn = 2 * 4 * NX
                yb, mb, hb = layer * NG * YT, layer * NG * YM, layer * NG * hn

                def root(j):
                    act.wait_ge(ln_var, j)
                    act.activation(rstd[:, 0:GT], mv[:, 0:GT, 1], ACT.Sqrt, bias=eps_ln[:, 0:1]).then_inc(ln_sd, 1)

                def group(g, last):
                    gg = g + layer * NG
                    nr = 2 - layer
                    act.wait_ge(xn_tr, gg + 1)
                    act.activation(xnT[:, 0:512], bank[0][:, :], ACT.Copy)
                    act.activation(xnT[:, 512:1024], bank[1][:, :], ACT.Copy)
                    act.activation(xnT[:, 1024:KD * GC], bank[2][:, 0:KD * GC - 1024], ACT.Copy).then_inc(xnT_ok, 1)
                    for e in range(NX):
                        act.wait_ge(y_mm, LEAD + g * YM + (mb + (len(UNITS) * (e - 1) if e >= 2 else 0)))
                        for c in range(4):
                            r = 4 * e + c
                            for j in range(2):
                                act.wait_ge(hid_mm, g * hn + (hb + 2 * r + j + 1))
                                o = hid[:, e % 2, c, j * HG:(j + 1) * HG]
                                i_ = bank[2 * (r % 2) + j][:, 0:HG]
                                if layer == 0:
                                    act.activation(o, i_, ACT.Gelu, bias=par[:, 160 + r:161 + r]).then_inc(hid_ok, 1)
                                else:
                                    q = 2 * e + c % 2
                                    act.activation(o, i_, ACT.Relu, bias=bn_t[:, c // 2, q:q + 1],
                                                   scale=bn_s[:, c // 2, q:q + 1]).then_inc(hid_ok, 1)
                            if e == 2 and c == 1:
                                act.wait_ge(wT_tr, gg + 1)
                                act.activation(wT[:, 0:512], bank[7][0:NX, :], ACT.Copy)
                                act.activation(wT[:, 512:GC], bank[6][0:NX, 256:384], ACT.Copy).then_inc(wT_ok, 1)
                        if e == 0:
                            act.wait_ge(gate_in, gg + 1)
                            if layer == 0:
                                act.activation(gsm[:, 1, :], gsm[:, 0, :], ACT.Exp).then_inc(gate_exp, 1)
                            else:
                                act.activation(wf2[:, :, :], lg[:, :, :], ACT.Exp).then_inc(gate_exp, 1)
                        if not last and (e == 4 or (e == 5 and layer == 0)):
                            root(g * nr + (layer * 2 * NG + nr + 1 + (e - 4)))

                for j in range(2 - layer):
                    root(layer * 2 * NG + j + 1)
                with act.Fori(0, NG - 1) as g:
                    group(g, False)
                group(NG - 1, True)

            experts(0)
            table(1)

            with act.Fori(0, rounds) as i:
                for b in range(2):
                    act.wait_ge(g_in[b], i * 64 + 64 * (rounds + 1))
                    act.wait_ge(m_mm[b], LEAD + i)
                    for u in range(UG):
                        for h in range(NH):
                            last = act.activation(Dm[b][u][:, h * P:(h + 1) * P], ident[:, :], ACT.Copy,
                                                  scale=hre[:, b, u * NH + h:u * NH + h + 1])
                    last.then_inc(d_ready[b], 1)

            act.wait_ge(r_ready, 1)
            with act.Fori(0, rounds) as i:
                for b in range(2):
                    act.wait_ge(st_tr[b], i + 1)
                    act.activation(ST[b], bank[4 + b][:, :], ACT.Copy).then_inc(st_ok[b], 1)
                for b in range(2):
                    act.wait_ge(e_in[b], LEAD + i + 1)
                    act.activation(G4[b][:, :, D:AGG], ez[:, 2 * b, :, :], ACT.Exp).then_inc(e_exp[b], 1)

            experts(1)

        @block.vector
        def _(dve):
            step = Steps(dve, vec_step)

            def all_stats(layer):
                for t in range(NT):
                    last = dve.bn_stats(stats[:, t, :], X3[:, t, :])
                step.done(last)
                step.settle()
                for t in range(NT):
                    last = dve.bn_aggr(mv[:, t, :], stats[:, t, :])
                last.then_inc(t_stats, 1)
                dve.wait_ge(t_sqrt, layer + 1)
                step.done(dve.reciprocal(rstd[:, 0:NT], rstd[:, 0:NT]))
                step.settle()
                dve.scalar_tensor_tensor(out=nbias[:, 0:NT], in0=mv[:, :, 0], scalar=-1.0, in1=rstd[:, 0:NT],
                                         op0=ALU.mult, op1=ALU.mult).then_inc(t_rstd, 1)

            dve.wait_ge(const_set, NCONST)
            dve.wait_ge(x_in, 32)
            all_stats(0)

            def keys(w):
                key = ints[w]
                other = ints[1 - w]
                a, b = ints[4], ints[5]
                v3 = [vals[:, (0, 5)[w] + k, :] for k in range((5, 2)[w])]
                step.done(dve.tensor_scalar(a, key, 7, None, ALU.arith_shift_right))
                step.done(dve.tensor_scalar(b, key, P - 1, None, ALU.bitwise_and))
                step.settle()
                step.done(dve.tensor_copy(bucket_f, a))
                step.settle()
                if w == 0:
                    step.done(dve.scalar_tensor_tensor(out=a, in0=other, scalar=float(NR), in1=ints[2],
                                                       op0=ALU.mult, op1=ALU.add))
                    step.settle()
                    step.done(dve.scalar_tensor_tensor(out=a, in0=a, scalar=float(P), in1=b,
                                                       op0=ALU.mult, op1=ALU.add))
                else:
                    step.done(dve.tensor_scalar(b, b, 1.0, None, ALU.add))
                    step.settle()
                    step.done(dve.scalar_tensor_tensor(out=a, in0=other, scalar=float(2 * P), in1=b,
                                                       op0=ALU.mult, op1=ALU.add))
                step.settle()
                mask = (1 << PIECE) - 1
                step.done(dve.tensor_scalar(b, a, mask, None, ALU.bitwise_and))
                step.settle()
                step.done(dve.tensor_copy(v3[0], b))
                step.settle()
                step.done(dve.tensor_scalar(b, a, PIECE, mask, ALU.logical_shift_right, ALU.bitwise_and))
                step.settle()
                step.done(dve.tensor_copy(v3[1], b))
                if w == 0:
                    for k in range(3):
                        step.settle()
                        step.done(dve.tensor_scalar(b, ints[3], PIECE * k, mask, ALU.logical_shift_right, ALU.bitwise_and))
                        step.settle()
                        step.done(dve.tensor_copy(v3[2 + k], b))
                step.done(dve.tensor_tensor(onehot_b3, bucket_f.unsqueeze(1).to_broadcast([P, NB, EC]),
                                            iota_b[:, :].unsqueeze(2).to_broadcast([P, NB, EC]), ALU.is_equal))
                step.settle()
                step.done(dve.tensor_tensor_scan(count_b, ones[:, 0:1].to_broadcast([P, NB * EC]), onehot_b, 0.0,
                                                 ALU.mult, ALU.add))
                step.settle()
                step.done(dve.tensor_copy(totals[:, 0, 0:1], count_b3[:, 0:1, EC - 1]))
                step.done(dve.tensor_copy(totals[:, 1, :], count_b3[:, :, EC - 1]))
                step.settle()
                dve.tensor_tensor(totals[:, 0, 1:NB], totals[:, 1, 1:NB], totals[:, 1, 0:NB - 1],
                                  ALU.subtract).then_inc(tot_in, 1)
                dve.wait_ge(tot_ok, w + 1)
                step.done(dve.tensor_scalar(tiles_i[:, 0, :], bank[6][:, 32:32 + NB], float(P - 1), None, ALU.add))
                step.settle()
                step.done(dve.tensor_scalar(tiles_i[:, 1, :], tiles_i[:, 0, :], 7, None, ALU.arith_shift_right))
                step.settle()
                step.done(dve.tensor_copy(totals[:, 2, :], tiles_i[:, 1, :]))
                step.settle()
                step.done(dve.tensor_tensor_scan(totals[:, 3, :], ones[:, 0:NB], totals[:, 2, :], 0.0,
                                                 ALU.mult, ALU.add))
                step.settle()
                step.done(dve.tensor_tensor(totals[:, 4, :], totals[:, 3, :], totals[:, 2, :], ALU.subtract))
                step.settle()
                step.done(dve.scalar_tensor_tensor(out=totals[:, 5, :], in0=totals[:, 4, :], scalar=float(P),
                                                   in1=bank[6][:, 0:NB], op0=ALU.mult, op1=ALU.add))
                step.settle()
                step.done(dve.tensor_tensor(totals[:, 5, 1:NB], totals[:, 5, 1:NB], totals[:, 1, 0:NB - 1],
                                            ALU.subtract))
                step.settle()
                step.done(dve.tensor_tensor(count_b3, count_b3,
                                            totals[:, 5, :].unsqueeze(2).to_broadcast([P, NB, EC]), ALU.add))
                step.settle()
                step.done(dve.tensor_tensor(onehot_b, onehot_b, count_b, ALU.mult))
                step.settle()
                step.done(dve.tensor_reduce(bucket_f, onehot_b.rearrange("p (b c) -> p c b", c=EC), AX, ALU.add))
                step.settle()
                step.done(dve.tensor_scalar(a, bucket_f, -1.0, None, ALU.add))
                step.settle()
                step.done(dve.tensor_scalar(b, a, P - 1, None, ALU.bitwise_and))
                step.settle()
                step.done(dve.tensor_copy(slot_f[:, w, :], b))
                step.settle()
                step.done(dve.tensor_scalar(b, a, 7, None, ALU.arith_shift_right))
                step.settle()
                step.done(dve.tensor_copy(tile_f[:, w, :], b))
                at = arena[0:1, 0:T * (NB - 1)].rearrange("p (t b) -> p t b", b=NB - 1)
                row = arena[0:1, T * NB:T * NB + T]
                step.done(dve.tensor_tensor(at, iota_tile[0:1, :].unsqueeze(2).to_broadcast([1, T, NB - 1]),
                                            totals[0:1, 4, 1:NB].unsqueeze(1).to_broadcast([1, T, NB - 1]), ALU.is_ge))
                step.settle()
                step.done(dve.tensor_reduce(row, at, AX, ALU.add))
                step.settle()
                step.done(dve.tensor_copy(bucket_row[w][:, 0:T], row))
                step.settle()

            def place(w):
                nf = (5, 2)[w]
                f0 = (0, 5)[w]

                def group(j):
                    for u in range(4):
                        c = j * 4 + u
                        dve.wait_ge(oh_used[u], LEAD + j + w * (EC // 4))
                        dve.tensor_scalar(tile_oh[u], iota_tile[:, :], tile_f[:, w, ds(c, 1)], None, ALU.is_equal)
                        for f in range(nf):
                            last = dve.tensor_scalar(slot_oh[u][:, f * P:(f + 1) * P], iota_slot[:, :],
                                                     slot_f[:, w, ds(c, 1)], vals[:, f0 + f, ds(c, 1)],
                                                     ALU.is_equal, ALU.mult)
                        last.then_inc(oh_ready[u], 1)

                with dve.Fori(0, EC // 4) as j:
                    group(j)
                for u in range(4):
                    dve.wait_ge(oh_used[u], LEAD + (w + 1) * (EC // 4))

                step.done(dve.tensor_copy(wordf[0], bank[0][:, 0:T]))
                step.settle()
                step.done(dve.scalar_tensor_tensor(out=words[:, 0, :], in0=bank[1][:, 0:T], scalar=float(1 << PIECE),
                                                   in1=wordf[0], op0=ALU.mult, op1=ALU.add))
                step.settle()
                if w == 0:
                    step.done(dve.tensor_scalar(idx0[:, 0:T], words[:, 0, :], 7, None, ALU.logical_shift_right))
                    step.done(dve.tensor_scalar(words[:, 1, :], words[:, 0, :], P - 1, None, ALU.bitwise_and))
                    step.settle()
                    step.done(dve.tensor_copy(loc0[:, 0:T], words[:, 1, :]))
                    step.done(dve.tensor_copy(wordf[0], bank[2][:, 0:T]))
                    step.settle()
                    step.done(dve.scalar_tensor_tensor(out=words[:, 0, :], in0=bank[3][:, 0:T],
                                                       scalar=float(1 << PIECE), in1=wordf[0],
                                                       op0=ALU.mult, op1=ALU.add))
                    step.done(dve.tensor_copy(words[:, 1, :], bank[4][:, 0:T]))
                    step.settle()
                    step.done(dve.tensor_scalar(words[:, 1, :], words[:, 1, :], 2 * PIECE, None,
                                                ALU.logical_shift_left))
                    step.settle()
                    dve.tensor_tensor(wgt0[:, 0:T], words[:, 0, :], words[:, 1, :], ALU.bitwise_or
                                      ).then_inc(order_ok, 1)
                else:
                    step.done(dve.tensor_scalar(idx1[:, 0:T], words[:, 0, :], 8, None, ALU.logical_shift_right))
                    step.done(dve.tensor_scalar(words[:, 1, :], words[:, 0, :], 2 * P - 1, None, ALU.bitwise_and))
                    step.settle()
                    dve.tensor_scalar(loc1[:, 0:T], words[:, 1, :], -1.0, None, ALU.add).then_inc(order_ok, 1)

            dve.wait_ge(edges_in, 16 * 8)
            for w in range(2):
                keys(w)
                place(w)
            dve.wait_ge(bn_sq, 2)
            step.done(dve.reciprocal(bn_s[:, :, :], bn_s[:, :, :]))
            step.settle()
            for j, (cb, cg, cbe, cm) in enumerate(((0, 16, 32, 48), (80, 96, 112, 128))):
                step.done(dve.tensor_tensor(bn_s[:, j, :], bn_s[:, j, :], par[:, cg:cg + 16], ALU.mult))
                step.done(dve.tensor_tensor(bn_t[:, j, :], par[:, cb:cb + 16], par[:, cm:cm + 16], ALU.subtract))
                step.settle()
                step.done(dve.tensor_tensor(bn_t[:, j, :], bn_t[:, j, :], bn_s[:, j, :], ALU.mult))
                step.settle()
                step.done(dve.tensor_tensor(bn_t[:, j, :], bn_t[:, j, :], par[:, cbe:cbe + 16], ALU.add))

            regs = [dve.alloc_register(f"dve_b{k}") for k in range(2 * UG)]

            def buckets(w, i):
                dve.load(regs, bucket_row[w][0:1, ds(i * (2 * UG), 2 * UG)])
                return [dve.snap(r, min_val=0, max_val=NB - 1) for r in regs]

            dve.wait_ge(order_ok, 2)
            wgt0_f = wgt0[:, :].bitcast(F32)

            def weighted(i, off, b, used_at):
                if used_at is not None:
                    dve.wait_ge(g_used[b], LEAD + used_at)
                for u in range(UG):
                    c = i * (2 * UG) + (off * UG + u)
                    last = dve.tensor_scalar(S[b][:, u, :], iota_p[:, :], loc0[:, ds(c, 1)], wgt0_f[:, ds(c, 1)],
                                             ALU.is_equal, ALU.mult)
                last.then_inc(s_ready[b], 1)

            def add_up(i, b, bs, got, got_at, ok, view, target, width):
                for u in range(UG):
                    dve.wait_ge(got[b], LEAD + got_at(i, u))
                    if u:
                        dve.wait_ge(ok[b], LEAD + i * UG + u)
                    elif b:
                        dve.wait_ge(ok[0], LEAD + i * UG + UG)
                    else:
                        dve.wait_ge(ok[1], LEAD + i * UG)
                    t = target[:, ds(bs[b * UG + u] * width, width)]
                    dve.tensor_tensor(t, t, view(b, u), ALU.add).then_inc(ok[b], 1)

            weighted(0, 0, 0, None)
            with dve.Fori(0, rounds) as i:
                bs = buckets(0, i)
                def view(b, u):
                    return bank[2 * b + u // 2][:, (u % 2) * D:(u % 2 + 1) * D]
                weighted(i, 1, 1, i)
                add_up(i, 0, bs, g_used, lambda i, u: i + 1, acc_ok, view, X[:, :], D)
                weighted(i, 2, 0, i + 1)
                add_up(i, 1, bs, g_used, lambda i, u: i + 1, acc_ok, view, X[:, :], D)
            for b in range(2):
                dve.wait_ge(acc_ok[b], LEAD + rounds * UG)

            def experts(layer):
                yb, mb = layer * NG * YT, layer * NG * YM
                yslot = [bank[4 + t // 2][:, (t % 2) * D:(t % 2 + 1) * D] for t in range(GT)]
                nr = 2 - layer

                def ln(g, first):
                    gg = g + layer * NG
                    if not first:
                        dve.wait_ge(xn_tr, gg)
                    for k in range(nr):
                        for t in range(GT):
                            src_ = X[:, ds((g * GT + t) * D, D)] if k == 0 else xn[:, t, :]
                            last = dve.bn_stats(stats[:, t, :], src_)
                        step.done(last)
                        step.settle()
                        dve.memset(pause[:, 1:2], 0.0)
                        for t in range(GT):
                            last = dve.bn_aggr(mv[:, t, :], stats[:, t, :])
                        last.then_inc(ln_var, 1)
                        dve.wait_ge(ln_sd, g * nr + (layer * 2 * NG + k + 1))
                        step.done(dve.reciprocal(rstd[:, 0:GT], rstd[:, 0:GT]))
                        step.settle()
                        for t in range(GT):
                            src_ = X[:, ds((g * GT + t) * D, D)] if k == 0 else xn[:, t, :]
                            last = dve.tensor_scalar(xn[:, t, :], src_, mv[:, t, 0:1], rstd[:, t:t + 1],
                                                     ALU.subtract, ALU.mult)
                            if k < nr - 1 or layer == 0:
                                step.done(last)
                        if k < nr - 1 or layer == 0:
                            step.settle()
                    if layer == 0:
                        step.done(dve.tensor_tensor(xn, xn, gamma_b.unsqueeze(1).to_broadcast([P, GT, D]), ALU.mult))
                        step.settle()
                        last = dve.tensor_tensor(xn, xn, beta_b.unsqueeze(1).to_broadcast([P, GT, D]), ALU.add)
                    last.then_inc(xn_ok, 1)
                ln_steps = 2 * (2 + GT) + 1 if layer == 0 else 2

                def gates(g):
                    gg = g + layer * NG
                    n0 = step.n
                    dve.wait_ge(logit_ok, gg + 1)
                    logits = bank[7][:, 0:GT * NX].rearrange("p (t e) -> p t e", e=NX)
                    step.done(dve.tensor_tensor(lg[:, :, :], logits,
                                                br_b[layer].unsqueeze(1).to_broadcast([P, GT, NX]), ALU.add))
                    step.settle()
                    if layer == 0:
                        dve.memset(pause[:, 1:2], 0.0)
                        for t in range(GT):
                            step.done(dve.max(top[:, t, :], lg[:, t, :]))
                        step.settle()
                        dve.memset(pause[:, 1:2], 0.0)
                        for t in range(GT):
                            step.done(dve.max_index(topi[:, t, :], top[:, t, :], lg[:, t, :]))
                        step.settle()
                        step.done(dve.tensor_copy(topf[:, :, :], topi[:, :, :]))
                        dve.tensor_tensor(gsm[:, 0, :], top[:, :, 1], top[:, :, 0], ALU.subtract).then_inc(gate_in, 1)
                        dve.wait_ge(gate_exp, gg + 1)
                        step.done(dve.tensor_scalar(gsm[:, 2, :], gsm[:, 1, :], 1.0, None, ALU.add))
                        step.settle()
                        step.done(dve.reciprocal(gsm[:, 3, :], gsm[:, 2, :]))
                        step.settle()
                        step.done(dve.tensor_tensor(gsm[:, 0, :], gsm[:, 1, :], gsm[:, 3, :], ALU.mult))
                        step.settle()
                        for t in range(GT):
                            step.done(dve.tensor_scalar(wf[:, t, :], iota_x[:, :], topf[:, t, 0:1],
                                                        gsm[:, 3, t:t + 1], ALU.is_equal, ALU.mult))
                            step.done(dve.tensor_scalar(wf2[:, t, :], iota_x[:, :], topf[:, t, 1:2],
                                                        gsm[:, 0, t:t + 1], ALU.is_equal, ALU.mult))
                        step.settle()
                        dve.tensor_tensor(wf[:, :, :], wf[:, :, :], wf2[:, :, :], ALU.add).then_inc(gate_ok, 1)
                    else:
                        step.done(dve.tensor_reduce(gsm[:, 0, :], lg[:, :, :], AX, ALU.max))
                        step.settle()
                        dve.tensor_tensor(lg[:, :, :], lg[:, :, :],
                                          gsm[:, 0, :].unsqueeze(2).to_broadcast([P, GT, NX]),
                                          ALU.subtract).then_inc(gate_in, 1)
                        dve.wait_ge(gate_exp, gg + 1)
                        step.done(dve.tensor_reduce(gsm[:, 1, :], wf2[:, :, :], AX, ALU.add))
                        step.settle()
                        step.done(dve.reciprocal(gsm[:, 2, :], gsm[:, 1, :]))
                        step.settle()
                        dve.tensor_tensor(wf[:, :, :], wf2[:, :, :],
                                          gsm[:, 2, :].unsqueeze(2).to_broadcast([P, GT, NX]),
                                          ALU.mult).then_inc(gate_ok, 1)
                    dve.wait_ge(gate_ok, gg + 1)
                gate_steps = 1 + 2 * GT + 1 + 3 + 2 * GT if layer == 0 else 4

                def group(g, last):
                    gates(g)
                    for e in range(NX + 1):
                        for t in range(GT):
                            n = 5 * e + t
                            xt = X[:, ds((g * GT + t) * D, D)]
                            dve.wait_ge(y_mm, LEAD + g * YM + (mb + len(UNITS) * e + t // 2 + 1))
                            if e:
                                dve.wait_ge(y_ok, LEAD + g * YT + (yb + n - GT + 1))
                            if e < NX:
                                dve.scalar_tensor_tensor(out=xt, in0=yslot[t], scalar=wf[:, t, e:e + 1], in1=xt,
                                                         op0=ALU.mult, op1=ALU.add).then_inc(y_ok, 1)
                            else:
                                dve.tensor_tensor(xt, yslot[t], xt, ALU.add).then_inc(y_ok, 1)
                        if e == 3 and not last:
                            ln(g + 1, False)

                ln(0, layer == 0)
                with dve.Fori(0, NG - 1) as g:
                    step.enter(g, gate_steps + ln_steps)
                    group(g, False)
                step.leave(NG - 1)
                group(NG - 1, True)

            experts(0)
            dve.wait_ge(y_ok, LEAD + NG * YT)

            dve.wait_ge(wg_in, 16)
            for k in range(KD):
                for j, a in enumerate((ar_b, al_b)):
                    step.done(dve.tensor_tensor(prod, Wg_sb[:, k, 0:D], a, ALU.mult))
                    step.settle()
                    last = step.done(dve.tensor_reduce(Wg_sb[:, k, D + j * NH:D + (j + 1) * NH],
                                                       prod.rearrange("p (h d) -> p h d", d=DH), AX, ALU.add))
                    step.settle()
            dve.memset(shift[:, :, :], 0.0).then_inc(wa_ok, 1)
            all_stats(1)
            with dve.Fori(0, NT) as i:
                dve.wait_ge(t_ev[0], LEAD + i + (NT + 1))
                dve.tensor_copy(HRL[:, ds(i, 1), :], tb1[:, D:WG].unsqueeze(1)).then_inc(hrl_ok, 1)
            dve.wait_ge(hrl_ok, LEAD + NT)
            dve.wait_ge(wa_ok, 1)
            HR3 = HR[:, :].rearrange("p (t h) -> p t h", h=NH)
            step.done(dve.tensor_scalar(HR3, HRL[:, :, 0:NH], -1.0, None, ALU.mult))
            step.settle()
            dve.tensor_reduce(shift[:, 0, :], HR[:, :].rearrange("p (t h) -> p h t", h=NH), AX, ALU.max
                              ).then_inc(low_ok, 1)
            dve.wait_ge(shift_ok, 1)
            dve.tensor_tensor(HR3, HRL[:, :, 0:NH], shift[:, 1, :].unsqueeze(1).to_broadcast([P, NT, NH]),
                              ALU.add).then_inc(hrt_ok, 1)

            def targets(i, off, b, used, used_at):
                if used_at is not None:
                    dve.wait_ge(used[b], LEAD + used_at)
                c = i * (2 * UG) + off * UG
                dve.tensor_tensor(S[b], iota_p[:, :].unsqueeze(1).to_broadcast([P, UG, P]),
                                  loc1[:, ds(c, UG)].unsqueeze(2).to_broadcast([P, UG, P]),
                                  ALU.is_equal).then_inc(s_ready[b], 1)

            def maxima(i, b, bs):
                for u in range(UG):
                    dve.wait_ge(m_mm[b], LEAD + i + 1)
                    dve.tensor_reduce(tmx[:, b, u, :], bank[4 * b + u][:, :].rearrange("p (h j) -> p h j", j=P),
                                      AX, ALU.max).then_inc(m_red[b], 1)
                for u in range(UG):
                    dve.wait_ge(m_red[b], LEAD + i * UG + u + 1)
                    if u:
                        dve.wait_ge(m_ok[b], LEAD + i * UG + u)
                    elif b:
                        dve.wait_ge(m_ok[0], LEAD + i * UG + UG)
                    else:
                        dve.wait_ge(m_ok[1], LEAD + i * UG)
                    m = M[:, ds(bs[b * UG + u] * NH, NH)]
                    dve.tensor_tensor(m, m, tmx[:, b, u, :], ALU.max).then_inc(m_ok[b], 1)

            targets(0, 0, 0, None, None)
            with dve.Fori(0, rounds) as i:
                bs = buckets(1, i)
                targets(i, 1, 1, m_mm, i)
                maxima(i, 0, bs)
                targets(i, 2, 0, m_mm, i + 1)
                maxima(i, 1, bs)
            for b in range(2):
                dve.wait_ge(m_ok[b], LEAD + rounds * UG)

            M3 = M[:, :].rearrange("p (t h) -> p t h", h=NH)
            R3 = R[:, :].rearrange("p (t h) -> p t h", h=2 * NH)
            step.done(dve.memset(ACC, 0.0))
            step.done(dve.tensor_tensor(M3, M3, shift[:, 1, :].unsqueeze(1).to_broadcast([P, NT, NH]), ALU.subtract))
            step.done(dve.tensor_copy(R3[:, :, 0:NH], HRL[:, :, NH:2 * NH]))
            step.settle()
            step.done(dve.tensor_tensor(M3, M3, HRL[:, :, NH:2 * NH], ALU.add))
            step.settle()
            dve.scalar_tensor_tensor(out=R3[:, :, NH:2 * NH], in0=M3, scalar=SLOPE, in1=M3, op0=ALU.mult,
                                     op1=ALU.max).then_inc(r_ready, 1)

            def logits(i, b):
                re = bank[6 + b][:, 0:UG * 2 * NH].rearrange("p (u h) -> p u h", h=2 * NH)
                dve.wait_ge(g_in[b], i * 64 + 64 * (2 * rounds + 1))
                dve.wait_ge(re_mm[b], i + 1)
                dve.wait_ge(e_exp[b], LEAD + i)
                step.done(dve.tensor_tensor(ez[:, 2 * b + 1, :, :], re[:, :, 0:NH], G4[b][:, :, D:AGG], ALU.add))
                step.settle()
                step.done(dve.scalar_tensor_tensor(out=ez[:, 2 * b, :, :], in0=ez[:, 2 * b + 1, :, :], scalar=SLOPE,
                                                   in1=ez[:, 2 * b + 1, :, :], op0=ALU.mult, op1=ALU.max))
                step.settle()
                step.done(dve.tensor_tensor(ez[:, 2 * b + 1, :, :], ez[:, 2 * b, :, :], re[:, :, NH:2 * NH],
                                            ALU.subtract))
                step.settle()
                dve.tensor_scalar(ez[:, 2 * b, :, :], ez[:, 2 * b + 1, :, :], 1.0, None, ALU.min).then_inc(e_in[b], 1)

            def messages(i, b):
                dve.wait_ge(e_exp[b], LEAD + i + 1)
                for u in range(UG):
                    g3 = G[b][u][:, 0:D].rearrange("p (h d) -> p h d", d=DH)
                    w3 = G[b][u][:, D:AGG].unsqueeze(2).to_broadcast([P, NH, DH])
                    last = dve.tensor_tensor(g3, g3, w3, ALU.mult)
                last.then_inc(msg_ok[b], 1)

            targets(0, 0, 0, None, None)
            with dve.Fori(0, rounds) as i:
                step.enter(i, 6)
                bs = buckets(1, i)
                def view2(b, u):
                    return bank[u][:, 0:AGG]
                targets(i, 1, 1, acc2_mm, i * UG)
                logits(i, 0)
                logits(i, 1)
                messages(i, 0)
                messages(i, 1)
                add_up(i, 0, bs, acc2_mm, lambda i, u: i * UG + (u + 1), acc2_ok, view2, ACC, AGG)
                targets(i, 2, 0, acc2_mm, i * UG + UG)
                add_up(i, 1, bs, acc2_mm, lambda i, u: i * UG + (u + 1), acc2_ok, view2, ACC, AGG)
            step.leave(rounds)
            for b in range(2):
                dve.wait_ge(acc2_ok[b], LEAD + rounds * UG)
            acc3 = ACC.rearrange("p (t r) -> p t r", r=AGG)
            step.done(dve.tensor_scalar(M3, acc3[:, :, D:AGG], 1e-30, None, ALU.max))
            step.settle()
            step.done(dve.reciprocal(M[:, :], M[:, :]))
            step.settle()
            for h in range(NH):
                a = acc3[:, :, h * DH:(h + 1) * DH]
                step.done(dve.tensor_tensor(a, a, M3[:, :, h:h + 1].to_broadcast([P, NT, DH]), ALU.mult))
            step.settle()
            step.done(dve.tensor_tensor(X3[:, 0:NT, :], X3[:, 0:NT, :], acc3[:, :, 0:D], ALU.add))
            step.settle()

            experts(1)


_INS = ['x', 'src', 'dst', 'edge_type_8', 'edge_weight', 'L0_gnn_weight', 'L0_ffn_gamma', 'L0_ffn_beta',
        'L0_ffn_Wr', 'L0_ffn_br', 'L0_ffn_W1', 'L0_ffn_b1', 'L0_ffn_W2', 'L0_ffn_b2', 'L1_gnn_W', 'L1_gnn_a_l',
        'L1_gnn_a_r', 'L1_ffn_Wr', 'L1_ffn_br', 'L1_ffn_W1', 'L1_ffn_b1', 'L1_ffn_g1', 'L1_ffn_be1', 'L1_ffn_m1',
        'L1_ffn_v1', 'L1_ffn_W2', 'L1_ffn_b2', 'L1_ffn_g2', 'L1_ffn_be2', 'L1_ffn_m2', 'L1_ffn_v2', 'L1_ffn_Wo',
        'L1_ffn_bo']
_OUTS = [((3125, 256), 'float32')]


def kernel(**inputs):
    import numpy as _np
    import concourse.bacc as _bacc
    from concourse import mybir as _mybir
    from concourse.bass_utils import run_bass_kernel_spmd as _run

    nc = _bacc.Bacc("TRN2", target_bir_lowering=False, num_devices=1)
    arrays, args = {}, []
    for name in _INS:
        a = _np.ascontiguousarray(inputs[name])
        arrays[f"in_{name}_dram"] = a
        args.append(nc.dram_tensor(f"in_{name}_dram", a.shape, _mybir.dt.from_np(a.dtype), kind="ExternalInput").ap())
    for i, (shape, dtype) in enumerate(_OUTS):
        dt = _mybir.dt.from_np(_np.dtype(dtype))
        args.append(nc.dram_tensor(f"out_{i}_dram", shape, dt, kind="ExternalOutput").ap())
    program(nc, *args)
    r = _run(nc, [arrays], core_ids=[0])
    got = tuple(r.results[0][f"out_{i}_dram"] for i in range(len(_OUTS)))
    return got[0]
```

```python
from contextlib import ExitStack

import concourse.bass as bass
from concourse import mybir

ALU = mybir.AluOpType
ACT = mybir.ActivationFunctionType
AX = mybir.AxisListType.X
F32 = mybir.dt.float32
F16 = mybir.dt.float16
BF16 = mybir.dt.bfloat16
I32 = mybir.dt.int32
RMAX = bass.bass_isa.ReduceOp.max
ds = bass.ds

P = 128
UG = 4
LN_EPS = 1e-5
BN_EPS = 1e-3
SLOPE = 0.2
FAR = -1e30
PIECE = 11


class Steps:

    def __init__(self, eng, sem):
        self.eng, self.sem, self.n = eng, sem, 0

    def done(self, ins):
        ins.then_inc(self.sem, 1)
        self.n = self.n + 1
        return ins

    def settle(self):
        self.eng.wait_ge(self.sem, self.n)

    def enter(self, i, per):
        self.start, self.per = self.n, per
        self.n = i * per + self.start
        self.at = 0

    def leave(self, rounds):
        self.n = self.start + self.per * rounds


def program(nc, x, src, dst, rel, wgt, w_rgcn, gamma, beta, Wr0, br0, W10, b10, W20, b20,
            Wg, a_l, a_r, Wr1, br1, W11, b11, g1, be1, m1, v1, W21, b21, g2, be2, m2, v2, Wo, bo, out):
    N, D = x.shape
    E = src.shape[0]
    NR = w_rgcn.shape[0]
    NX = W10.shape[0]
    H0 = W10.shape[2]
    NH, DH = a_l.shape[1], a_l.shape[2]
    SB = 32
    KD = D // P
    NT = -(-N // P)
    SC = 7
    EC = 4 * SC * -(-E // (4 * SC * P))
    BUF = 4
    T = BUF * UG * -(-(E + NT * (P - 1)) // (BUF * UG * P))
    TX = T + UG
    HC = H0 // P
    GT = 5
    NG = NT // GT
    GC = GT * P
    HG = GC // 2
    AGG = D + NH
    ROW = AGG
    WG = D + 2 * NH
    NB = NT
    UNITS = [(0, 1), (2, 3), (4,)]
    YM = len(UNITS) * (NX + 1)
    YT = GT * (NX + 1)
    assert NT % GT == 0 and NR * D == 4 * 512 and D == NH * DH and NX == 8

    table0 = nc.dram_tensor("relation_table", (NT * P * NR, D), F32, kind="Internal").ap()
    table1 = nc.dram_tensor("gat_table", (NT * P, ROW), F32, kind="Internal").ap()
    sorted0 = nc.dram_tensor("sorted_edges", (P * T + P * EC, 2), I32, kind="Internal").ap()
    table_hr = nc.dram_tensor("hr_table", (NT * P, NH), F32, kind="Internal").ap()

    with ExitStack() as ctx:
        def sb(name, shape, dt=F32):
            return ctx.enter_context(nc.sbuf_tensor(name, shape, dt))

        def sem(name):
            return ctx.enter_context(nc.semaphore(name))

        bank = [ctx.enter_context(nc.psum_tensor(f"bank{i}", [P, 512], F32)) for i in range(8)]

        X = sb("X", [P, (NT + 2) * D])
        X3 = X[:, :].rearrange("p (t d) -> p t d", d=D)
        arena = sb("arena", [P, 20480])
        work = sb("work", [P, 11584])
        W_rel = sb("W_rel", [P, KD, NR, P])
        vals = sb("vals", [P, 2, EC])
        slot_f = sb("slot_f", [P, EC])
        tile_f = sb("tile_f", [P, EC])
        record = sb("record", [P, EC, 2], I32)
        place0 = sb("place0", [P, EC], I32)
        sorted_sb = sb("sorted_sb", [P, T, 2], I32)
        stage_r = sb("stage_r", [P, 2, SC, 2], I32)
        stage_p = sb("stage_p", [P, 2, SC], I32)
        dump = sb("dump", [P, EC])
        neg_id = sb("neg_id", [P, P], BF16)

        ident = sb("ident", [P, P])
        ones = sb("ones", [P, P])
        lower = sb("lower", [P, P])
        iota_p = sb("iota_p", [P, P])
        iota_slot = sb("iota_slot", [P, P], F16)
        iota_tile = sb("iota_tile", [P, T], F16)
        iota_b = sb("iota_b", [P, NB])
        iota_x = sb("iota_x", [P, NX])
        eps_ln = sb("eps_ln", [P, 1])
        eps_bn = sb("eps_bn", [P, 1])

        idx0 = sb("idx0", [P, TX], I32)
        loc0 = sb("loc0", [P, TX])
        wgt0 = sb("wgt0", [P, TX], I32)
        idx1 = sb("idx1", [P, TX], I32)
        loc1 = sb("loc1", [P, TX])
        bucket_row = [sb(f"bucket_row{w}", [1, TX], I32) for w in range(2)]
        stage = sb("stage", [P, BUF, UG], I32)
        pause = sb("pause", [P, 2])

        totals = sb("totals", [P, 6, NB])
        tiles_i = sb("tiles_i", [P, 2, NB], I32)
        bc = sb("bc", [P, 4 * D + 2 * NX])
        gamma_b = bc[:, 0:D]
        beta_b = bc[:, D:2 * D]
        al_b = bc[:, 2 * D:3 * D]
        ar_b = bc[:, 3 * D:4 * D]
        br_b = [bc[:, 4 * D:4 * D + NX], bc[:, 4 * D + NX:4 * D + 2 * NX]]
        par = sb("par", [P, 192])
        bn_s = sb("bn_s", [P, 2, 2 * NX])
        bn_t = sb("bn_t", [P, 2, 2 * NX])
        Wr_sb = sb("Wr_sb", [P, 2, KD, NX])
        b2_sb = sb("b2_sb", [NX, 2, D])

        stats = sb("stats", [P, NT, 6])
        mv = sb("mv", [P, NT, 2])
        rstd = sb("rstd", [P, NT + 2])
        nbias = sb("nbias", [P, NT + 2])
        lg = sb("lg", [P, GT, NX])
        top = sb("top", [P, GT, 8])
        topi = sb("topi", [P, GT, 8], mybir.dt.uint32)
        topf = sb("topf", [P, GT, 8])
        gsm = sb("gsm", [P, 4, GT])
        wf = sb("wf", [P, GT, NX])
        wf2 = sb("wf2", [P, GT, NX])
        wT = sb("wT", [NX, GC])

        HRL = sb("HRL", [P, NT, 2 * NH])
        M = sb("M", [P, (NT) * NH])
        R = sb("R", [P, NT * 2 * NH])
        hre = sb("hre", [P, 2, UG * NH])
        tmx = sb("tmx", [P, 2, UG, NH])
        ez = sb("ez", [P, 2, BUF, UG, NH])

        def wk(a, n):
            return work[:, a:a + n]
        tbl = [wk(0, NR * D), wk(7424, NR * D)]
        h_t = wk(2048, D)
        hT_t = wk(2304, D)
        ints = [wk(2560 + k * EC, EC).bitcast(I32) for k in range(6)]
        bucket_f = wk(2560 + 6 * EC, EC)
        oh0 = 5312
        tile_oh = [wk(oh0 + u * 528, 208).bitcast(F16) for u in range(4)]
        slot_oh = [wk(oh0 + u * 528 + 208, P).bitcast(F16) for u in range(4)]
        zeros = wk(10560, 2 * T).bitcast(I32)
        G = [[wk(7424 + (b * UG + u) * ROW, ROW) for u in range(UG)] for b in range(2)]
        S = [wk(9536 + b * 512, 512).rearrange("p (u r) -> p u r", r=P) for b in range(2)]
        words = wk(9536, 2 * T).bitcast(I32).rearrange("p (a t) -> p a t", a=2)
        wordf = [wk(9536 + 2 * T, T)]
        row_a = work[0:1, 7424:7424 + 4 * D + 2 * NX]
        par_a = wk(8480, P)
        par_b = work[0:64, 8608:8608 + P]
        SP0 = 3 * NX * KD * D
        G2 = [arena[:, SP0 + b * UG * ROW:SP0 + (b + 1) * UG * ROW].rearrange("p (u r) -> p u r", r=ROW)
              for b in range(BUF)]
        SP1 = SP0 + BUF * UG * ROW
        S2 = [arena[:, SP1 + b * 512:SP1 + (b + 1) * 512].rearrange("p (u r) -> p u r", r=P) for b in range(BUF)]
        ST = [wk(7424 + b * 512, 512) for b in range(BUF)]
        hid = wk(0, 2 * HC * GC).rearrange("p (b c n) -> p b c n", b=2, c=HC)
        xn = wk(5120, GT * D).rearrange("p (t d) -> p t d", d=D)
        xnT = wk(6400, KD * GC)
        notS = [wk(9536 + b * 256, 256).bitcast(BF16).rearrange("p (u r) -> p u r", r=P) for b in range(2)]
        ACC = wk(0, NT * AGG)
        tb1 = [wk(7424, WG), wk(7424 + 512, WG)]
        prod = wk(8704, D)

        onehot_b = arena[:, 0:NB * EC]
        onehot_b3 = onehot_b.rearrange("p (b c) -> p b c", c=EC)
        count_b = arena[:, NB * EC:2 * NB * EC]
        count_b3 = count_b.rearrange("p (b c) -> p b c", c=EC)
        W10_sb = arena[:, 0:NX * KD * H0].rearrange("p (e k h) -> p e k h", e=NX, k=KD)
        W20_sb = arena[:, NX * KD * H0:NX * KD * H0 + NX * HC * D].rearrange("p (e k h) -> p e k h", e=NX, k=HC)
        W1_sb = [arena[:, j * NX * KD * D:(j + 1) * NX * KD * D].rearrange("p (e k h) -> p e k h", e=NX, k=KD)
                 for j in range(3)]
        Wg_sb = arena[:, 20480 - KD * WG:20480].rearrange("p (k h) -> p k h", k=KD)

        const_set = sem("const_set")
        pool_step = sem("pool_step")
        vec_step = sem("vec_step")
        act_step = sem("act_step")
        x_in = sem("x_in")
        edges_in = sem("edges_in")
        par_in = sem("par_in")
        wg_in = sem("wg_in")
        w0_in = sem("w0_in")
        w1_in = sem("w1_in")
        par_T = sem("par_T")
        par_ok = sem("par_ok")
        bn_sq = sem("bn_sq")
        bn_v = sem("bn_v")
        t_stats = sem("t_stats")
        t_sqrt = sem("t_sqrt")
        t_rstd = sem("t_rstd")
        t_h = sem("t_h")
        t_tr = sem("t_tr")
        t_hT = sem("t_hT")
        t_mm = sem("t_mm")
        t_ev = [sem(f"t_ev{k}") for k in range(4)]
        t_out = [sem(f"t_out{b}") for b in range(2)]
        tot_in = sem("tot_in")
        tot_ok = sem("tot_ok")
        oh_ready = [sem(f"oh_ready{u}") for u in range(4)]
        oh_used = [sem(f"oh_used{u}") for u in range(4)]
        order_ok = sem("order_ok")
        zero_set = sem("zero_set")
        record_ok = sem("record_ok")
        zero_in = sem("zero_in")
        sc_done = [sem(f"sc_done{b}") for b in range(2)]
        sorted_in = sem("sorted_in")
        staged = sem("staged")
        g_in = [sem(f"g_in{b}") for b in range(2)]
        g_used = [sem(f"g_used{b}") for b in range(2)]
        s_ready = [sem(f"s_ready{b}") for b in range(2)]
        acc_ok = [sem(f"acc_ok{b}") for b in range(2)]
        agg_ok = sem("agg_ok")
        ln_var = sem("ln_var")
        ln_sd = sem("ln_sd")
        xn_ok = sem("xn_ok")
        xn_tr = sem("xn_tr")
        xnT_ok = sem("xnT_ok")
        logit_ok = sem("logit_ok")
        gate_in = sem("gate_in")
        gate_exp = sem("gate_exp")
        gate_ok = sem("gate_ok")
        wT_tr = sem("wT_tr")
        wT_ok = sem("wT_ok")
        hid_mm = sem("hid_mm")
        hid_ok = sem("hid_ok")
        y_mm = sem("y_mm")
        y_ok = sem("y_ok")
        ffn_ok = sem("ffn_ok")
        hrl_ok = sem("hrl_ok")
        wa_ok = sem("wa_ok")
        hrt_ok = sem("hrt_ok")
        hrt_out = sem("hrt_out")
        m_mm = [sem(f"m_mm{b}") for b in range(2)]
        m_red = [sem(f"m_red{b}") for b in range(2)]
        m_ok = [sem(f"m_ok{b}") for b in range(2)]
        r_ready = sem("r_ready")
        nots_ok = [sem(f"nots_ok{b}") for b in range(2)]
        g2_in = [sem(f"g2_in{b}") for b in range(BUF)]
        s2_ready = [sem(f"s2_ready{b}") for b in range(BUF)]
        st_tr = [sem(f"st_tr{b}") for b in range(BUF)]
        st_ok = [sem(f"st_ok{b}") for b in range(BUF)]
        re_mm = [sem(f"re_mm{b}") for b in range(BUF)]
        e_in = [sem(f"e_in{b}") for b in range(BUF)]
        e_exp = [sem(f"e_exp{b}") for b in range(BUF)]
        msg_ok = [sem(f"msg_ok{b}") for b in range(BUF)]
        acc2_mm = [sem(f"acc2_mm{b}") for b in range(BUF)]
        acc2_ok = [sem(f"acc2_ok{b}") for b in range(BUF)]
        stored = sem("stored")

        LEAD = 1
        led = [hid_ok, y_ok, y_mm, hrl_ok, *t_ev, *oh_used, *g_used, *acc_ok, *m_mm, *m_red, *m_ok,
               *acc2_mm, *acc2_ok, *e_exp, *st_ok, *e_in]
        tails = (idx0, loc0, wgt0, idx1, loc1, *bucket_row)
        NCONST = 14 + 5 + 2 + len(tails)
        RB = 16 * (D // SB) // 2
        stores = [16 * -(-(NT - b) // 2) for b in range(2)]
        NPAR = 8 + 2 + 1 + 4 + 2 + 2 + 2
        rounds = T // (2 * UG)
        rounds4 = T // (BUF * UG)
        scatters = EC // (2 * SC)
        block = ctx.enter_context(nc.Block())

        @block.sync
        def _(sp):
            full = (NT - 1) * P
            sp.wait_ge(const_set, NCONST)
            sp.dma_start(X3[:, 0:NT - 1, :], x[0:full, :].rearrange("(t p) d -> p t d", p=P)).then_inc(x_in, 16)
            sp.dma_start(X3[0:N - full, NT - 1, :], x[full:N, :]).then_inc(x_in, 16)
            lastp = E // EC
            for k, a in enumerate((dst, src, rel, wgt.bitcast(I32))):
                sp.dma_start(ints[k][0:lastp, :], a[0:lastp * EC].rearrange("(p c) -> p c", c=EC)).then_inc(edges_in, 16)
                sp.dma_start(ints[k][lastp:lastp + 1, 0:E - lastp * EC],
                             a[lastp * EC:E].rearrange("(p c) -> p c", p=1)).then_inc(edges_in, 16)
            for b in range(D // SB):
                q = b % (P // SB)
                sp.dma_start(W_rel[q * SB:(q + 1) * SB, b // (P // SB), :, q * SB:(q + 1) * SB],
                             w_rgcn[:, b * SB * SB:(b + 1) * SB * SB].rearrange("r (i o) -> i r o", o=SB)
                             ).then_inc(t_out[b % 2], 16)
            for k, a in enumerate((b11, g1, be1, m1, v1, b21, g2, be2)):
                sp.dma_start(par_a[16 * k:16 * k + 16, :], a.rearrange("e (c p) -> (e c) p", p=P)).then_inc(par_in, 16)
            for k, a in enumerate((m2, v2)):
                sp.dma_start(par_b[16 * k:16 * k + 16, :], a.rearrange("e (c p) -> (e c) p", p=P)).then_inc(par_in, 16)
            sp.dma_start(par_b[32:64, :], b10.rearrange("e (c p) -> (e c) p", p=P)).then_inc(par_in, 16)
            for a, o, n in ((gamma, 0, D), (beta, D, D), (br0, 4 * D, NX), (br1, 4 * D + NX, NX)):
                sp.dma_start(row_a[0:1, o:o + n], a.rearrange("(a n) -> a n", a=1)).then_inc(par_in, 16)
            for a, o in ((a_l, 2 * D), (a_r, 3 * D)):
                sp.dma_start(row_a[0:1, o:o + D], a.rearrange("a h d -> a (h d)")).then_inc(par_in, 16)
            for j, a in enumerate((Wr0, Wr1)):
                sp.dma_start(Wr_sb[:, j, :, :], a.rearrange("(k p) e -> p k e", p=P)).then_inc(par_in, 16)
            for j, a in enumerate((b20, bo)):
                sp.dma_start(b2_sb[:, j, :], a).then_inc(par_in, 16)

            sp.wait_ge(zero_set, 1)
            for b in range(2):
                sp.dma_start(sorted0[b * (P // 2) * T:(b + 1) * (P // 2) * T, :].rearrange("(p t) w -> p (t w)", t=T),
                             zeros[b * (P // 2):(b + 1) * (P // 2), :]).then_inc(zero_in, 16)

            def store_table0(i, b):
                for k in range(4):
                    sp.wait_ge(t_ev[k], LEAD + i + 1)
                sp.dma_start(table0[ds(i * (P * NR), P * NR), :].rearrange("(p r) d -> p (r d)", r=NR),
                             tbl[b]).then_inc(t_out[b], 16)

            with sp.Fori(0, NT // 2) as i:
                store_table0(i * 2, 0)
                store_table0(i * 2 + 1, 1)
            store_table0(NT - 1, 0)
            for b in range(2):
                sp.wait_ge(sc_done[b], 16 * SC * scatters)
            sp.dma_start(sorted_sb[:, :, :], sorted0[0:P * T, :].rearrange("(p t) w -> p t w", t=T)).then_inc(sorted_in, 16)
            sp.wait_ge(order_ok, 1)
            for e in range(NX):
                sp.dma_start(W10_sb[:, e], W10[e].rearrange("(k p) h -> p k h", p=P)).then_inc(w0_in, 16)
                sp.dma_start(W20_sb[:, e], W20[e].rearrange("(k p) h -> p k h", p=P)).then_inc(w0_in, 16)
            sp.dma_start(Wg_sb[:, :, 0:D], Wg.rearrange("(k p) h -> p k h", p=P)).then_inc(wg_in, 16)
            sp.wait_ge(y_mm, LEAD + NG * YM)
            for e in range(NX):
                for j, a in enumerate((W11, W21, Wo)):
                    sp.dma_start(W1_sb[j][:, e], a[e].rearrange("(k p) h -> p k h", p=P)).then_inc(w1_in, 16)
            def store_table1(i, b):
                sp.wait_ge(t_ev[0], LEAD + i + (NT + 1))
                sp.dma_start(table1[ds(i * P, P), :], tb1[b][:, 0:ROW]).then_inc(t_out[b], 16)

            with sp.Fori(0, NT // 2) as i:
                store_table1(i * 2, 0)
                store_table1(i * 2 + 1, 1)
            store_table1(NT - 1, 0)
            sp.wait_ge(hrl_ok, LEAD + NT)
            sp.dma_start(table_hr[:, :].rearrange("(t p) h -> p t h", p=P), HRL[:, :, 0:NH]).then_inc(hrt_out, 16)
            with sp.Fori(0, NG - 1) as g:
                sp.wait_ge(y_ok, LEAD + g * YT + (NG + 1) * YT)
                sp.dma_start(out[ds(g * GC, GC), :].rearrange("(t p) d -> p t d", p=P),
                             X3[:, ds(g * GT, GT), :]).then_inc(stored, 16)
            sp.wait_ge(y_ok, LEAD + 2 * NG * YT)
            sp.dma_start(out[(NG - 1) * GC:full, :].rearrange("(t p) d -> p t d", p=P),
                         X3[:, (NG - 1) * GT:NT - 1, :]).then_inc(stored, 16)
            sp.dma_start(out[full:N, :], X3[0:N - full, NT - 1, :]).then_inc(stored, 16)
            sp.wait_ge(stored, 16 * (NG + 1))

        @block.gpsimd
        def _(pool):
            step = Steps(pool, pool_step)
            step.done(pool.memset(ident[:, :], 0.0))
            step.done(pool.memset(lower[:, :], 1.0))
            step.done(pool.memset(pause[:, 0:1], 0.0))
            step.done(pool.memset(neg_id[:, :], 0.0))
            pool.memset(zeros, 0).then_inc(zero_set, 1)
            for s in led:
                pool.sem_inc(s, LEAD)
            pool.memset(ones[:, :], 1.0).then_inc(const_set, 1)
            pool.memset(X[:, (NT - 1) * D:(NT + 2) * D], 0.0).then_inc(const_set, 1)
            pool.memset(ints[0][:, :], -1).then_inc(const_set, 1)
            pool.memset(ints[1][:, :], -1).then_inc(const_set, 1)
            pool.memset(ints[2][:, :], 0).then_inc(const_set, 1)
            pool.memset(ints[3][:, :], 0).then_inc(const_set, 1)
            pool.memset(W_rel[:, :, :, :], 0.0).then_inc(const_set, 1)
            pool.memset(eps_ln[:, :], LN_EPS).then_inc(const_set, 1)
            pool.memset(eps_bn[:, :], BN_EPS).then_inc(const_set, 1)
            for a in (rstd[:, NT:NT + 2], nbias[:, NT:NT + 2], *(a[:, T:TX] for a in tails)):
                pool.memset(a, 0).then_inc(const_set, 1)
            pool.memset(M[:, :], FAR).then_inc(const_set, 1)
            step.settle()
            pool.affine_select(out=ident[:, :], in_=ident[:, :], compare_op=ALU.not_equal, fill=1.0, base=0,
                               pattern=[[-1, P]], channel_multiplier=1).then_inc(const_set, 1)
            pool.affine_select(out=lower[:, :], in_=lower[:, :], compare_op=ALU.is_gt, fill=0.0, base=0,
                               pattern=[[1, P]], channel_multiplier=-1).then_inc(const_set, 1)
            pool.affine_select(out=neg_id[:, :], in_=neg_id[:, :], compare_op=ALU.not_equal, fill=FAR, base=0,
                               pattern=[[-1, P]], channel_multiplier=1).then_inc(const_set, 1)
            pool.iota(dump[:, :], pattern=[[1, EC]], base=P * T - ((P - 1) * T - 1), channel_multiplier=EC,
                      allow_small_or_imprecise_dtypes=True).then_inc(const_set, 1)
            for t, n in ((iota_p, P), (iota_slot, P), (iota_tile, T), (iota_b, NB), (iota_x, NX)):
                pool.iota(t[:, :], pattern=[[1, n]], base=0, channel_multiplier=0,
                          allow_small_or_imprecise_dtypes=True).then_inc(const_set, 1)

            def gathers(idx, table, dest, used, used_at, k, b, arrived):
                pool.wait_ge(used, LEAD + used_at)
                step.done(pool.tensor_copy(stage[:, b, :], idx[:, ds(k * UG, UG)]))
                step.settle()
                pool.tensor_tensor(pause[:, 0:1], pause[:, 0:1], pause[:, 0:1], ALU.add)
                for u in range(UG):
                    pool.indirect_dma_start(dest[u], None, table,
                                            bass.IndirectOffsetOnAxis(ap=stage[:, b, u:u + 1], axis=0)
                                            ).then_inc(arrived, 16)

            pool.wait_ge(record_ok, 1)
            pool.wait_ge(zero_in, 32)

            def scatter(i, b, first):
                c = i * (2 * SC) + b * SC
                if not first:
                    pool.wait_ge(sc_done[b], i * (16 * SC))
                step.done(pool.tensor_copy(stage_p[:, b, :], place0[:, ds(c, SC)]))
                step.done(pool.tensor_copy(stage_r[:, b, :, :], record[:, ds(c, SC), :]))
                step.settle()
                pool.tensor_tensor(pause[:, 0:1], pause[:, 0:1], pause[:, 0:1], ALU.add)
                for u in range(SC):
                    pool.indirect_dma_start(sorted0, bass.IndirectOffsetOnAxis(ap=stage_p[:, b, u:u + 1], axis=0),
                                            stage_r[:, b, u, :], None).then_inc(sc_done[b], 16)

            for b in range(2):
                scatter(0, b, True)
            with pool.Fori(0, scatters - 1) as i:
                step.enter(i, 4)
                for b in range(2):
                    scatter(i + 1, b, False)
            step.leave(scatters - 1)

            for b in range(2):
                pool.wait_ge(t_out[b], RB + stores[b])
            pool.wait_ge(order_ok, 2)
            with pool.Fori(0, rounds) as i:
                step.enter(i, 2)
                for b in range(2):
                    gathers(idx0, table0, [G[b][u][:, 0:D] for u in range(UG)], g_used[b], i, i * 2 + b, b, g_in[b])
            step.leave(rounds)
            for b in range(2):
                pool.wait_ge(g_used[b], LEAD + rounds)
            pool.wait_ge(hrt_out, 16)
            with pool.Fori(0, rounds) as i:
                step.enter(i, 2)
                for b in range(2):
                    gathers(idx1, table_hr, [hre[:, b, u * NH:(u + 1) * NH] for u in range(UG)],
                            m_mm[b], i, i * 2 + b, b, g_in[b])
            step.leave(rounds)
            for b in range(2):
                pool.wait_ge(m_mm[b], LEAD + rounds)
            for b in range(2):
                pool.wait_ge(t_out[b], RB + 2 * stores[b])
            with pool.Fori(0, rounds4) as i:
                step.enter(i, BUF)
                for b in range(BUF):
                    gathers(idx1, table1, [G2[b][:, u, :] for u in range(UG)], acc2_mm[b], i * UG,
                            i * BUF + b, b, g2_in[b])
            step.leave(rounds4)

        @block.tensor
        def _(pe):
            pe.wait_ge(const_set, NCONST)
            pe.wait_ge(par_in, 16 * NPAR)
            pe.transpose(bank[0][:, 0:P], par_a[:, :], ident[:, :])
            pe.transpose(bank[0][:, P:P + 64], par_b[:, :], ident[0:64, 0:64])
            nrow = 4 * D + 2 * NX
            for k in range(3):
                a, b = 512 * k, min(512 * k + 512, nrow)
                mm = pe.matmul(bank[1 + k][:, 0:b - a], ones[0:1, :], row_a[0:1, a:b], start=True, stop=True)
            mm.then_inc(par_T, 1)

            def turn(tr, h_ready, free):
                pe.wait_ge(h_ready[0], h_ready[1])
                pe.wait_ge(free[0], free[1])
                for k in range(KD):
                    t = pe.transpose(bank[7][:, k * P:(k + 1) * P], h_t[:, k * P:(k + 1) * P], ident[:, :])
                t.then_inc(tr, 1)

            def totals_mm(n):
                pe.wait_ge(tot_in, n)
                pe.matmul(bank[6][:, 0:NB], lower[:, :], totals[:, 0, :], start=True, stop=True)
                pe.matmul(bank[6][:, 32:32 + NB], ones[:, :], totals[:, 0, :], start=True, stop=True
                          ).then_inc(tot_ok, 1)

            totals_mm(1)
            pe.wait_ge(t_h, 1)
            for k in range(KD):
                t = pe.transpose(bank[7][:, k * P:(k + 1) * P], h_t[:, k * P:(k + 1) * P], ident[:, :])
            t.then_inc(t_tr, 1)
            for b in range(2):
                pe.wait_ge(t_out[b], RB)
            pe.wait_ge(par_ok, 1)
            with pe.Fori(0, NT) as i:
                pe.wait_ge(t_hT, i + 1)
                for k in range(4):
                    pe.wait_ge(t_ev[k], LEAD + i)
                    half, c = k // 2, k % 2
                    pe.matmul(bank[k][:, :], hT_t[:, half * P:(half + 1) * P],
                              W_rel[:, half, 4 * c:4 * c + 4, :].rearrange("p r o -> p (r o)"),
                              start=True, stop=True).then_inc(t_mm, 1)
                turn(t_tr, (t_h, i + 2), (t_hT, i + 1))

            def sort_group(j, first, last):
                for u in range(4):
                    pe.wait_ge(oh_ready[u], j + 1)
                    for f in range(2):
                        mm = pe.matmul(bank[f][:, 0:T], slot_oh[u][:, f * P:(f + 1) * P], tile_oh[u],
                                       start=(first and u == 0), stop=(last and u == 3))
                    mm.then_inc(oh_used[u], 1)

            totals_mm(2)
            for k in range(2):
                pe.wait_ge(t_ev[k], LEAD + NT)
            sort_group(0, True, False)
            with pe.Fori(1, EC // 4 - 1) as j:
                sort_group(j, False, False)
            sort_group(EC // 4 - 1, False, True)

            pe.wait_ge(order_ok, 2)
            with pe.Fori(0, rounds) as i:
                for b in range(2):
                    pe.wait_ge(g_in[b], i * 64 + 64)
                    pe.wait_ge(s_ready[b], i + 1)
                    pe.wait_ge(acc_ok[b], LEAD + i * UG)
                    for u in range(UG):
                        mm = pe.matmul(bank[2 * b + u // 2][:, (u % 2) * D:(u % 2 + 1) * D], S[b][:, u, :],
                                       G[b][u][:, 0:D], start=True, stop=True)
                    mm.then_inc(g_used[b], 1)

            def experts(layer):
                hn = 2 * 4 * NX
                yb, mb, hb = layer * NG * YT, layer * NG * YM, layer * NG * hn
                yslot = [bank[4 + t // 2][:, (t % 2) * D:(t % 2 + 1) * D] for t in range(GT)]

                def group(g):
                    gg = g + layer * NG
                    pe.wait_ge(xn_ok, gg + 1)
                    pe.wait_ge(hid_ok, LEAD + g * hn + hb)
                    for k in range(KD):
                        for t in range(GT):
                            q = k * GT + t
                            tr = pe.transpose(bank[q // 4][:, (q % 4) * P:(q % 4 + 1) * P],
                                              xn[:, t, k * P:(k + 1) * P], ident[:, :])
                    tr.then_inc(xn_tr, 1)
                    pe.wait_ge(xnT_ok, gg + 1)
                    for t in range(GT):
                        for k in range(KD):
                            mm = pe.matmul(bank[7][:, t * NX:(t + 1) * NX],
                                           xnT[:, k * GC + t * P:k * GC + (t + 1) * P], Wr_sb[:, layer, k, :],
                                           start=(k == 0), stop=(k == KD - 1))
                    mm.then_inc(logit_ok, 1)

                    def hidden(e, c, weights, source):
                        r = 4 * e + c
                        pe.wait_ge(hid_ok, LEAD + g * hn + (hb + max(0, 2 * r - 2)))
                        n = len(weights)
                        for j in range(2):
                            for k in range(n):
                                mm = pe.matmul(bank[2 * (r % 2) + j][:, 0:HG], weights[k], source(k, j),
                                               start=(k == 0), stop=(k == n - 1))
                            mm.then_inc(hid_mm, 1)

                    def x_in_cols(k, j):
                        return xnT[:, k * GC + j * HG:k * GC + (j + 1) * HG]

                    def first(e):
                        if layer == 0:
                            for c in range(HC):
                                hidden(e, c, [W10_sb[:, e, k, c * P:(c + 1) * P] for k in range(KD)], x_in_cols)
                        else:
                            for c in range(KD):
                                hidden(e, c, [W1_sb[0][:, e, k, c * P:(c + 1) * P] for k in range(KD)], x_in_cols)

                    def second(e):
                        pe.wait_ge(hid_ok, LEAD + g * hn + (hb + 8 * e + 4))
                        for c in range(KD):
                            hidden(e, 2 + c, [W1_sb[1][:, e, k, c * P:(c + 1) * P] for k in range(KD)],
                                   lambda k, j: hid[:, e % 2, k, j * HG:(j + 1) * HG])

                    def outs(e):
                        pe.wait_ge(hid_ok, LEAD + g * hn + (hb + 8 * e + 8))
                        ks = range(HC) if layer == 0 else range(2, 4)
                        for q, tiles in enumerate(UNITS):
                            pe.wait_ge(y_ok, LEAD + g * YT + (yb + (GT * (e - 1) + tiles[-1] + 1 if e else 0)))
                            if e == 1 and q == 2:
                                pe.wait_ge(wT_ok, gg + 1)
                            for t in tiles:
                                for k in ks:
                                    w = W20_sb[:, e, k, :] if layer == 0 else W1_sb[2][:, e, k - 2, :]
                                    mm = pe.matmul(yslot[t], hid[:, e % 2, k, t * P:(t + 1) * P], w,
                                                   start=(k == ks[0]), stop=(k == ks[-1]))
                            mm.then_inc(y_mm, 1)

                    first(0)
                    if layer == 1:
                        second(0)
                    for e in range(NX):
                        if e + 1 < NX:
                            first(e + 1)
                        if e == 1:
                            pe.wait_ge(gate_ok, gg + 1)
                            pe.wait_ge(y_ok, LEAD + g * YT + (yb + GT))
                            for t in range(GT):
                                o = bank[7][0:NX, t * P:(t + 1) * P] if t < 4 else bank[6][0:NX, 256:384]
                                tr = pe.transpose(o, wf[:, t, :], ident[:, :])
                            tr.then_inc(wT_tr, 1)
                        outs(e)
                        if layer == 1 and e + 1 < NX:
                            second(e + 1)
                    for q, tiles in enumerate(UNITS):
                        pe.wait_ge(y_ok, LEAD + g * YT + (yb + GT * (NX - 1) + tiles[-1] + 1))
                        for t in tiles:
                            mm = pe.matmul(yslot[t], wT[:, t * P:(t + 1) * P], b2_sb[:, layer, :],
                                           start=True, stop=True)
                        mm.then_inc(y_mm, 1)

                with pe.Fori(0, NG) as g:
                    group(g)

            pe.wait_ge(w0_in, 16 * 2 * NX)
            experts(0)

            pe.wait_ge(wa_ok, 1)
            pe.wait_ge(t_h, NT + 3)
            for k in range(KD):
                tr = pe.transpose(bank[7][:, k * P:(k + 1) * P], h_t[:, k * P:(k + 1) * P], ident[:, :])
            tr.then_inc(t_tr, 1)
            with pe.Fori(0, NT) as i:
                pe.wait_ge(t_hT, i + (NT + 2))
                pe.wait_ge(t_ev[0], LEAD + i + NT)
                for k in range(KD):
                    mm = pe.matmul(bank[0][:, 0:WG], hT_t[:, k * P:(k + 1) * P], Wg_sb[:, k, :],
                                   start=(k == 0), stop=(k == KD - 1))
                mm.then_inc(t_mm, 1)
                turn(t_tr, (t_h, i + (NT + 4)), (t_hT, i + (NT + 2)))

            with pe.Fori(0, rounds) as i:
                for b in range(2):
                    pe.wait_ge(g_in[b], i * 64 + 64 * (rounds + 1))
                    pe.wait_ge(nots_ok[b], i + 1)
                    pe.wait_ge(m_red[b], LEAD + i * UG)
                    for u in range(UG):
                        o = bank[4 * b + u]
                        pe.matmul(o[:, :].rearrange("p (h j) -> p h j", j=P), notS[b][:, u, :],
                                  neg_id[:, :].unsqueeze(1).to_broadcast([P, NH, P]), start=True, stop=False)
                        for h in range(NH):
                            c = u * NH + h
                            mm = pe.matmul(o[:, h * P:(h + 1) * P], hre[:, b, c:c + 1].to_broadcast([P, P]),
                                           ident[:, :], start=False, stop=(h == NH - 1))
                    mm.then_inc(m_mm[b], 1)

            def turn_targets(i, b, lead=0):
                pe.wait_ge(s2_ready[b], i + 1)
                pe.wait_ge(st_ok[(b - 2) % BUF], LEAD + i + (1 if b >= 2 else 0))
                for u in range(UG):
                    tr = pe.transpose(bank[4 + b % 2][:, u * P:(u + 1) * P], S2[b][:, u, :], ident[:, :])
                tr.then_inc(st_tr[b], 1)

            def rows_of_edges(i, b, bs):
                pe.wait_ge(st_ok[b], LEAD + i + 1)
                pe.wait_ge(e_in[(b - 2) % BUF], LEAD + i + (1 if b >= 2 else 0))
                for u in range(UG):
                    mm = pe.matmul(bank[6 + b % 2][:, u * 2 * NH:(u + 1) * 2 * NH], ST[b][:, u * P:(u + 1) * P],
                                   R[:, ds(bs[u] * (2 * NH), 2 * NH)], start=True, stop=True)
                mm.then_inc(re_mm[b], 1)

            def sums(i, b):
                pe.wait_ge(msg_ok[b], i + 1)
                for u in range(UG):
                    pe.wait_ge(acc2_ok[(b - 1) % BUF], LEAD + i * UG + (u + 1 if b else 0))
                    pe.matmul(bank[u][:, 0:AGG], S2[b][:, u, :], G2[b][:, u, :],
                              start=True, stop=True).then_inc(acc2_mm[b], 1)

            pe.wait_ge(r_ready, 1)
            regs = [pe.alloc_register(f"pe_b{k}") for k in range(BUF * UG)]

            def buckets(at):
                pe.load(regs, bucket_row[1][0:1, at])
                return [pe.snap(r, min_val=0, max_val=NB - 1) for r in regs]

            turn_targets(0, 0)
            turn_targets(0, 1)
            bs = buckets(slice(0, BUF * UG))
            rows_of_edges(0, 0, bs[0:UG])

            def pe_round(i, last):
                bs = buckets(ds(i * (BUF * UG) + UG, BUF * UG))
                for b in range(BUF):
                    if b < 2 or not last:
                        turn_targets(i + (b + 2) // BUF, (b + 2) % BUF)
                    if b < 3 or not last:
                        rows_of_edges(i + (b + 1) // BUF, (b + 1) % BUF, bs[b * UG:(b + 1) * UG])
                    sums(i, b)

            with pe.Fori(0, rounds4 - 1) as i:
                pe_round(i, False)
            pe_round(rounds4 - 1, True)

            pe.wait_ge(w1_in, 16 * 3 * NX)
            experts(1)


        @block.scalar
        def _(act):
            act.wait_ge(const_set, NCONST)
            act.wait_ge(par_T, 1)
            act.activation(par[:, 0:P + 64], bank[0][:, 0:P + 64], ACT.Copy)
            nrow = 4 * D + 2 * NX
            for k in range(3):
                a, b = 512 * k, min(512 * k + 512, nrow)
                cp = act.activation(bc[:, a:b], bank[1 + k][:, 0:b - a], ACT.Copy)
            cp.then_inc(par_ok, 1)
            act.wait_ge(par_ok, 1)
            for j, c in enumerate((64, 144)):
                act.activation(bn_s[:, j, :], par[:, c:c + 16], ACT.Sqrt, bias=eps_bn[:, 0:1]).then_inc(bn_sq, 1)

            def norm(i):
                act.activation(h_t, X[:, ds(i * D, D)], ACT.Identity, bias=nbias[:, ds(i, 1)],
                               scale=rstd[:, ds(i, 1)]).then_inc(t_h, 1)

            def table(layer):
                tb, hb, nb = layer * (NT + 1), layer * (NT + 1), (4, 1)[layer]

                def turned(i):
                    act.wait_ge(t_tr, i + (tb + 1))
                    act.activation(hT_t, bank[7][:, 0:D], ACT.Copy).then_inc(t_hT, 1)

                def evacuate(i, b, k):
                    if layer == 0:
                        act.wait_ge(t_mm, i * 4 + (k + 1))
                        o = tbl[b].rearrange("p (r d) -> p r d", d=D)[:, 4 * (k % 2):4 * (k % 2) + 4,
                                                                      (k // 2) * P:(k // 2 + 1) * P]
                        act.activation(o, bank[k][:, :].rearrange("p (r o) -> p r o", o=P), ACT.Copy).then_inc(t_ev[k], 1)
                    else:
                        act.wait_ge(t_mm, i + (4 * NT + 1))
                        act.activation(tb1[b], bank[0][:, 0:WG], ACT.Copy).then_inc(t_ev[0], 1)

                act.wait_ge(t_stats, layer + 1)
                act.activation(rstd[:, 0:NT], mv[:, :, 1], ACT.Sqrt, bias=eps_ln[:, 0:1]).then_inc(t_sqrt, 1)
                act.wait_ge(t_rstd, layer + 1)
                norm(0)
                turned(0)
                norm(1)

                def tile_rows(i, h, b):
                    act.wait_ge(t_out[b], h * 16 + (RB + layer * stores[b]))
                    if layer == 1:
                        act.wait_ge(hrl_ok, LEAD + i)
                    for k in range(nb - 1):
                        evacuate(i, b, k)
                    turned(i + 1)
                    norm(i + 2)
                    evacuate(i, b, nb - 1)

                with act.Fori(0, NT // 2) as i:
                    tile_rows(i * 2, i, 0)
                    tile_rows(i * 2 + 1, i, 1)
                tile_rows(NT - 1, NT // 2, 0)

            table(0)

            def experts(layer):
                hn = 2 * 4 * NX
                yb, mb, hb = layer * NG * YT, layer * NG * YM, layer * NG * hn

                def root(j):
                    act.wait_ge(ln_var, j)
                    act.activation(rstd[:, 0:GT], mv[:, 0:GT, 1], ACT.Sqrt, bias=eps_ln[:, 0:1]).then_inc(ln_sd, 1)

                def group(g, last):
                    gg = g + layer * NG
                    nr = 2 - layer
                    act.wait_ge(xn_tr, gg + 1)
                    act.activation(xnT[:, 0:512], bank[0][:, :], ACT.Copy)
                    act.activation(xnT[:, 512:1024], bank[1][:, :], ACT.Copy)
                    act.activation(xnT[:, 1024:KD * GC], bank[2][:, 0:KD * GC - 1024], ACT.Copy).then_inc(xnT_ok, 1)
                    for e in range(NX):
                        act.wait_ge(y_mm, LEAD + g * YM + (mb + (len(UNITS) * (e - 1) if e >= 2 else 0)))
                        for c in range(4):
                            r = 4 * e + c
                            for j in range(2):
                                act.wait_ge(hid_mm, g * hn + (hb + 2 * r + j + 1))
                                o = hid[:, e % 2, c, j * HG:(j + 1) * HG]
                                i_ = bank[2 * (r % 2) + j][:, 0:HG]
                                if layer == 0:
                                    act.activation(o, i_, ACT.Gelu, bias=par[:, 160 + r:161 + r]).then_inc(hid_ok, 1)
                                else:
                                    q = 2 * e + c % 2
                                    act.activation(o, i_, ACT.Relu, bias=bn_t[:, c // 2, q:q + 1],
                                                   scale=bn_s[:, c // 2, q:q + 1]).then_inc(hid_ok, 1)
                            if e == 2 and c == 1:
                                act.wait_ge(wT_tr, gg + 1)
                                act.activation(wT[:, 0:512], bank[7][0:NX, :], ACT.Copy)
                                act.activation(wT[:, 512:GC], bank[6][0:NX, 256:384], ACT.Copy).then_inc(wT_ok, 1)
                        if e == 0:
                            act.wait_ge(gate_in, gg + 1)
                            if layer == 0:
                                act.activation(gsm[:, 1, :], gsm[:, 0, :], ACT.Exp).then_inc(gate_exp, 1)
                            else:
                                act.activation(wf2[:, :, :], lg[:, :, :], ACT.Exp).then_inc(gate_exp, 1)
                        if not last and (e == 4 or (e == 5 and layer == 0)):
                            root(g * nr + (layer * 2 * NG + nr + 1 + (e - 4)))

                for j in range(2 - layer):
                    root(layer * 2 * NG + j + 1)
                with act.Fori(0, NG - 1) as g:
                    group(g, False)
                group(NG - 1, True)

            experts(0)
            table(1)

            def copy_turned(i, b):
                act.wait_ge(st_tr[b], i + 1)
                act.activation(ST[b], bank[4 + b % 2][:, :], ACT.Copy).then_inc(st_ok[b], 1)

            def exponentials(i, b):
                act.wait_ge(e_in[b], LEAD + i + 1)
                act.activation(G2[b][:, :, D:AGG], ez[:, 0, b, :, :], ACT.Exp).then_inc(e_exp[b], 1)

            act.activation(pause[:, 1:2], eps_ln[:, 0:1], ACT.Exp)
            for b in range(2):
                act.wait_ge(t_out[b], RB + 2 * stores[b])
            copy_turned(0, 0)
            copy_turned(0, 1)
            exponentials(0, 0)

            def act_round(i, last):
                for b in range(BUF):
                    if b < 2 or not last:
                        copy_turned(i + (b + 2) // BUF, (b + 2) % BUF)
                    if b < 3 or not last:
                        exponentials(i + (b + 1) // BUF, (b + 1) % BUF)

            with act.Fori(0, rounds4 - 1) as i:
                act_round(i, False)
            act_round(rounds4 - 1, True)

            experts(1)

        @block.vector
        def _(dve):
            step = Steps(dve, vec_step)

            def all_stats(layer):
                for t in range(NT):
                    last = dve.bn_stats(stats[:, t, :], X3[:, t, :])
                step.done(last)
                step.settle()
                for t in range(NT):
                    last = dve.bn_aggr(mv[:, t, :], stats[:, t, :])
                last.then_inc(t_stats, 1)
                dve.wait_ge(t_sqrt, layer + 1)
                step.done(dve.reciprocal(rstd[:, 0:NT], rstd[:, 0:NT]))
                step.settle()
                dve.scalar_tensor_tensor(out=nbias[:, 0:NT], in0=mv[:, :, 0], scalar=-1.0, in1=rstd[:, 0:NT],
                                         op0=ALU.mult, op1=ALU.mult).then_inc(t_rstd, 1)

            dve.wait_ge(const_set, NCONST)
            dve.wait_ge(x_in, 32)
            all_stats(0)

            def keys(w):
                key = ints[w]
                other = ints[1 - w]
                a, b = ints[4], ints[5]
                step.done(dve.tensor_scalar(a, key, 7, None, ALU.arith_shift_right))
                step.done(dve.tensor_scalar(b, key, P - 1, None, ALU.bitwise_and))
                step.settle()
                step.done(dve.tensor_copy(bucket_f, a))
                step.settle()
                if w == 0:
                    step.done(dve.scalar_tensor_tensor(out=a, in0=other, scalar=float(NR), in1=ints[2],
                                                       op0=ALU.mult, op1=ALU.add))
                    step.settle()
                    step.done(dve.scalar_tensor_tensor(out=a, in0=a, scalar=float(P), in1=b,
                                                       op0=ALU.mult, op1=ALU.add))
                else:
                    step.done(dve.tensor_scalar(b, b, 1.0, None, ALU.add))
                    step.settle()
                    step.done(dve.scalar_tensor_tensor(out=a, in0=other, scalar=float(2 * P), in1=b,
                                                       op0=ALU.mult, op1=ALU.add))
                step.settle()
                if w == 0:
                    step.done(dve.tensor_copy(record[:, :, 0], a))
                    step.done(dve.tensor_copy(record[:, :, 1], ints[3]))
                else:
                    mask = (1 << PIECE) - 1
                    step.done(dve.tensor_scalar(b, a, mask, None, ALU.bitwise_and))
                    step.settle()
                    step.done(dve.tensor_copy(vals[:, 0, :], b))
                    step.settle()
                    step.done(dve.tensor_scalar(b, a, PIECE, mask, ALU.logical_shift_right, ALU.bitwise_and))
                    step.settle()
                    step.done(dve.tensor_copy(vals[:, 1, :], b))
                step.done(dve.tensor_tensor(onehot_b3, bucket_f.unsqueeze(1).to_broadcast([P, NB, EC]),
                                            iota_b[:, :].unsqueeze(2).to_broadcast([P, NB, EC]), ALU.is_equal))
                step.settle()
                step.done(dve.tensor_tensor_scan(count_b, ones[:, 0:1].to_broadcast([P, NB * EC]), onehot_b, 0.0,
                                                 ALU.mult, ALU.add))
                step.settle()
                step.done(dve.tensor_copy(totals[:, 0, 0:1], count_b3[:, 0:1, EC - 1]))
                step.done(dve.tensor_copy(totals[:, 1, :], count_b3[:, :, EC - 1]))
                step.settle()
                dve.tensor_tensor(totals[:, 0, 1:NB], totals[:, 1, 1:NB], totals[:, 1, 0:NB - 1],
                                  ALU.subtract).then_inc(tot_in, 1)
                dve.wait_ge(tot_ok, w + 1)
                step.done(dve.tensor_scalar(tiles_i[:, 0, :], bank[6][:, 32:32 + NB], float(P - 1), None, ALU.add))
                step.settle()
                step.done(dve.tensor_scalar(tiles_i[:, 1, :], tiles_i[:, 0, :], 7, None, ALU.arith_shift_right))
                step.settle()
                step.done(dve.tensor_copy(totals[:, 2, :], tiles_i[:, 1, :]))
                step.settle()
                step.done(dve.tensor_tensor_scan(totals[:, 3, :], ones[:, 0:NB], totals[:, 2, :], 0.0,
                                                 ALU.mult, ALU.add))
                step.settle()
                step.done(dve.tensor_tensor(totals[:, 4, :], totals[:, 3, :], totals[:, 2, :], ALU.subtract))
                step.settle()
                step.done(dve.scalar_tensor_tensor(out=totals[:, 5, :], in0=totals[:, 4, :], scalar=float(P),
                                                   in1=bank[6][:, 0:NB], op0=ALU.mult, op1=ALU.add))
                step.settle()
                step.done(dve.tensor_tensor(totals[:, 5, 1:NB], totals[:, 5, 1:NB], totals[:, 1, 0:NB - 1],
                                            ALU.subtract))
                step.settle()
                step.done(dve.tensor_tensor(count_b3, count_b3,
                                            totals[:, 5, :].unsqueeze(2).to_broadcast([P, NB, EC]), ALU.add))
                step.settle()
                step.done(dve.tensor_tensor(onehot_b, onehot_b, count_b, ALU.mult))
                step.settle()
                step.done(dve.tensor_reduce(bucket_f, onehot_b.rearrange("p (b c) -> p c b", c=EC), AX, ALU.add))
                step.settle()
                step.done(dve.tensor_scalar(a, bucket_f, -1.0, None, ALU.add))
                step.settle()
                step.done(dve.tensor_scalar(b, a, P - 1, None, ALU.bitwise_and))
                step.settle()
                step.done(dve.tensor_copy(slot_f[:, :], b))
                step.settle()
                step.done(dve.tensor_scalar(b, a, 7, None, ALU.arith_shift_right))
                step.settle()
                step.done(dve.tensor_copy(tile_f[:, :], b))
                if w == 0:
                    step.settle()
                    step.done(dve.scalar_tensor_tensor(out=slot_f[:, :], in0=slot_f[:, :], scalar=float(T),
                                                       in1=tile_f[:, :], op0=ALU.mult, op1=ALU.add))
                    step.settle()
                    step.done(dve.scalar_tensor_tensor(out=tile_f[:, :], in0=bucket_f, scalar=0.0, in1=dump[:, :],
                                                       op0=ALU.is_equal, op1=ALU.mult))
                    step.settle()
                    dve.tensor_tensor(place0[:, :], slot_f[:, :], tile_f[:, :], ALU.add).then_inc(record_ok, 1)
                at = arena[0:1, 0:T * (NB - 1)].rearrange("p (t b) -> p t b", b=NB - 1)
                row = arena[0:1, T * NB:T * NB + T]
                step.done(dve.tensor_tensor(at, iota_tile[0:1, :].unsqueeze(2).to_broadcast([1, T, NB - 1]),
                                            totals[0:1, 4, 1:NB].unsqueeze(1).to_broadcast([1, T, NB - 1]), ALU.is_ge))
                step.settle()
                step.done(dve.tensor_reduce(row, at, AX, ALU.add))
                step.settle()
                step.done(dve.tensor_copy(bucket_row[w][:, 0:T], row))
                step.settle()

            def sort1():
                def group(j):
                    for u in range(4):
                        c = j * 4 + u
                        dve.wait_ge(oh_used[u], LEAD + j)
                        dve.tensor_scalar(tile_oh[u], iota_tile[:, :], tile_f[:, ds(c, 1)], None, ALU.is_equal)
                        for f in range(2):
                            last = dve.tensor_scalar(slot_oh[u][:, f * P:(f + 1) * P], iota_slot[:, :],
                                                     slot_f[:, ds(c, 1)], vals[:, f, ds(c, 1)],
                                                     ALU.is_equal, ALU.mult)
                        last.then_inc(oh_ready[u], 1)

                with dve.Fori(0, EC // 4) as j:
                    group(j)
                for u in range(4):
                    dve.wait_ge(oh_used[u], LEAD + EC // 4)

                step.done(dve.tensor_copy(wordf[0], bank[0][:, 0:T]))
                step.settle()
                step.done(dve.scalar_tensor_tensor(out=words[:, 0, :], in0=bank[1][:, 0:T], scalar=float(1 << PIECE),
                                                   in1=wordf[0], op0=ALU.mult, op1=ALU.add))
                step.settle()
                step.done(dve.tensor_scalar(idx1[:, 0:T], words[:, 0, :], 8, None, ALU.logical_shift_right))
                step.done(dve.tensor_scalar(words[:, 1, :], words[:, 0, :], 2 * P - 1, None, ALU.bitwise_and))
                step.settle()
                dve.tensor_scalar(loc1[:, 0:T], words[:, 1, :], -1.0, None, ALU.add).then_inc(order_ok, 1)

            def decode0():
                dve.wait_ge(sorted_in, 16)
                step.done(dve.tensor_scalar(idx0[:, 0:T], sorted_sb[:, :, 0], 7, None, ALU.logical_shift_right))
                step.done(dve.tensor_scalar(words[:, 1, :], sorted_sb[:, :, 0], P - 1, None, ALU.bitwise_and))
                step.done(dve.tensor_copy(wgt0[:, 0:T], sorted_sb[:, :, 1]))
                step.settle()
                dve.tensor_copy(loc0[:, 0:T], words[:, 1, :]).then_inc(order_ok, 1)

            dve.wait_ge(edges_in, 16 * 8)
            keys(0)
            keys(1)
            sort1()
            dve.wait_ge(bn_sq, 2)
            step.done(dve.reciprocal(bn_s[:, :, :], bn_s[:, :, :]))
            step.settle()
            for j, (cb, cg, cbe, cm) in enumerate(((0, 16, 32, 48), (80, 96, 112, 128))):
                step.done(dve.tensor_tensor(bn_s[:, j, :], bn_s[:, j, :], par[:, cg:cg + 16], ALU.mult))
                step.done(dve.tensor_tensor(bn_t[:, j, :], par[:, cb:cb + 16], par[:, cm:cm + 16], ALU.subtract))
                step.settle()
                step.done(dve.tensor_tensor(bn_t[:, j, :], bn_t[:, j, :], bn_s[:, j, :], ALU.mult))
                step.settle()
                step.done(dve.tensor_tensor(bn_t[:, j, :], bn_t[:, j, :], par[:, cbe:cbe + 16], ALU.add))

            regs = [dve.alloc_register(f"dve_b{k}") for k in range(2 * UG)]

            def buckets(w, i):
                dve.load(regs, bucket_row[w][0:1, ds(i * (2 * UG), 2 * UG)])
                return [dve.snap(r, min_val=0, max_val=NB - 1) for r in regs]

            decode0()
            dve.wait_ge(order_ok, 2)
            wgt0_f = wgt0[:, :].bitcast(F32)

            def weighted(i, off, b, used_at):
                if used_at is not None:
                    dve.wait_ge(g_used[b], LEAD + used_at)
                for u in range(UG):
                    c = i * (2 * UG) + (off * UG + u)
                    last = dve.tensor_scalar(S[b][:, u, :], iota_p[:, :], loc0[:, ds(c, 1)], wgt0_f[:, ds(c, 1)],
                                             ALU.is_equal, ALU.mult)
                last.then_inc(s_ready[b], 1)

            def add_up(i, b, bs, got, got_at, ok, view, target, width):
                for u in range(UG):
                    dve.wait_ge(got[b], LEAD + got_at(i, u))
                    if u:
                        dve.wait_ge(ok[b], LEAD + i * UG + u)
                    elif b:
                        dve.wait_ge(ok[0], LEAD + i * UG + UG)
                    else:
                        dve.wait_ge(ok[1], LEAD + i * UG)
                    t = target[:, ds(bs[b * UG + u] * width, width)]
                    dve.tensor_tensor(t, t, view(b, u), ALU.add).then_inc(ok[b], 1)

            weighted(0, 0, 0, None)
            with dve.Fori(0, rounds) as i:
                bs = buckets(0, i)
                def view(b, u):
                    return bank[2 * b + u // 2][:, (u % 2) * D:(u % 2 + 1) * D]
                weighted(i, 1, 1, i)
                add_up(i, 0, bs, g_used, lambda i, u: i + 1, acc_ok, view, X[:, :], D)
                weighted(i, 2, 0, i + 1)
                add_up(i, 1, bs, g_used, lambda i, u: i + 1, acc_ok, view, X[:, :], D)
            for b in range(2):
                dve.wait_ge(acc_ok[b], LEAD + rounds * UG)

            def experts(layer):
                yb, mb = layer * NG * YT, layer * NG * YM
                yslot = [bank[4 + t // 2][:, (t % 2) * D:(t % 2 + 1) * D] for t in range(GT)]
                nr = 2 - layer

                def ln(g, first):
                    gg = g + layer * NG
                    if not first:
                        dve.wait_ge(xn_tr, gg)
                    for k in range(nr):
                        for t in range(GT):
                            src_ = X[:, ds((g * GT + t) * D, D)] if k == 0 else xn[:, t, :]
                            last = dve.bn_stats(stats[:, t, :], src_)
                        step.done(last)
                        step.settle()
                        dve.memset(pause[:, 1:2], 0.0)
                        for t in range(GT):
                            last = dve.bn_aggr(mv[:, t, :], stats[:, t, :])
                        last.then_inc(ln_var, 1)
                        dve.wait_ge(ln_sd, g * nr + (layer * 2 * NG + k + 1))
                        step.done(dve.reciprocal(rstd[:, 0:GT], rstd[:, 0:GT]))
                        step.settle()
                        for t in range(GT):
                            src_ = X[:, ds((g * GT + t) * D, D)] if k == 0 else xn[:, t, :]
                            last = dve.tensor_scalar(xn[:, t, :], src_, mv[:, t, 0:1], rstd[:, t:t + 1],
                                                     ALU.subtract, ALU.mult)
                            if k < nr - 1 or layer == 0:
                                step.done(last)
                        if k < nr - 1 or layer == 0:
                            step.settle()
                    if layer == 0:
                        step.done(dve.tensor_tensor(xn, xn, gamma_b.unsqueeze(1).to_broadcast([P, GT, D]), ALU.mult))
                        step.settle()
                        last = dve.tensor_tensor(xn, xn, beta_b.unsqueeze(1).to_broadcast([P, GT, D]), ALU.add)
                    last.then_inc(xn_ok, 1)
                ln_steps = 2 * (2 + GT) + 1 if layer == 0 else 2

                def gates(g):
                    gg = g + layer * NG
                    n0 = step.n
                    dve.wait_ge(logit_ok, gg + 1)
                    logits = bank[7][:, 0:GT * NX].rearrange("p (t e) -> p t e", e=NX)
                    step.done(dve.tensor_tensor(lg[:, :, :], logits,
                                                br_b[layer].unsqueeze(1).to_broadcast([P, GT, NX]), ALU.add))
                    step.settle()
                    if layer == 0:
                        dve.memset(pause[:, 1:2], 0.0)
                        for t in range(GT):
                            step.done(dve.max(top[:, t, :], lg[:, t, :]))
                        step.settle()
                        dve.memset(pause[:, 1:2], 0.0)
                        for t in range(GT):
                            step.done(dve.max_index(topi[:, t, :], top[:, t, :], lg[:, t, :]))
                        step.settle()
                        step.done(dve.tensor_copy(topf[:, :, :], topi[:, :, :]))
                        dve.tensor_tensor(gsm[:, 0, :], top[:, :, 1], top[:, :, 0], ALU.subtract).then_inc(gate_in, 1)
                        dve.wait_ge(gate_exp, gg + 1)
                        step.done(dve.tensor_scalar(gsm[:, 2, :], gsm[:, 1, :], 1.0, None, ALU.add))
                        step.settle()
                        step.done(dve.reciprocal(gsm[:, 3, :], gsm[:, 2, :]))
                        step.settle()
                        step.done(dve.tensor_tensor(gsm[:, 0, :], gsm[:, 1, :], gsm[:, 3, :], ALU.mult))
                        step.settle()
                        for t in range(GT):
                            step.done(dve.tensor_scalar(wf[:, t, :], iota_x[:, :], topf[:, t, 0:1],
                                                        gsm[:, 3, t:t + 1], ALU.is_equal, ALU.mult))
                            step.done(dve.tensor_scalar(wf2[:, t, :], iota_x[:, :], topf[:, t, 1:2],
                                                        gsm[:, 0, t:t + 1], ALU.is_equal, ALU.mult))
                        step.settle()
                        dve.tensor_tensor(wf[:, :, :], wf[:, :, :], wf2[:, :, :], ALU.add).then_inc(gate_ok, 1)
                    else:
                        step.done(dve.tensor_reduce(gsm[:, 0, :], lg[:, :, :], AX, ALU.max))
                        step.settle()
                        dve.tensor_tensor(lg[:, :, :], lg[:, :, :],
                                          gsm[:, 0, :].unsqueeze(2).to_broadcast([P, GT, NX]),
                                          ALU.subtract).then_inc(gate_in, 1)
                        dve.wait_ge(gate_exp, gg + 1)
                        step.done(dve.tensor_reduce(gsm[:, 1, :], wf2[:, :, :], AX, ALU.add))
                        step.settle()
                        step.done(dve.reciprocal(gsm[:, 2, :], gsm[:, 1, :]))
                        step.settle()
                        dve.tensor_tensor(wf[:, :, :], wf2[:, :, :],
                                          gsm[:, 2, :].unsqueeze(2).to_broadcast([P, GT, NX]),
                                          ALU.mult).then_inc(gate_ok, 1)
                    dve.wait_ge(gate_ok, gg + 1)
                gate_steps = 1 + 2 * GT + 1 + 3 + 2 * GT if layer == 0 else 4

                def group(g, last):
                    gates(g)
                    for e in range(NX + 1):
                        for t in range(GT):
                            n = 5 * e + t
                            xt = X[:, ds((g * GT + t) * D, D)]
                            dve.wait_ge(y_mm, LEAD + g * YM + (mb + len(UNITS) * e + t // 2 + 1))
                            if e:
                                dve.wait_ge(y_ok, LEAD + g * YT + (yb + n - GT + 1))
                            if e < NX:
                                dve.scalar_tensor_tensor(out=xt, in0=yslot[t], scalar=wf[:, t, e:e + 1], in1=xt,
                                                         op0=ALU.mult, op1=ALU.add).then_inc(y_ok, 1)
                            else:
                                dve.tensor_tensor(xt, yslot[t], xt, ALU.add).then_inc(y_ok, 1)
                        if e == 3 and not last:
                            ln(g + 1, False)

                ln(0, layer == 0)
                with dve.Fori(0, NG - 1) as g:
                    step.enter(g, gate_steps + ln_steps)
                    group(g, False)
                step.leave(NG - 1)
                group(NG - 1, True)

            experts(0)
            dve.wait_ge(y_ok, LEAD + NG * YT)

            dve.wait_ge(wg_in, 16)
            for k in range(KD):
                for j, a in enumerate((ar_b, al_b)):
                    step.done(dve.tensor_tensor(prod, Wg_sb[:, k, 0:D], a, ALU.mult))
                    step.settle()
                    last = step.done(dve.tensor_reduce(Wg_sb[:, k, D + j * NH:D + (j + 1) * NH],
                                                       prod.rearrange("p (h d) -> p h d", d=DH), AX, ALU.add))
                    step.settle()
            dve.memset(pause[:, 1:2], 0.0).then_inc(wa_ok, 1)
            all_stats(1)

            def copy_hr(i, b):
                dve.wait_ge(t_ev[0], LEAD + i + (NT + 1))
                dve.tensor_copy(HRL[:, ds(i, 1), :], tb1[b][:, D:WG].unsqueeze(1)).then_inc(hrl_ok, 1)

            with dve.Fori(0, NT // 2) as i:
                copy_hr(i * 2, 0)
                copy_hr(i * 2 + 1, 1)
            copy_hr(NT - 1, 0)
            dve.wait_ge(hrl_ok, LEAD + NT)

            def others(i, off, b, used_at):
                if used_at is not None:
                    dve.wait_ge(m_mm[b], LEAD + used_at)
                dve.tensor_tensor(notS[b], iota_p[:, :].unsqueeze(1).to_broadcast([P, UG, P]),
                                  loc1[:, ds(i * (2 * UG) + off * UG, UG)].unsqueeze(2).to_broadcast([P, UG, P]),
                                  ALU.not_equal).then_inc(nots_ok[b], 1)

            def maxima(i, b, bs):
                for u in range(UG):
                    dve.wait_ge(m_mm[b], LEAD + i + 1)
                    dve.tensor_reduce(tmx[:, b, u, :], bank[4 * b + u][:, :].rearrange("p (h j) -> p h j", j=P),
                                      AX, ALU.max).then_inc(m_red[b], 1)
                for u in range(UG):
                    dve.wait_ge(m_red[b], LEAD + i * UG + u + 1)
                    if u:
                        dve.wait_ge(m_ok[b], LEAD + i * UG + u)
                    elif b:
                        dve.wait_ge(m_ok[0], LEAD + i * UG + UG)
                    else:
                        dve.wait_ge(m_ok[1], LEAD + i * UG)
                    m = M[:, ds(bs[b * UG + u] * NH, NH)]
                    dve.tensor_tensor(m, m, tmx[:, b, u, :], ALU.max).then_inc(m_ok[b], 1)

            others(0, 0, 0, None)
            with dve.Fori(0, rounds) as i:
                bs = buckets(1, i)
                others(i, 1, 1, i)
                maxima(i, 0, bs)
                others(i, 2, 0, i + 1)
                maxima(i, 1, bs)
            for b in range(2):
                dve.wait_ge(m_ok[b], LEAD + rounds * UG)

            M3 = M[:, :].rearrange("p (t h) -> p t h", h=NH)
            R3 = R[:, :].rearrange("p (t h) -> p t h", h=2 * NH)
            step.done(dve.memset(ACC, 0.0))
            step.done(dve.tensor_copy(R3[:, :, 0:NH], HRL[:, :, NH:2 * NH]))
            step.settle()
            step.done(dve.tensor_tensor(M3, M3, HRL[:, :, NH:2 * NH], ALU.add))
            step.settle()
            dve.scalar_tensor_tensor(out=R3[:, :, NH:2 * NH], in0=M3, scalar=SLOPE, in1=M3, op0=ALU.mult,
                                     op1=ALU.max).then_inc(r_ready, 1)

            def targets(i, b):
                dve.tensor_tensor(S2[b], iota_p[:, :].unsqueeze(1).to_broadcast([P, UG, P]),
                                  loc1[:, ds(i * (BUF * UG) + b * UG, UG)].unsqueeze(2).to_broadcast([P, UG, P]),
                                  ALU.is_equal).then_inc(s2_ready[b], 1)

            def logits(i, b):
                re = bank[6 + b % 2][:, 0:UG * 2 * NH].rearrange("p (u h) -> p u h", h=2 * NH)
                z, y = ez[:, 1, b, :, :], ez[:, 0, b, :, :]
                dve.wait_ge(g2_in[b], i * 64 + 64)
                dve.wait_ge(re_mm[b], i + 1)
                step.done(dve.tensor_tensor(z, re[:, :, 0:NH], G2[b][:, :, D:AGG], ALU.add))
                step.settle()
                step.done(dve.scalar_tensor_tensor(out=y, in0=z, scalar=SLOPE, in1=z, op0=ALU.mult, op1=ALU.max))
                step.settle()
                step.done(dve.tensor_tensor(z, y, re[:, :, NH:2 * NH], ALU.subtract))
                step.settle()
                dve.tensor_scalar(y, z, 1.0, None, ALU.min).then_inc(e_in[b], 1)

            def messages(i, b):
                dve.wait_ge(e_exp[b], LEAD + i + 1)
                g4 = G2[b][:, :, 0:D].rearrange("p u (h d) -> p u h d", d=DH)
                w4 = G2[b][:, :, D:AGG].unsqueeze(3).to_broadcast([P, UG, NH, DH])
                dve.tensor_tensor(g4, g4, w4, ALU.mult).then_inc(msg_ok[b], 1)

            def add_sums(i, b, bs):
                for u in range(UG):
                    dve.wait_ge(acc2_mm[b], LEAD + i * UG + (u + 1))
                    if u:
                        dve.wait_ge(acc2_ok[b], LEAD + i * UG + u)
                    else:
                        dve.wait_ge(acc2_ok[(b - 1) % BUF], LEAD + i * UG + (UG if b else 0))
                    t = ACC[:, ds(bs[u] * AGG, AGG)]
                    dve.tensor_tensor(t, t, bank[u][:, 0:AGG], ALU.add).then_inc(acc2_ok[b], 1)

            regs4 = [*regs, *(dve.alloc_register(f"dve_c{k}") for k in range(2 * UG))]
            for b in range(3):
                targets(0, b)
            logits(0, 0)

            def dve_round(i, last):
                dve.load(regs4, bucket_row[1][0:1, ds(i * (BUF * UG), BUF * UG)])
                bs = [dve.snap(r, min_val=0, max_val=NB - 1) for r in regs4]
                for b in range(BUF):
                    messages(i, b)
                    if b < 3 or not last:
                        logits(i + (b + 1) // BUF, (b + 1) % BUF)
                    if b < 1 or not last:
                        dve.wait_ge(acc2_mm[(b - 1) % BUF], LEAD + i * UG + (UG if b else 0))
                        targets(i + (b + 3) // BUF, (b + 3) % BUF)
                    add_sums(i, b, bs[b * UG:(b + 1) * UG])

            with dve.Fori(0, rounds4 - 1) as i:
                step.enter(i, 3 * BUF)
                dve_round(i, False)
            step.leave(rounds4 - 1)
            dve_round(rounds4 - 1, True)
            for b in range(BUF):
                dve.wait_ge(acc2_ok[b], LEAD + rounds4 * UG)
            acc3 = ACC.rearrange("p (t r) -> p t r", r=AGG)
            step.done(dve.tensor_scalar(M3, acc3[:, :, D:AGG], 1e-30, None, ALU.max))
            step.settle()
            step.done(dve.reciprocal(M[:, :], M[:, :]))
            step.settle()
            for h in range(NH):
                a = acc3[:, :, h * DH:(h + 1) * DH]
                step.done(dve.tensor_tensor(a, a, M3[:, :, h:h + 1].to_broadcast([P, NT, DH]), ALU.mult))
            step.settle()
            step.done(dve.tensor_tensor(X3[:, 0:NT, :], X3[:, 0:NT, :], acc3[:, :, 0:D], ALU.add))
            step.settle()

            experts(1)


_INS = ['x', 'src', 'dst', 'edge_type_8', 'edge_weight', 'L0_gnn_weight', 'L0_ffn_gamma', 'L0_ffn_beta',
        'L0_ffn_Wr', 'L0_ffn_br', 'L0_ffn_W1', 'L0_ffn_b1', 'L0_ffn_W2', 'L0_ffn_b2', 'L1_gnn_W', 'L1_gnn_a_l',
        'L1_gnn_a_r', 'L1_ffn_Wr', 'L1_ffn_br', 'L1_ffn_W1', 'L1_ffn_b1', 'L1_ffn_g1', 'L1_ffn_be1', 'L1_ffn_m1',
        'L1_ffn_v1', 'L1_ffn_W2', 'L1_ffn_b2', 'L1_ffn_g2', 'L1_ffn_be2', 'L1_ffn_m2', 'L1_ffn_v2', 'L1_ffn_Wo',
        'L1_ffn_bo']
_OUTS = [((3125, 256), 'float32')]


def kernel(**inputs):
    import numpy as _np
    import concourse.bacc as _bacc
    from concourse import mybir as _mybir
    from concourse.bass_utils import run_bass_kernel_spmd as _run

    nc = _bacc.Bacc("TRN2", target_bir_lowering=False, num_devices=1)
    arrays, args = {}, []
    for name in _INS:
        a = _np.ascontiguousarray(inputs[name])
        arrays[f"in_{name}_dram"] = a
        args.append(nc.dram_tensor(f"in_{name}_dram", a.shape, _mybir.dt.from_np(a.dtype), kind="ExternalInput").ap())
    for i, (shape, dtype) in enumerate(_OUTS):
        dt = _mybir.dt.from_np(_np.dtype(dtype))
        args.append(nc.dram_tensor(f"out_{i}_dram", shape, dt, kind="ExternalOutput").ap())
    program(nc, *args)
    r = _run(nc, [arrays], core_ids=[0])
    got = tuple(r.results[0][f"out_{i}_dram"] for i in range(len(_OUTS)))
    return got[0]
```

```python
from contextlib import ExitStack

import concourse.bass as bass
from concourse import mybir

ALU = mybir.AluOpType
ACT = mybir.ActivationFunctionType
AX = mybir.AxisListType.X
F32 = mybir.dt.float32
F16 = mybir.dt.float16
BF16 = mybir.dt.bfloat16
I32 = mybir.dt.int32
ds = bass.ds

P = 128
UG = 4
LN_EPS = 1e-5
BN_EPS = 1e-3
SLOPE = 0.2
FAR = -1e30
PIECE = 11


class Steps:

    def __init__(self, eng, sem):
        self.eng, self.sem, self.n = eng, sem, 0

    def done(self, ins):
        ins.then_inc(self.sem, 1)
        self.n = self.n + 1
        return ins

    def settle(self):
        self.eng.wait_ge(self.sem, self.n)

    def enter(self, i, per):
        self.start, self.per = self.n, per
        self.n = i * per + self.start

    def leave(self, rounds):
        self.n = self.start + self.per * rounds


def wait_from(eng, sem, value):
    if not isinstance(value, int) or value > 0:
        eng.wait_ge(sem, value)


def program(nc, x, src, dst, rel, wgt, w_rgcn, gamma, beta, Wr0, br0, W10, b10, W20, b20,
            Wg, a_l, a_r, Wr1, br1, W11, b11, g1, be1, m1, v1, W21, b21, g2, be2, m2, v2, Wo, bo, out):
    N, D = x.shape
    E = src.shape[0]
    NR = w_rgcn.shape[0]
    NX = W10.shape[0]
    H0 = W10.shape[2]
    NH, DH = a_l.shape[1], a_l.shape[2]
    SB = 32
    KD = D // P
    NT = -(-N // P)
    SC = 7
    EC = 4 * SC * -(-E // (4 * SC * P))
    BUF = 4
    T = BUF * UG * -(-(E + NT * (P - 1)) // (BUF * UG * P))
    TX = T + UG
    HC = H0 // P
    GT = 5
    NG = NT // GT
    GC = GT * P
    HG = GC // 2
    AGG = D + NH
    ROW = AGG
    WG = D + 2 * NH
    NB = NT
    TE = 2 * -(-(2 * NT * P + NX * (P - 1)) // (2 * P))
    ER = TE // 2
    RING = 6
    UNITS = [(0, 1), (2, 3), (4,)]
    YM = len(UNITS) * (NX + 1)
    YT = GT * (NX + 1)
    assert NT % GT == 0 and NR * D == 4 * 512 and D == NH * DH and NX == 8

    table0 = nc.dram_tensor("relation_table", (NT * P * NR, D), F32, kind="Internal").ap()
    table1 = nc.dram_tensor("gat_table", (NT * P, ROW), F32, kind="Internal").ap()
    sorted0 = nc.dram_tensor("sorted_edges", (P * T + P * EC, 2), I32, kind="Internal").ap()
    routed_x = nc.dram_tensor("routed_nodes", (TE * P, D), F32, kind="Internal").ap()
    routed_y = nc.dram_tensor("routed_outputs", (TE * P, D), F32, kind="Internal").ap()
    table_hr = nc.dram_tensor("hr_table", (NT * P, NH), F32, kind="Internal").ap()

    with ExitStack() as ctx:
        def sb(name, shape, dt=F32):
            return ctx.enter_context(nc.sbuf_tensor(name, shape, dt))

        def sem(name):
            return ctx.enter_context(nc.semaphore(name))

        bank = [ctx.enter_context(nc.psum_tensor(f"bank{i}", [P, 512], F32)) for i in range(8)]

        X = sb("X", [P, NT * D])
        X3 = X[:, :].rearrange("p (t d) -> p t d", d=D)
        arena = sb("arena", [P, 20480])
        work = sb("work", [P, 11584])
        W_rel = sb("W_rel", [P, KD, NR, P])
        vals = sb("vals", [P, 2, EC])
        slot_f = sb("slot_f", [P, EC])
        tile_f = sb("tile_f", [P, EC])
        record = sb("record", [P, EC, 2], I32)
        place0 = sb("place0", [P, EC], I32)
        sorted_sb = sb("sorted_sb", [P, T, 2], I32)
        stage_r = sb("stage_r", [P, 2, SC, 2], I32)
        stage_p = sb("stage_p", [P, 2, SC], I32)
        dump = sb("dump", [P, EC])
        neg_id = sb("neg_id", [P, P], BF16)

        ident = sb("ident", [P, P])
        ones = sb("ones", [P, P])
        lower = sb("lower", [P, P])
        iota_p = sb("iota_p", [P, P])
        iota_slot = sb("iota_slot", [P, P], F16)
        iota_tile = sb("iota_tile", [P, T], F16)
        iota_b = sb("iota_b", [P, NB])
        iota_x = sb("iota_x", [P, NX])
        eps_ln = sb("eps_ln", [P, 1])
        eps_bn = sb("eps_bn", [P, 1])

        idx0 = sb("idx0", [P, TX], I32)
        loc0 = sb("loc0", [P, TX])
        wgt0 = sb("wgt0", [P, TX], I32)
        idx1 = sb("idx1", [P, TX], I32)
        loc1 = sb("loc1", [P, TX])
        bucket_row = [sb(f"bucket_row{w}", [1, TX], I32) for w in range(2)]
        stage = sb("stage", [P, BUF * UG], I32)
        pause = sb("pause", [P, 2])

        totals = sb("totals", [P, 6, NB])
        tiles_i = sb("tiles_i", [P, 2, NB], I32)
        bc = sb("bc", [P, 4 * D + 2 * NX])
        gamma_b = bc[:, 0:D]
        beta_b = bc[:, D:2 * D]
        al_b = bc[:, 2 * D:3 * D]
        ar_b = bc[:, 3 * D:4 * D]
        br_b = [bc[:, 4 * D:4 * D + NX], bc[:, 4 * D + NX:4 * D + 2 * NX]]
        par = sb("par", [P, 192])
        bn_s = sb("bn_s", [P, 2, 2 * NX])
        bn_t = sb("bn_t", [P, 2, 2 * NX])
        Wr_sb = sb("Wr_sb", [P, 2, KD, NX])
        b2_sb = sb("b2_sb", [NX, D])
        TF = sb("TF", [P, NT, 2])
        W12 = sb("W12", [P, NT, 2])
        D12 = sb("D12", [P, 2, NT])
        place_x = sb("place_x", [P, 2, NT], I32)
        expert_row = sb("expert_row", [1, TE + 2], I32)

        stats = sb("stats", [P, NT, 6])
        mv = sb("mv", [P, NT, 2])
        rstd = sb("rstd", [P, NT])
        nbias = sb("nbias", [P, NT])
        lg = sb("lg", [P, GT, NX])
        top = sb("top", [P, GT, 8])
        topi = sb("topi", [P, GT, 8], mybir.dt.uint32)
        gsm = sb("gsm", [P, 4, GT])
        wf = sb("wf", [P, GT, NX])
        wf2 = sb("wf2", [P, GT, NX])
        wT = sb("wT", [NX, GC])

        HRL = sb("HRL", [P, NT, 2 * NH])
        M = sb("M", [P, (NT) * NH])
        R = sb("R", [P, NT * 2 * NH])
        hre = sb("hre", [P, BUF, UG * NH])
        tmx = sb("tmx", [P, BUF, UG, NH])
        ez = sb("ez", [P, 2, BUF, UG, NH])

        def wk(a, n):
            return work[:, a:a + n]
        tbl = [wk(0, NR * D), wk(7424, NR * D)]
        h_t = [wk(2048, D), wk(9536, D)]
        hT_t = [wk(2304, D), wk(9792, D)]
        ints = [wk(2560 + k * EC, EC).bitcast(I32) for k in range(6)]
        bucket_f = wk(2560 + 6 * EC, EC)
        oh0 = 5312
        tile_oh = [wk(oh0 + u * 528, 208).bitcast(F16) for u in range(4)]
        slot_oh = [wk(oh0 + u * 528 + 208, P).bitcast(F16) for u in range(4)]
        away = [wk(10048 + k * 208, 208).bitcast(F16) for k in range(2)]
        zeros = wk(10560, 2 * T).bitcast(I32)
        G = [[wk(7424 + (b * UG + u) * D, D) for u in range(UG)] for b in range(BUF)]
        S = [wk(b * 512, 512).rearrange("p (u r) -> p u r", r=P) for b in range(BUF)]
        words = wk(9536, 2 * T).bitcast(I32).rearrange("p (a t) -> p a t", a=2)
        wordf = [wk(9536 + 2 * T, T)]
        row_a = work[0:1, 7424:7424 + 4 * D + 2 * NX]
        par_a = wk(8480, P)
        par_b = work[0:32, 8608:8608 + P]
        SP0 = 3 * NX * KD * D
        G2 = [arena[:, SP0 + b * UG * ROW:SP0 + (b + 1) * UG * ROW].rearrange("p (u r) -> p u r", r=ROW)
              for b in range(BUF)]
        SP1 = SP0 + BUF * UG * ROW
        S2 = [arena[:, SP1 + b * 512:SP1 + (b + 1) * 512].rearrange("p (u r) -> p u r", r=P) for b in range(BUF)]
        ST = [wk(7424 + b * 512, 512) for b in range(BUF)]
        hid = arena[:, SP0:SP0 + 2 * HC * GC].rearrange("p (b c n) -> p b c n", b=2, c=HC)
        xn = wk(6528, GT * D).rearrange("p (t d) -> p t d", d=D)
        xnT = wk(7808, KD * GC)
        notS = [wk(9536 + b * 256, 256).bitcast(BF16).rearrange("p (u r) -> p u r", r=P)
                for b in range(BUF)]
        ACC = wk(0, NT * AGG)
        XN_all = wk(0, NT * D)
        XN3 = XN_all.rearrange("p (t d) -> p t d", d=D)
        hot = wk(9280, 2 * NX * NT).rearrange("p (k e t) -> p k e t", k=2, e=NX)
        hot_sum = wk(10080, NX * NT)
        hot_count = wk(10280, NX * NT)
        b1_b = wk(0, NX * H0)
        xt = [wk(6400 + b * D, D) for b in range(2)]
        xT = [wk(6912 + b * D, D) for b in range(2)]
        hp = [wk(7424 + b * H0, H0) for b in range(2)]
        hT = [wk(8448 + b * H0, H0) for b in range(2)]
        ys = [wk(9472 + b * D, D) for b in range(2)]
        ring = [wk(r * D, D) for r in range(RING)]
        tb1 = [wk(7424, WG), wk(7424 + 512, WG)]
        prod = wk(8704, D)

        onehot_b = arena[:, 0:NB * EC]
        onehot_b3 = onehot_b.rearrange("p (b c) -> p b c", c=EC)
        count_b = arena[:, NB * EC:2 * NB * EC]
        count_b3 = count_b.rearrange("p (b c) -> p b c", c=EC)
        W10_f = arena[:, 0:NX * KD * H0]
        W20_f = arena[:, NX * KD * H0:NX * KD * H0 + NX * HC * D]
        W10_sb = W10_f.rearrange("p (e k h) -> p e k h", e=NX, k=KD)
        W20_sb = W20_f.rearrange("p (e k h) -> p e k h", e=NX, k=HC)
        b2_b = arena[:, 2 * NX * KD * H0:2 * NX * KD * H0 + NX * D]
        W1_sb = [arena[:, j * NX * KD * D:(j + 1) * NX * KD * D].rearrange("p (e k h) -> p e k h", e=NX, k=KD)
                 for j in range(3)]
        Wg_sb = arena[:, 20480 - KD * WG:20480].rearrange("p (k h) -> p k h", k=KD)

        const_set = sem("const_set")
        pool_step = sem("pool_step")
        vec_step = sem("vec_step")
        act_step = sem("act_step")
        x_in = sem("x_in")
        edges_in = sem("edges_in")
        par_in = sem("par_in")
        wg_in = sem("wg_in")
        w0_in = sem("w0_in")
        w1_in = sem("w1_in")
        par_T = sem("par_T")
        par_ok = sem("par_ok")
        bn_sq = sem("bn_sq")
        t_stats = sem("t_stats")
        t_sqrt = sem("t_sqrt")
        t_rstd = sem("t_rstd")
        t_h = sem("t_h")
        t_tr = sem("t_tr")
        t_hT = sem("t_hT")
        t_mm = sem("t_mm")
        t_ev = [sem(f"t_ev{k}") for k in range(4)]
        t_out = [sem(f"t_out{b}") for b in range(2)]
        tot_in = sem("tot_in")
        tot_ok = sem("tot_ok")
        oh_ready = sem("oh_ready")
        places_ok = sem("places_ok")
        toh_ok = sem("toh_ok")
        oh_used = [sem(f"oh_used{u}") for u in range(4)]
        order_ok = sem("order_ok")
        zero_set = sem("zero_set")
        record_ok = sem("record_ok")
        zero_in = sem("zero_in")
        sc_done = [sem(f"sc_done{b}") for b in range(2)]
        sorted_in = sem("sorted_in")
        g_in = [sem(f"g_in{b}") for b in range(BUF)]
        g_used = [sem(f"g_used{b}") for b in range(BUF)]
        s_ready = sem("s_ready")
        acc_ok = [sem(f"acc_ok{b}") for b in range(BUF)]
        ln_var = sem("ln_var")
        ln_sd = sem("ln_sd")
        xn_ok = sem("xn_ok")
        xn_tr = sem("xn_tr")
        xnT_ok = sem("xnT_ok")
        logit_ok = sem("logit_ok")
        x1_ok = sem("x1_ok")
        lg_ok = sem("lg_ok")
        w_in = sem("w_in")
        w_exp = sem("w_exp")
        place_ok = sem("place_ok")
        experts_ok = sem("experts_ok")
        rx_zero = sem("rx_zero")
        rx_in = sem("rx_in")
        bias_in = sem("bias_in")
        xt_in = [sem(f"xt_in{b}") for b in range(2)]
        xt_tr = sem("xt_tr")
        xT_ok = sem("xT_ok")
        l1_mm = sem("l1_mm")
        hb_ok = sem("hb_ok")
        h_ok = sem("h_ok")
        h_tr = sem("h_tr")
        hT_ok = sem("hT_ok")
        l2_mm = sem("l2_mm")
        ye_ok = sem("ye_ok")
        ys_out = [sem(f"ys_out{b}") for b in range(2)]
        yg_in = [sem(f"yg_in{r}") for r in range(RING)]
        comb_ok = sem("comb_ok")
        gate_in = sem("gate_in")
        gate_exp = sem("gate_exp")
        gate_ok = sem("gate_ok")
        wT_tr = sem("wT_tr")
        wT_ok = sem("wT_ok")
        hid_mm = sem("hid_mm")
        hid_ok = sem("hid_ok")
        y_mm = sem("y_mm")
        y_ok = sem("y_ok")
        hrl_ok = sem("hrl_ok")
        wa_ok = sem("wa_ok")
        hrt_ok = sem("hrt_ok")
        hrt_out = sem("hrt_out")
        m_mm = [sem(f"m_mm{b}") for b in range(BUF)]
        m_red = [sem(f"m_red{b}") for b in range(BUF)]
        m_ok = sem("m_ok")
        r_ready = sem("r_ready")
        nots_ok = sem("nots_ok")
        g2_in = [sem(f"g2_in{b}") for b in range(BUF)]
        s2_ready = [sem(f"s2_ready{b}") for b in range(BUF)]
        st_tr = [sem(f"st_tr{b}") for b in range(BUF)]
        st_ok = [sem(f"st_ok{b}") for b in range(BUF)]
        re_mm = sem("re_mm")
        e_in = [sem(f"e_in{b}") for b in range(BUF)]
        e_exp = [sem(f"e_exp{b}") for b in range(BUF)]
        msg_ok = sem("msg_ok")
        acc2_mm = [sem(f"acc2_mm{b}") for b in range(BUF)]
        acc2_ok = [sem(f"acc2_ok{b}") for b in range(BUF)]
        stored = sem("stored")

        LEAD = UG
        led = [lg_ok, hid_ok, y_ok, y_mm, hrl_ok, *t_ev, *oh_used, *g_used, *acc_ok, *m_mm, *m_red, m_ok,
               *acc2_mm, *acc2_ok, *e_exp, *st_ok, *e_in]
        tails = (idx0, loc0, wgt0, idx1, loc1, *bucket_row)
        NCONST = 15 + 5 + len(tails)
        RB = 16 * (D // SB) // 2
        stores = [16 * -(-(NT - b) // 2) for b in range(2)]
        NPAR = 8 + 2 + 4 + 2 + 2 + 1
        rounds4 = T // (BUF * UG)
        scatters = EC // (2 * SC)
        block = ctx.enter_context(nc.Block())

        @block.sync
        def _(sp):
            full = (NT - 1) * P
            sp.wait_ge(const_set, NCONST)
            lastp = E // EC
            for k, a in enumerate((dst, src, rel, wgt.bitcast(I32))):
                sp.dma_start(ints[k][0:lastp, :], a[0:lastp * EC].rearrange("(p c) -> p c", c=EC)).then_inc(edges_in, 16)
                sp.dma_start(ints[k][lastp:lastp + 1, 0:E - lastp * EC],
                             a[lastp * EC:E].rearrange("(p c) -> p c", p=1)).then_inc(edges_in, 16)
            sp.dma_start(X3[:, 0:NT - 1, :], x[0:full, :].rearrange("(t p) d -> p t d", p=P)).then_inc(x_in, 16)
            sp.dma_start(X3[0:N - full, NT - 1, :], x[full:N, :]).then_inc(x_in, 16)
            for b in range(D // SB):
                q = b % (P // SB)
                sp.dma_start(W_rel[q * SB:(q + 1) * SB, b // (P // SB), :, q * SB:(q + 1) * SB],
                             w_rgcn[:, b * SB * SB:(b + 1) * SB * SB].rearrange("r (i o) -> i r o", o=SB)
                             ).then_inc(t_out[b % 2], 16)
            for k, a in enumerate((b11, g1, be1, m1, v1, b21, g2, be2)):
                sp.dma_start(par_a[16 * k:16 * k + 16, :], a.rearrange("e (c p) -> (e c) p", p=P)).then_inc(par_in, 16)
            for k, a in enumerate((m2, v2)):
                sp.dma_start(par_b[16 * k:16 * k + 16, :], a.rearrange("e (c p) -> (e c) p", p=P)).then_inc(par_in, 16)
            for a, o, n in ((gamma, 0, D), (beta, D, D), (br0, 4 * D, NX), (br1, 4 * D + NX, NX)):
                sp.dma_start(row_a[0:1, o:o + n], a.rearrange("(a n) -> a n", a=1)).then_inc(par_in, 16)
            for a, o in ((a_l, 2 * D), (a_r, 3 * D)):
                sp.dma_start(row_a[0:1, o:o + D], a.rearrange("a h d -> a (h d)")).then_inc(par_in, 16)
            for j, a in enumerate((Wr0, Wr1)):
                sp.dma_start(Wr_sb[:, j, :, :], a.rearrange("(k p) e -> p k e", p=P)).then_inc(par_in, 16)
            sp.dma_start(b2_sb[:, :], bo).then_inc(par_in, 16)

            sp.wait_ge(zero_set, 1)
            for b in range(2):
                sp.dma_start(sorted0[b * (P // 2) * T:(b + 1) * (P // 2) * T, :].rearrange("(p t) w -> p (t w)", t=T),
                             zeros[b * (P // 2):(b + 1) * (P // 2), :]).then_inc(zero_in, 16)

            def store_table0(i, b):
                for k in range(4):
                    sp.wait_ge(t_ev[k], LEAD + i + 1)
                sp.dma_start(table0[ds(i * (P * NR), P * NR), :].rearrange("(p r) d -> p (r d)", r=NR),
                             tbl[b]).then_inc(t_out[b], 16)

            with sp.Fori(0, NT // 2) as i:
                store_table0(i * 2, 0)
                store_table0(i * 2 + 1, 1)
            store_table0(NT - 1, 0)
            with sp.Fori(0, TE // 2) as q:
                sp.dma_start(routed_x[ds(q * (2 * P), 2 * P), :].rearrange("(p r) d -> p (r d)", r=2),
                             wk(10816, 2 * D)).then_inc(rx_zero, 16)
            for b in range(2):
                sp.wait_ge(sc_done[b], 16 * SC * scatters)
            sp.dma_start(sorted_sb[:, :, :], sorted0[0:P * T, :].rearrange("(p t) w -> p t w", t=T)).then_inc(sorted_in, 16)
            sp.wait_ge(order_ok, 1)
            for e in range(NX):
                sp.wait_ge(g_used[0], LEAD + e + 1)
                sp.dma_start(W10_sb[:, e], W10[e].rearrange("(k p) h -> p k h", p=P)).then_inc(w0_in, 16)
                sp.dma_start(W20_sb[:, e], W20[e].rearrange("(k p) h -> p k h", p=P)).then_inc(w0_in, 16)
            sp.dma_start(Wg_sb[:, :, 0:D], Wg.rearrange("(k p) h -> p k h", p=P)).then_inc(wg_in, 16)
            sp.dma_start(b2_b, b20.rearrange("e d -> (e d)").unsqueeze(0).to_broadcast([P, NX * D])).then_inc(bias_in, 16)
            sp.wait_ge(rx_in, 16 * 2 * NT)
            sp.dma_start(b1_b, b10.rearrange("e h -> (e h)").unsqueeze(0).to_broadcast([P, NX * H0])).then_inc(bias_in, 16)
            for b in range(2):
                sp.dma_start(xt[b], routed_x[b * P:(b + 1) * P, :]).then_inc(xt_in[b], 16)

            def store_outputs(i, b):
                sp.wait_ge(ye_ok, i + 1)
                sp.dma_start(routed_y[ds(i * P, P), :], ys[b]).then_inc(ys_out[b], 16)

            def load_and_store(j, first):
                for b in range(2):
                    sp.wait_ge(xt_tr, j * 2 + (b + 1))
                    sp.dma_start(xt[b], routed_x[ds(j * (2 * P) + (b + 2) * P, P), :]).then_inc(xt_in[b], 16)
                    if not first:
                        store_outputs(j * 2 + (b - 2), b)

            load_and_store(0, True)
            with sp.Fori(1, ER - 1) as j:
                load_and_store(j, False)
            for i in range(TE - 4, TE):
                store_outputs(i, i % 2)
            sp.wait_ge(l2_mm, TE)
            for e in range(NX):
                for j, a in enumerate((W11, W21, Wo)):
                    sp.dma_start(W1_sb[j][:, e], a[e].rearrange("(k p) h -> p k h", p=P)).then_inc(w1_in, 16)
            def store_table1(i, b):
                sp.wait_ge(t_ev[0], LEAD + i + (NT + 1))
                sp.dma_start(table1[ds(i * P, P), :], tb1[b][:, 0:ROW]).then_inc(t_out[b], 16)

            with sp.Fori(0, NT // 2) as i:
                store_table1(i * 2, 0)
                store_table1(i * 2 + 1, 1)
            store_table1(NT - 1, 0)
            sp.wait_ge(hrl_ok, LEAD + NT)
            sp.dma_start(table_hr[:, :].rearrange("(t p) h -> p t h", p=P), HRL[:, :, 0:NH]).then_inc(hrt_out, 16)
            with sp.Fori(0, NG - 1) as g:
                sp.wait_ge(y_ok, LEAD + g * YT + YT)
                sp.dma_start(out[ds(g * GC, GC), :].rearrange("(t p) d -> p t d", p=P),
                             X3[:, ds(g * GT, GT), :]).then_inc(stored, 16)
            sp.wait_ge(y_ok, LEAD + NG * YT)
            sp.dma_start(out[(NG - 1) * GC:full, :].rearrange("(t p) d -> p t d", p=P),
                         X3[:, (NG - 1) * GT:NT - 1, :]).then_inc(stored, 16)
            sp.dma_start(out[full:N, :], X3[0:N - full, NT - 1, :]).then_inc(stored, 16)
            sp.wait_ge(stored, 16 * (NG + 1))

        @block.gpsimd
        def _(pool):
            step = Steps(pool, pool_step)
            step.done(pool.memset(ident[:, :], 0.0))
            step.done(pool.memset(lower[:, :], 1.0))
            step.done(pool.memset(pause[:, 0:1], 0.0))
            step.done(pool.memset(neg_id[:, :], 0.0))
            pool.memset(zeros, 0).then_inc(zero_set, 1)
            for s in led:
                pool.sem_inc(s, LEAD)
            pool.memset(ones[:, :], 1.0).then_inc(const_set, 1)
            pool.memset(X[:, (NT - 1) * D:NT * D], 0.0).then_inc(const_set, 1)
            pool.memset(ints[0][:, :], -1).then_inc(const_set, 1)
            pool.memset(ints[1][:, :], -1).then_inc(const_set, 1)
            pool.memset(ints[2][:, :], 0).then_inc(const_set, 1)
            pool.memset(ints[3][:, :], 0).then_inc(const_set, 1)
            pool.memset(W_rel[:, :, :, :], 0.0).then_inc(const_set, 1)
            pool.memset(eps_ln[:, :], LN_EPS).then_inc(const_set, 1)
            pool.memset(eps_bn[:, :], BN_EPS).then_inc(const_set, 1)
            for a in tails:
                pool.memset(a[:, T:TX], 0).then_inc(const_set, 1)
            pool.memset(M[:, :], FAR).then_inc(const_set, 1)
            pool.memset(expert_row[:, :], 0).then_inc(const_set, 1)
            step.settle()
            pool.affine_select(out=ident[:, :], in_=ident[:, :], compare_op=ALU.not_equal, fill=1.0, base=0,
                               pattern=[[-1, P]], channel_multiplier=1).then_inc(const_set, 1)
            pool.affine_select(out=lower[:, :], in_=lower[:, :], compare_op=ALU.is_gt, fill=0.0, base=0,
                               pattern=[[1, P]], channel_multiplier=-1).then_inc(const_set, 1)
            pool.affine_select(out=neg_id[:, :], in_=neg_id[:, :], compare_op=ALU.not_equal, fill=FAR, base=0,
                               pattern=[[-1, P]], channel_multiplier=1).then_inc(const_set, 1)
            pool.iota(dump[:, :], pattern=[[1, EC]], base=P * T - ((P - 1) * T - 1), channel_multiplier=EC,
                      allow_small_or_imprecise_dtypes=True).then_inc(const_set, 1)
            for t, n in ((iota_p, P), (iota_slot, P), (iota_tile, T), (iota_b, NB), (iota_x, NX)):
                pool.iota(t[:, :], pattern=[[1, n]], base=0, channel_multiplier=0,
                          allow_small_or_imprecise_dtypes=True).then_inc(const_set, 1)

            def gathers(idx, table, dest, used, per, i, arrived, span):
                for b in range(0, BUF, span):
                    pool.wait_ge(used[b + span - 1], LEAD + i * per)
                    step.done(pool.tensor_copy(stage[:, b * UG:(b + span) * UG],
                                               idx[:, ds(i * (BUF * UG) + b * UG, span * UG)]))
                    step.settle()
                    pool.tensor_tensor(pause[:, 0:1], pause[:, 0:1], pause[:, 0:1], ALU.add)
                    for c in range(b, b + span):
                        for u in range(UG):
                            at = c * UG + u
                            pool.indirect_dma_start(dest[c][u], None, table,
                                                    bass.IndirectOffsetOnAxis(ap=stage[:, at:at + 1], axis=0)
                                                    ).then_inc(arrived[c], 16)

            pool.wait_ge(record_ok, 1)
            pool.wait_ge(zero_in, 32)

            def scatter(i, b, first):
                c = i * (2 * SC) + b * SC
                if not first:
                    pool.wait_ge(sc_done[b], i * (16 * SC))
                step.done(pool.tensor_copy(stage_p[:, b, :], place0[:, ds(c, SC)]))
                step.done(pool.tensor_copy(stage_r[:, b, :, :], record[:, ds(c, SC), :]))
                step.settle()
                pool.tensor_tensor(pause[:, 0:1], pause[:, 0:1], pause[:, 0:1], ALU.add)
                for u in range(SC):
                    pool.indirect_dma_start(sorted0, bass.IndirectOffsetOnAxis(ap=stage_p[:, b, u:u + 1], axis=0),
                                            stage_r[:, b, u, :], None).then_inc(sc_done[b], 16)

            for b in range(2):
                scatter(0, b, True)
            with pool.Fori(0, scatters - 1) as i:
                step.enter(i, 4)
                for b in range(2):
                    scatter(i + 1, b, False)
            step.leave(scatters - 1)

            for b in range(2):
                pool.wait_ge(t_out[b], RB + stores[b])
            pool.wait_ge(order_ok, 2)
            pool.wait_ge(rx_zero, 16 * (TE // 2))
            with pool.Fori(0, rounds4) as i:
                step.enter(i, BUF // 2)
                gathers(idx0, table0, G, g_used, 1, i, g_in, 2)
            step.leave(rounds4)
            for b in range(BUF):
                pool.wait_ge(g_used[b], LEAD + rounds4)

            pool.wait_ge(xn_ok, NG)
            pool.wait_ge(place_ok, 1)
            for t in range(NT):
                for k in range(2):
                    pool.indirect_dma_start(routed_x, bass.IndirectOffsetOnAxis(ap=place_x[:, k, t:t + 1], axis=0),
                                            XN_all[:, t * D:(t + 1) * D], None).then_inc(rx_in, 16)
            for b in range(2):
                pool.wait_ge(ys_out[b], 16 * ER)
            for n in range(2 * NT):
                if n >= RING:
                    pool.wait_ge(comb_ok, n - RING + 1)
                pool.indirect_dma_start(ring[n % RING], None, routed_y,
                                        bass.IndirectOffsetOnAxis(ap=place_x[:, n % 2, n // 2:n // 2 + 1], axis=0)
                                        ).then_inc(yg_in[n % RING], 16)
            pool.wait_ge(hrt_out, 16)
            with pool.Fori(0, rounds4) as i:
                step.enter(i, BUF // 2)
                gathers(idx1, table_hr, [[hre[:, b, u * NH:(u + 1) * NH] for u in range(UG)] for b in range(BUF)],
                        m_mm, 1, i, g_in, 2)
            step.leave(rounds4)
            for b in range(BUF):
                pool.wait_ge(m_mm[b], LEAD + rounds4)
            for b in range(2):
                pool.wait_ge(t_out[b], RB + 2 * stores[b])
            with pool.Fori(0, rounds4) as i:
                step.enter(i, BUF)
                gathers(idx1, table1, [[G2[b][:, u, :] for u in range(UG)] for b in range(BUF)],
                        acc2_mm, UG, i, g2_in, 1)
            step.leave(rounds4)

        @block.tensor
        def _(pe):
            pe.wait_ge(const_set, NCONST)
            pe.wait_ge(par_in, 16 * NPAR)
            pe.transpose(bank[0][:, 0:P], par_a[:, :], ident[:, :])
            pe.transpose(bank[0][:, P:P + 32], par_b[:, :], ident[0:32, 0:32])
            nrow = 4 * D + 2 * NX
            for k in range(3):
                a, b = 512 * k, min(512 * k + 512, nrow)
                mm = pe.matmul(bank[1 + k][:, 0:b - a], ones[0:1, :], row_a[0:1, a:b], start=True, stop=True)
            mm.then_inc(par_T, 1)

            def turn(i, b, layer):
                pe.wait_ge(t_h, i + (layer * NT + 1))
                for k in range(KD):
                    t = pe.transpose(bank[5 + 2 * b][:, k * P:(k + 1) * P], h_t[b][:, k * P:(k + 1) * P], ident[:, :])
                t.then_inc(t_tr, 1)

            def table(layer, product):
                for b in range(2):
                    turn(b, b, layer)

                def tile_rows(i, b, more):
                    pe.wait_ge(t_hT, i + (layer * NT + 1))
                    product(i, b)
                    if more:
                        turn(i + 2, b, layer)

                with pe.Fori(0, NT // 2 - 1) as i:
                    for b in range(2):
                        tile_rows(i * 2 + b, b, True)
                for i in range(NT - 3, NT):
                    tile_rows(i, i % 2, i + 2 < NT)

            def totals_mm(n):
                pe.wait_ge(tot_in, n)
                pe.matmul(bank[6][:, 0:NB], lower[:, :], totals[:, 0, :], start=True, stop=True)
                pe.matmul(bank[6][:, 32:32 + NB], ones[:, :], totals[:, 0, :], start=True, stop=True
                          ).then_inc(tot_ok, 1)

            totals_mm(1)
            for b in range(2):
                pe.wait_ge(t_out[b], RB)
            pe.wait_ge(par_ok, 1)

            def relations(i, b):
                for k in range(4):
                    pe.wait_ge(t_ev[k], LEAD + i)
                    half, c = k // 2, k % 2
                    pe.matmul(bank[k][:, :], hT_t[b][:, half * P:(half + 1) * P],
                              W_rel[:, half, 4 * c:4 * c + 4, :].rearrange("p r o -> p (r o)"),
                              start=True, stop=True).then_inc(t_mm, 1)

            table(0, relations)

            def sort_group(j, first, last):
                for u in range(4):
                    pe.wait_ge(oh_ready, j * 4 + (u + 1))
                    if u >= 2:
                        pe.wait_ge(toh_ok, j * 2 + (u - 1))
                    for f in range(2):
                        mm = pe.matmul(bank[f][:, 0:T], slot_oh[u][:, f * P:(f + 1) * P], tile_oh[u],
                                       start=(first and u == 0), stop=(last and u == 3))
                    mm.then_inc(oh_used[u], 1)

            totals_mm(2)
            for k in range(2):
                pe.wait_ge(t_ev[k], LEAD + NT)
            sort_group(0, True, False)
            with pe.Fori(1, EC // 4 - 1) as j:
                sort_group(j, False, False)
            sort_group(EC // 4 - 1, False, True)

            pe.wait_ge(order_ok, 2)
            with pe.Fori(0, rounds4) as i:
                for b in range(BUF):
                    pe.wait_ge(g_in[b], i * 64 + 64)
                    pe.wait_ge(s_ready, i * BUF + (b + 1))
                    pe.wait_ge(acc_ok[b], LEAD + i * UG)
                    for u in range(UG):
                        mm = pe.matmul(bank[2 * b + u // 2][:, (u % 2) * D:(u % 2 + 1) * D], S[b][:, u, :],
                                       G[b][u], start=True, stop=True)
                    mm.then_inc(g_used[b], 1)

            def turn_rows(rows, first_bank):
                for k in range(KD):
                    for t in range(GT):
                        q = k * GT + t
                        tr = pe.transpose(bank[first_bank + q // 4][:, (q % 4) * P:(q % 4 + 1) * P],
                                          rows[:, t, k * P:(k + 1) * P], ident[:, :])
                tr.then_inc(xn_tr, 1)

            def gate_logits(layer):
                for t in range(GT):
                    for k in range(KD):
                        mm = pe.matmul(bank[7][:, t * NX:(t + 1) * NX],
                                       xnT[:, k * GC + t * P:k * GC + (t + 1) * P], Wr_sb[:, layer, k, :],
                                       start=(k == 0), stop=(k == KD - 1))
                mm.then_inc(logit_ok, 1)

            for g in range(NG + 1):
                if g < NG:
                    pe.wait_ge(xn_ok, g + 1)
                    turn_rows(XN3[:, g * GT:(g + 1) * GT, :], 3 * (g % 2))
                if g:
                    pe.wait_ge(xnT_ok, g)
                    pe.wait_ge(lg_ok, LEAD + g - 1)
                    gate_logits(0)
            totals_mm(3)

            e_regs = [pe.alloc_register(f"pe_e{k}") for k in range(3)]

            def turn_nodes(i, b, at):
                pe.wait_ge(xt_in[b], at)
                wait_from(pe, xT_ok, i - 1)
                for k in range(KD):
                    tr = pe.transpose(bank[6 + b][:, k * P:(k + 1) * P], xt[b][:, k * P:(k + 1) * P], ident[:, :])
                tr.then_inc(xt_tr, 1)

            def first_layer(i, b, e):
                pe.wait_ge(xT_ok, i + 1)
                wait_from(pe, hb_ok, i - 1)
                for k in range(KD):
                    mm = pe.matmul(bank[b][:, 0:H0], xT[b][:, k * P:(k + 1) * P],
                                   W10_f[:, ds(e * (KD * H0) + k * H0, H0)], start=(k == 0), stop=(k == KD - 1))
                mm.then_inc(l1_mm, 1)

            def turn_hidden(i, b):
                pe.wait_ge(h_ok, i + 1)
                wait_from(pe, hT_ok, i - 1)
                for k in range(HC):
                    tr = pe.transpose(bank[2 + b][:, k * P:(k + 1) * P], hp[b][:, k * P:(k + 1) * P], ident[:, :])
                tr.then_inc(h_tr, 1)

            def second_layer(i, b, e):
                pe.wait_ge(hT_ok, i + 1)
                wait_from(pe, ye_ok, i - 1)
                for k in range(HC):
                    mm = pe.matmul(bank[4 + b][:, 0:D], hT[b][:, k * P:(k + 1) * P],
                                   W20_f[:, ds(e * (HC * D) + k * D, D)], start=(k == 0), stop=(k == HC - 1))
                mm.then_inc(l2_mm, 1)

            def expert_round(j, last):
                pe.load(e_regs, expert_row[0:1, ds(j * 2, 3)])
                es = [pe.snap(r, min_val=0, max_val=NX - 1) for r in e_regs]
                for b in range(2):
                    i = j * 2 + b
                    if not last:
                        turn_nodes(i + 2, b, j * 16 + 32)
                    turn_hidden(i, b)
                    if b == 0 or not last:
                        first_layer(i + 1, 1 - b, es[b + 1])
                    second_layer(i, b, es[b])

            pe.wait_ge(w0_in, 16 * 2 * NX)
            pe.wait_ge(experts_ok, 1)
            for b in range(2):
                turn_nodes(b, b, 16)
            pe.load(e_regs, expert_row[0:1, 0:3])
            first_layer(0, 0, pe.snap(e_regs[0], min_val=0, max_val=NX - 1))
            expert_round(0, False)
            with pe.Fori(1, ER - 1) as j:
                expert_round(j, False)
            expert_round(ER - 1, True)

            def experts():
                hn = 2 * 4 * NX
                yslot = [bank[4 + t // 2][:, (t % 2) * D:(t % 2 + 1) * D] for t in range(GT)]

                def group(g):
                    gg = g + NG
                    pe.wait_ge(xn_ok, gg + 1)
                    pe.wait_ge(hid_ok, LEAD + g * hn)
                    turn_rows(xn, 0)
                    pe.wait_ge(xnT_ok, gg + 1)

                    def hidden(e, c, weights, source):
                        r = 4 * e + c
                        pe.wait_ge(hid_ok, LEAD + g * hn + max(0, 2 * r - 2))
                        n = len(weights)
                        for j in range(2):
                            for k in range(n):
                                mm = pe.matmul(bank[2 * (r % 2) + j][:, 0:HG], weights[k], source(k, j),
                                               start=(k == 0), stop=(k == n - 1))
                            mm.then_inc(hid_mm, 1)

                    def x_in_cols(k, j):
                        return xnT[:, k * GC + j * HG:k * GC + (j + 1) * HG]

                    def first(e):
                        for c in range(KD):
                            hidden(e, c, [W1_sb[0][:, e, k, c * P:(c + 1) * P] for k in range(KD)], x_in_cols)

                    def second(e):
                        pe.wait_ge(hid_ok, LEAD + g * hn + (8 * e + 4))
                        for c in range(KD):
                            hidden(e, 2 + c, [W1_sb[1][:, e, k, c * P:(c + 1) * P] for k in range(KD)],
                                   lambda k, j: hid[:, e % 2, k, j * HG:(j + 1) * HG])

                    def outs(e):
                        pe.wait_ge(hid_ok, LEAD + g * hn + (8 * e + 8))
                        ks = range(2, 4)
                        for q, tiles in enumerate(UNITS):
                            pe.wait_ge(y_ok, LEAD + g * YT + (GT * (e - 1) + tiles[-1] + 1 if e else 0))
                            if e == 1 and q == 2:
                                pe.wait_ge(wT_ok, g + 1)
                            for t in tiles:
                                for k in ks:
                                    w = W1_sb[2][:, e, k - 2, :]
                                    mm = pe.matmul(yslot[t], hid[:, e % 2, k, t * P:(t + 1) * P], w,
                                                   start=(k == ks[0]), stop=(k == ks[-1]))
                            mm.then_inc(y_mm, 1)

                    first(0)
                    gate_logits(1)
                    second(0)
                    for e in range(NX):
                        if e + 1 < NX:
                            first(e + 1)
                        if e == 1:
                            pe.wait_ge(gate_ok, g + 1)
                            pe.wait_ge(y_ok, LEAD + g * YT + GT)
                            for t in range(GT):
                                o = bank[7][0:NX, t * P:(t + 1) * P] if t < 4 else bank[6][0:NX, 256:384]
                                tr = pe.transpose(o, wf[:, t, :], ident[:, :])
                            tr.then_inc(wT_tr, 1)
                        outs(e)
                        if e + 1 < NX:
                            second(e + 1)
                    for q, tiles in enumerate(UNITS):
                        pe.wait_ge(y_ok, LEAD + g * YT + (GT * (NX - 1) + tiles[-1] + 1))
                        for t in tiles:
                            mm = pe.matmul(yslot[t], wT[:, t * P:(t + 1) * P], b2_sb[:, :],
                                           start=True, stop=True)
                        mm.then_inc(y_mm, 1)

                with pe.Fori(0, NG) as g:
                    group(g)

            pe.wait_ge(wa_ok, 1)

            def projections(i, b):
                pe.wait_ge(t_ev[0], LEAD + i + (NT - 1))
                for k in range(KD):
                    mm = pe.matmul(bank[b][:, 0:WG], hT_t[b][:, k * P:(k + 1) * P], Wg_sb[:, k, :],
                                   start=(k == 0), stop=(k == KD - 1))
                mm.then_inc(t_mm, 1)

            table(1, projections)

            with pe.Fori(0, rounds4) as i:
                for b in range(BUF):
                    pe.wait_ge(g_in[b], i * 64 + 64 * (rounds4 + 1))
                    pe.wait_ge(nots_ok, i * BUF + (b + 1))
                    for u in range(UG):
                        pe.wait_ge(m_red[(b - 2) % BUF], LEAD + i * UG + (u + 1 if b >= 2 else 0))
                        o = bank[4 * (b % 2) + u]
                        pe.matmul(o[:, :].rearrange("p (h j) -> p h j", j=P), notS[b][:, u, :],
                                  neg_id[:, :].unsqueeze(1).to_broadcast([P, NH, P]), start=True, stop=False)
                        for h in range(NH):
                            c = u * NH + h
                            mm = pe.matmul(o[:, h * P:(h + 1) * P], hre[:, b, c:c + 1].to_broadcast([P, P]),
                                           ident[:, :], start=False, stop=(h == NH - 1))
                    mm.then_inc(m_mm[b], 1)

            def turn_targets(i, b, lead=0):
                pe.wait_ge(s2_ready[b], i + 1)
                pe.wait_ge(st_ok[(b - 2) % BUF], LEAD + i + (1 if b >= 2 else 0))
                for u in range(UG):
                    tr = pe.transpose(bank[4 + b % 2][:, u * P:(u + 1) * P], S2[b][:, u, :], ident[:, :])
                tr.then_inc(st_tr[b], 1)

            def rows_of_edges(i, b, bs):
                pe.wait_ge(st_ok[b], LEAD + i + 1)
                pe.wait_ge(e_in[(b - 2) % BUF], LEAD + i + (1 if b >= 2 else 0))
                for u in range(UG):
                    mm = pe.matmul(bank[6 + b % 2][:, u * 2 * NH:(u + 1) * 2 * NH], ST[b][:, u * P:(u + 1) * P],
                                   R[:, ds(bs[u] * (2 * NH), 2 * NH)], start=True, stop=True)
                mm.then_inc(re_mm, 1)

            def sums(i, b):
                pe.wait_ge(msg_ok, i * BUF + (b + 1))
                for u in range(UG):
                    pe.wait_ge(acc2_ok[(b - 1) % BUF], LEAD + i * UG + (u + 1 - (0 if b else UG)))
                    pe.matmul(bank[u][:, 0:AGG], S2[b][:, u, :], G2[b][:, u, :],
                              start=True, stop=True).then_inc(acc2_mm[b], 1)

            pe.wait_ge(r_ready, 1)
            regs = [pe.alloc_register(f"pe_b{k}") for k in range(UG)]

            def buckets(at):
                pe.load(regs, bucket_row[1][0:1, at])
                return [pe.snap(r, min_val=0, max_val=NB - 1) for r in regs]

            for b in range(3):
                turn_targets(0, b)
            for b in range(2):
                rows_of_edges(0, b, buckets(slice(b * UG, (b + 1) * UG)))

            def pe_round(i, last):
                for b in range(BUF):
                    if b < 2 or not last:
                        bs = buckets(ds(i * (BUF * UG) + (b + 2) * UG, UG))
                    sums(i, b)
                    if b < 2 or not last:
                        rows_of_edges(i + (b + 2) // BUF, (b + 2) % BUF, bs)
                    if b < 1 or not last:
                        turn_targets(i + (b + 3) // BUF, (b + 3) % BUF)

            with pe.Fori(0, rounds4 - 1) as i:
                pe_round(i, False)
            pe_round(rounds4 - 1, True)

            pe.wait_ge(w1_in, 16 * 3 * NX)
            experts()


        @block.scalar
        def _(act):
            act.wait_ge(const_set, NCONST)
            act.wait_ge(par_T, 1)
            act.activation(par[:, 0:P + 32], bank[0][:, 0:P + 32], ACT.Copy)
            nrow = 4 * D + 2 * NX
            for k in range(3):
                a, b = 512 * k, min(512 * k + 512, nrow)
                cp = act.activation(bc[:, a:b], bank[1 + k][:, 0:b - a], ACT.Copy)
            cp.then_inc(par_ok, 1)
            act.wait_ge(par_ok, 1)
            for j, c in enumerate((64, 144)):
                act.activation(bn_s[:, j, :], par[:, c:c + 16], ACT.Sqrt, bias=eps_bn[:, 0:1]).then_inc(bn_sq, 1)

            def roots(turn):
                act.wait_ge(t_stats, turn)
                act.activation(rstd[:, 0:NT], mv[:, :, 1], ACT.Sqrt, bias=eps_ln[:, 0:1]).then_inc(t_sqrt, 1)

            def norm(i, b):
                act.activation(h_t[b], X[:, ds(i * D, D)], ACT.Identity, bias=nbias[:, ds(i, 1)],
                               scale=rstd[:, ds(i, 1)]).then_inc(t_h, 1)

            def table(layer):
                def turned(i, b):
                    act.wait_ge(t_tr, i + (layer * NT + 1))
                    act.activation(hT_t[b], bank[5 + 2 * b][:, 0:D], ACT.Copy).then_inc(t_hT, 1)

                def evacuate(i, b, k):
                    if layer == 0:
                        act.wait_ge(t_mm, i * 4 + (k + 1))
                        o = tbl[b].rearrange("p (r d) -> p r d", d=D)[:, 4 * (k % 2):4 * (k % 2) + 4,
                                                                      (k // 2) * P:(k // 2 + 1) * P]
                        act.activation(o, bank[k][:, :].rearrange("p (r o) -> p r o", o=P), ACT.Copy).then_inc(t_ev[k], 1)
                    else:
                        act.wait_ge(t_mm, i + (4 * NT + 1))
                        act.activation(tb1[b], bank[b][:, 0:WG], ACT.Copy).then_inc(t_ev[0], 1)

                roots(layer * 3 + 1)
                act.wait_ge(t_rstd, layer * 3 + 1)
                norm(0, 0)
                norm(1, 1)
                turned(0, 0)
                norm(2, 0)
                turned(1, 1)

                def tile_rows(i, h, b, ahead):
                    act.wait_ge(t_out[b], h * 16 + (RB + layer * stores[b]))
                    if layer == 1:
                        act.wait_ge(hrl_ok, LEAD + i + (-1))
                    for k in range((4, 1)[layer]):
                        evacuate(i, b, k)
                    if ahead > 1:
                        turned(i + 2, b)
                    if ahead > 2:
                        norm(i + 3, 1 - b)

                with act.Fori(0, NT // 2 - 1) as i:
                    for b in range(2):
                        tile_rows(i * 2 + b, i, b, 3)
                for i in range(NT - 3, NT):
                    tile_rows(i, i // 2, i % 2, NT - 1 - i)

            table(0)

            step = Steps(act, act_step)
            act.wait_ge(places_ok, 1)
            with act.Fori(0, EC // 4) as j:
                step.enter(j, 2)
                for u in (2, 3):
                    act.wait_ge(oh_used[u], LEAD + j)
                    step.done(act.activation(away[u - 2], iota_tile[:, :], ACT.Abs, scale=-1.0,
                                             bias=tile_f[:, ds(j * 4 + u, 1)]))
                    step.settle()
                    act.activation(tile_oh[u], away[u - 2], ACT.Relu, scale=-1.0, bias=ones[:, 0:1]).then_inc(toh_ok, 1)
            step.leave(EC // 4)

            def root(j):
                act.wait_ge(ln_var, j)
                act.activation(rstd[:, 0:GT], mv[:, 0:GT, 1], ACT.Sqrt, bias=eps_ln[:, 0:1]).then_inc(ln_sd, 1)

            def turned_rows(gg, first_bank):
                act.wait_ge(xn_tr, gg + 1)
                for k in range(3):
                    a, b = 512 * k, min(512 * k + 512, KD * GC)
                    cp = act.activation(xnT[:, a:b], bank[first_bank + k][:, 0:b - a], ACT.Copy)
                cp.then_inc(xnT_ok, 1)

            roots(2)
            act.wait_ge(t_rstd, 2)
            with act.Fori(0, NT) as i:
                act.activation(XN_all[:, ds(i * D, D)], X[:, ds(i * D, D)], ACT.Identity, bias=nbias[:, ds(i, 1)],
                               scale=rstd[:, ds(i, 1)]).then_inc(x1_ok, 1)
            roots(3)
            for g in range(NG):
                if g:
                    act.wait_ge(logit_ok, g)
                turned_rows(g, 3 * (g % 2))
            act.wait_ge(w_in, 1)
            act.activation(D12[:, 1, :], D12[:, 0, :], ACT.Exp).then_inc(w_exp, 1)

            def turned_nodes(i, b):
                act.wait_ge(xt_tr, i + 1)
                wait_from(act, l1_mm, i - 1)
                act.activation(xT[b], bank[6 + b][:, 0:D], ACT.Copy).then_inc(xT_ok, 1)

            def gelu(i, b):
                act.wait_ge(hb_ok, i + 1)
                act.activation(hp[b], hp[b], ACT.Gelu).then_inc(h_ok, 1)

            def expert_round(j, last):
                for b in range(2):
                    i = j * 2 + b
                    if not last:
                        turned_nodes(i + 2, b)
                    if b == 0 or not last:
                        gelu(i + 1, 1 - b)

            for b in range(2):
                turned_nodes(b, b)
            gelu(0, 0)
            expert_round(0, False)
            with act.Fori(1, ER - 1) as j:
                expert_round(j, False)
            expert_round(ER - 1, True)

            def experts():
                hn = 2 * 4 * NX

                def group(g, last):
                    turned_rows(g + NG, 0)
                    for e in range(NX):
                        act.wait_ge(y_mm, LEAD + g * YM + (len(UNITS) * (e - 1) if e >= 2 else 0))
                        for c in range(4):
                            r = 4 * e + c
                            for j in range(2):
                                act.wait_ge(hid_mm, g * hn + (2 * r + j + 1))
                                o = hid[:, e % 2, c, j * HG:(j + 1) * HG]
                                i_ = bank[2 * (r % 2) + j][:, 0:HG]
                                q = 2 * e + c % 2
                                act.activation(o, i_, ACT.Relu, bias=bn_t[:, c // 2, q:q + 1],
                                               scale=bn_s[:, c // 2, q:q + 1]).then_inc(hid_ok, 1)
                            if e == 2 and c == 1:
                                act.wait_ge(wT_tr, g + 1)
                                act.activation(wT[:, 0:512], bank[7][0:NX, :], ACT.Copy)
                                act.activation(wT[:, 512:GC], bank[6][0:NX, 256:384], ACT.Copy).then_inc(wT_ok, 1)
                        if e == 0:
                            act.wait_ge(gate_in, g + 1)
                            act.activation(wf2[:, :, :], lg[:, :, :], ACT.Exp).then_inc(gate_exp, 1)
                        if not last and e == 4:
                            root(g + 2)

                root(1)
                with act.Fori(0, NG - 1) as g:
                    group(g, False)
                group(NG - 1, True)

            table(1)

            def copy_turned(i, b):
                act.wait_ge(st_tr[b], i + 1)
                act.activation(ST[b], bank[4 + b % 2][:, :], ACT.Copy).then_inc(st_ok[b], 1)

            def exponentials(i, b):
                act.wait_ge(e_in[b], LEAD + i + 1)
                act.activation(G2[b][:, :, D:AGG], ez[:, 0, b, :, :], ACT.Exp).then_inc(e_exp[b], 1)

            act.activation(pause[:, 1:2], eps_ln[:, 0:1], ACT.Exp)
            for b in range(2):
                act.wait_ge(t_out[b], RB + 2 * stores[b])
            for b in range(3):
                copy_turned(0, b)
            exponentials(0, 0)

            def act_round(i, last):
                for b in range(BUF):
                    if b < 3 or not last:
                        exponentials(i + (b + 1) // BUF, (b + 1) % BUF)
                    if b < 1 or not last:
                        copy_turned(i + (b + 3) // BUF, (b + 3) % BUF)

            with act.Fori(0, rounds4 - 1) as i:
                act_round(i, False)
            act_round(rounds4 - 1, True)

            experts()

        @block.vector
        def _(dve):
            step = Steps(dve, vec_step)

            def tile_stats(rows, t):
                return dve.bn_stats(stats[:, t, :], rows[:, t, :])

            def deviations(turn):
                for t in range(NT):
                    last = dve.bn_aggr(mv[:, t, :], stats[:, t, :])
                last.then_inc(t_stats, 1)
                dve.wait_ge(t_sqrt, turn)
                step.done(dve.reciprocal(rstd[:, 0:NT], rstd[:, 0:NT]))
                step.settle()
                dve.scalar_tensor_tensor(out=nbias[:, 0:NT], in0=mv[:, :, 0], scalar=-1.0, in1=rstd[:, 0:NT],
                                         op0=ALU.mult, op1=ALU.mult).then_inc(t_rstd, 1)

            def all_stats(turn):
                for t in range(NT):
                    last = tile_stats(X3, t)
                step.done(last)
                step.settle()
                deviations(turn)

            dve.wait_ge(const_set, NCONST)

            def count_to_place(count, nb, nc_, turn):
                step.done(dve.tensor_copy(totals[:, 0, 0:1], count[:, 0:1, nc_ - 1]))
                step.done(dve.tensor_copy(totals[:, 1, 0:nb], count[:, :, nc_ - 1]))
                step.settle()
                dve.tensor_tensor(totals[:, 0, 1:nb], totals[:, 1, 1:nb], totals[:, 1, 0:nb - 1],
                                  ALU.subtract).then_inc(tot_in, 1)
                dve.wait_ge(tot_ok, turn)
                step.done(dve.tensor_scalar(tiles_i[:, 0, 0:nb], bank[6][:, 32:32 + nb], float(P - 1), None, ALU.add))
                step.settle()
                step.done(dve.tensor_scalar(tiles_i[:, 1, 0:nb], tiles_i[:, 0, 0:nb], 7, None,
                                            ALU.arith_shift_right))
                step.settle()
                step.done(dve.tensor_copy(totals[:, 2, 0:nb], tiles_i[:, 1, 0:nb]))
                step.settle()
                step.done(dve.tensor_tensor_scan(totals[:, 3, 0:nb], ones[:, 0:nb], totals[:, 2, 0:nb], 0.0,
                                                 ALU.mult, ALU.add))
                step.settle()
                step.done(dve.tensor_tensor(totals[:, 4, 0:nb], totals[:, 3, 0:nb], totals[:, 2, 0:nb],
                                            ALU.subtract))
                step.settle()
                step.done(dve.scalar_tensor_tensor(out=totals[:, 5, 0:nb], in0=totals[:, 4, 0:nb], scalar=float(P),
                                                   in1=bank[6][:, 0:nb], op0=ALU.mult, op1=ALU.add))
                step.settle()
                step.done(dve.tensor_tensor(totals[:, 5, 1:nb], totals[:, 5, 1:nb], totals[:, 1, 0:nb - 1],
                                            ALU.subtract))
                step.settle()

            def masked_places(hot_, count, nb):
                for k in range(nb):
                    step.done(dve.scalar_tensor_tensor(out=hot_[:, k, :], in0=count[:, k, :],
                                                       scalar=totals[:, 5, k:k + 1], in1=hot_[:, k, :],
                                                       op0=ALU.add, op1=ALU.mult))
                step.settle()

            def bucket_of_tiles(n, nb, at, row, to):
                at = at.rearrange("p (t b) -> p t b", b=nb - 1)
                step.done(dve.tensor_tensor(at, iota_tile[0:1, 0:n].unsqueeze(2).to_broadcast([1, n, nb - 1]),
                                            totals[0:1, 4, 1:nb].unsqueeze(1).to_broadcast([1, n, nb - 1]), ALU.is_ge))
                step.settle()
                step.done(dve.tensor_reduce(row, at, AX, ALU.add))
                step.settle()
                step.done(dve.tensor_copy(to, row))
                step.settle()

            def keys(w):
                key = ints[w]
                other = ints[1 - w]
                a, b = ints[4], ints[5]
                step.done(dve.tensor_scalar(a, key, 7, None, ALU.arith_shift_right))
                step.done(dve.tensor_scalar(b, key, P - 1, None, ALU.bitwise_and))
                step.settle()
                step.done(dve.tensor_copy(bucket_f, a))
                step.settle()
                if w == 0:
                    step.done(dve.scalar_tensor_tensor(out=a, in0=other, scalar=float(NR), in1=ints[2],
                                                       op0=ALU.mult, op1=ALU.add))
                    step.settle()
                    step.done(dve.scalar_tensor_tensor(out=a, in0=a, scalar=float(P), in1=b,
                                                       op0=ALU.mult, op1=ALU.add))
                else:
                    step.done(dve.tensor_scalar(b, b, 1.0, None, ALU.add))
                    step.settle()
                    step.done(dve.scalar_tensor_tensor(out=a, in0=other, scalar=float(2 * P), in1=b,
                                                       op0=ALU.mult, op1=ALU.add))
                step.settle()
                if w == 0:
                    step.done(dve.tensor_copy(record[:, :, 0], a))
                    step.done(dve.tensor_copy(record[:, :, 1], ints[3]))
                else:
                    mask = (1 << PIECE) - 1
                    step.done(dve.tensor_scalar(b, a, mask, None, ALU.bitwise_and))
                    step.settle()
                    step.done(dve.tensor_copy(vals[:, 0, :], b))
                    step.settle()
                    step.done(dve.tensor_scalar(b, a, PIECE, mask, ALU.logical_shift_right, ALU.bitwise_and))
                    step.settle()
                    step.done(dve.tensor_copy(vals[:, 1, :], b))
                step.done(dve.tensor_tensor(onehot_b3, bucket_f.unsqueeze(1).to_broadcast([P, NB, EC]),
                                            iota_b[:, :].unsqueeze(2).to_broadcast([P, NB, EC]), ALU.is_equal))
                step.settle()
                step.done(dve.tensor_tensor_scan(count_b, ones[:, 0:1].to_broadcast([P, NB * EC]), onehot_b, 0.0,
                                                 ALU.mult, ALU.add))
                step.settle()
                count_to_place(count_b3, NB, EC, w + 1)
                masked_places(onehot_b3, count_b3, NB)
                step.done(dve.tensor_reduce(bucket_f, onehot_b.rearrange("p (b c) -> p c b", c=EC), AX, ALU.add))
                step.settle()
                step.done(dve.tensor_scalar(a, bucket_f, -1.0, None, ALU.add))
                step.settle()
                step.done(dve.tensor_scalar(b, a, P - 1, None, ALU.bitwise_and))
                step.settle()
                step.done(dve.tensor_copy(slot_f[:, :], b))
                step.settle()
                step.done(dve.tensor_scalar(b, a, 7, None, ALU.arith_shift_right))
                step.settle()
                step.done(dve.tensor_copy(tile_f[:, :], b))
                if w == 0:
                    step.settle()
                    step.done(dve.scalar_tensor_tensor(out=slot_f[:, :], in0=slot_f[:, :], scalar=float(T),
                                                       in1=tile_f[:, :], op0=ALU.mult, op1=ALU.add))
                    step.settle()
                    step.done(dve.scalar_tensor_tensor(out=tile_f[:, :], in0=bucket_f, scalar=0.0, in1=dump[:, :],
                                                       op0=ALU.is_equal, op1=ALU.mult))
                    step.settle()
                    dve.tensor_tensor(place0[:, :], slot_f[:, :], tile_f[:, :], ALU.add).then_inc(record_ok, 1)
                bucket_of_tiles(T, NB, arena[0:1, 0:T * (NB - 1)], arena[0:1, T * NB:T * NB + T],
                                bucket_row[w][:, 0:T])

            def sort1():
                def group(j):
                    for u in range(4):
                        c = j * 4 + u
                        dve.wait_ge(oh_used[u], LEAD + j)
                        if u < 2:
                            dve.tensor_scalar(tile_oh[u], iota_tile[:, :], tile_f[:, ds(c, 1)], None, ALU.is_equal)
                        for f in range(2):
                            last = dve.tensor_scalar(slot_oh[u][:, f * P:(f + 1) * P], iota_slot[:, :],
                                                     slot_f[:, ds(c, 1)], vals[:, f, ds(c, 1)],
                                                     ALU.is_equal, ALU.mult)
                        last.then_inc(oh_ready, 1)

                with dve.Fori(0, EC // 4) as j:
                    group(j)
                for u in range(4):
                    dve.wait_ge(oh_used[u], LEAD + EC // 4)

                step.done(dve.tensor_copy(wordf[0], bank[0][:, 0:T]))
                step.settle()
                step.done(dve.scalar_tensor_tensor(out=words[:, 0, :], in0=bank[1][:, 0:T], scalar=float(1 << PIECE),
                                                   in1=wordf[0], op0=ALU.mult, op1=ALU.add))
                step.settle()
                step.done(dve.tensor_scalar(idx1[:, 0:T], words[:, 0, :], 8, None, ALU.logical_shift_right))
                step.done(dve.tensor_scalar(words[:, 1, :], words[:, 0, :], 2 * P - 1, None, ALU.bitwise_and))
                step.settle()
                dve.tensor_scalar(loc1[:, 0:T], words[:, 1, :], -1.0, None, ALU.add).then_inc(order_ok, 1)

            def decode0():
                dve.wait_ge(sorted_in, 16)
                step.done(dve.tensor_scalar(idx0[:, 0:T], sorted_sb[:, :, 0], 7, None, ALU.logical_shift_right))
                step.done(dve.tensor_scalar(words[:, 1, :], sorted_sb[:, :, 0], P - 1, None, ALU.bitwise_and))
                step.done(dve.tensor_copy(wgt0[:, 0:T], sorted_sb[:, :, 1]))
                step.settle()
                dve.tensor_copy(loc0[:, 0:T], words[:, 1, :]).then_inc(order_ok, 1)

            dve.wait_ge(edges_in, 16 * 8)
            keys(0)
            dve.wait_ge(x_in, 32)
            all_stats(1)
            keys(1)
            dve.memset(pause[:, 1:2], 0.0).then_inc(places_ok, 1)
            sort1()
            dve.wait_ge(bn_sq, 2)
            step.done(dve.reciprocal(bn_s[:, :, :], bn_s[:, :, :]))
            step.settle()
            for j, (cb, cg, cbe, cm) in enumerate(((0, 16, 32, 48), (80, 96, 112, 128))):
                step.done(dve.tensor_tensor(bn_s[:, j, :], bn_s[:, j, :], par[:, cg:cg + 16], ALU.mult))
                step.done(dve.tensor_tensor(bn_t[:, j, :], par[:, cb:cb + 16], par[:, cm:cm + 16], ALU.subtract))
                step.settle()
                step.done(dve.tensor_tensor(bn_t[:, j, :], bn_t[:, j, :], bn_s[:, j, :], ALU.mult))
                step.settle()
                step.done(dve.tensor_tensor(bn_t[:, j, :], bn_t[:, j, :], par[:, cbe:cbe + 16], ALU.add))

            regs = [dve.alloc_register(f"dve_b{k}") for k in range(BUF * UG)]

            def buckets(w, i):
                dve.load(regs, bucket_row[w][0:1, ds(i * (BUF * UG), BUF * UG)])
                return [dve.snap(r, min_val=0, max_val=NB - 1) for r in regs]

            decode0()
            dve.wait_ge(order_ok, 2)
            wgt0_f = wgt0[:, :].bitcast(F32)

            def weighted(i, b, fresh=False):
                if not fresh:
                    dve.wait_ge(g_used[b], LEAD + i)
                for u in range(UG):
                    c = i * (BUF * UG) + (b * UG + u)
                    last = dve.tensor_scalar(S[b][:, u, :], iota_p[:, :], loc0[:, ds(c, 1)], wgt0_f[:, ds(c, 1)],
                                             ALU.is_equal, ALU.mult)
                last.then_inc(s_ready, 1)

            def add_up(i, b, bs):
                dve.wait_ge(g_used[b], LEAD + i + 1)
                for u in range(UG):
                    if u:
                        dve.wait_ge(acc_ok[b], LEAD + i * UG + u)
                    else:
                        dve.wait_ge(acc_ok[(b - 1) % BUF], LEAD + i * UG + (UG if b else 0))
                    t = X[:, ds(bs[b * UG + u] * D, D)]
                    dve.tensor_tensor(t, t, bank[2 * b + u // 2][:, (u % 2) * D:(u % 2 + 1) * D],
                                      ALU.add).then_inc(acc_ok[b], 1)

            for b in range(2):
                dve.wait_ge(t_out[b], RB + stores[b])
            for b in range(2):
                weighted(0, b, True)

            def edge_round(i, first, last):
                bs = buckets(0, i)
                for b in range(BUF):
                    if b < 2 or not last:
                        weighted(i + (b + 2) // BUF, (b + 2) % BUF, first and b < 2)
                    add_up(i, b, bs)

            edge_round(0, True, False)
            with dve.Fori(1, rounds4 - 1) as i:
                edge_round(i, False, False)
            edge_round(rounds4 - 1, False, True)
            for b in range(BUF):
                dve.wait_ge(acc_ok[b], LEAD + rounds4 * UG)

            def ln(g):
                for t in range(GT):
                    last = dve.bn_stats(stats[:, t, :], X[:, ds((g * GT + t) * D, D)])
                step.done(last)
                step.settle()
                dve.memset(pause[:, 1:2], 0.0)
                for t in range(GT):
                    last = dve.bn_aggr(mv[:, t, :], stats[:, t, :])
                last.then_inc(ln_var, 1)
                dve.wait_ge(ln_sd, g + 1)
                step.done(dve.reciprocal(rstd[:, 0:GT], rstd[:, 0:GT]))
                step.settle()
                for t in range(GT):
                    last = dve.tensor_scalar(xn[:, t, :], X[:, ds((g * GT + t) * D, D)], mv[:, t, 0:1],
                                             rstd[:, t:t + 1], ALU.subtract, ALU.mult)
                last.then_inc(xn_ok, 1)

            all_stats(2)
            for t in range(NT):
                dve.wait_ge(x1_ok, t + 1)
                last = tile_stats(XN3, t)
            step.done(last)
            step.settle()
            deviations(3)

            def scaled(g):
                for t in range(GT):
                    row = XN_all[:, ds((g * GT + t) * D, D)]
                    step.done(dve.scalar_tensor_tensor(out=row, in0=row, scalar=mv[:, ds(g * GT + t, 1), 0],
                                                       in1=gamma_b, op0=ALU.subtract, op1=ALU.mult))
                step.settle()
                for t in range(GT):
                    row = XN_all[:, ds((g * GT + t) * D, D)]
                    last = dve.scalar_tensor_tensor(out=row, in0=row, scalar=rstd[:, ds(g * GT + t, 1)],
                                                    in1=beta_b, op0=ALU.mult, op1=ALU.add)
                last.then_inc(xn_ok, 1)

            def choose(g):
                dve.wait_ge(logit_ok, g + 1)
                dve.tensor_tensor(lg[:, :, :], bank[7][:, 0:GT * NX].rearrange("p (t e) -> p t e", e=NX),
                                  br_b[0].unsqueeze(1).to_broadcast([P, GT, NX]), ALU.add).then_inc(lg_ok, 1)
                dve.wait_ge(lg_ok, LEAD + g + 1)
                dve.memset(pause[:, 1:2], 0.0)
                for t in range(GT):
                    step.done(dve.max(top[:, t, :], lg[:, t, :]))
                step.settle()
                dve.memset(pause[:, 1:2], 0.0)
                for t in range(GT):
                    step.done(dve.max_index(topi[:, t, :], top[:, t, :], lg[:, t, :]))
                step.settle()
                step.done(dve.tensor_copy(TF[:, ds(g * GT, GT), :], topi[:, :, 0:2]))
                step.done(dve.tensor_tensor(D12[:, 0, ds(g * GT, GT)], top[:, :, 1], top[:, :, 0], ALU.subtract))
                step.settle()

            scaled(0)
            scaled(1)
            with dve.Fori(0, NG - 2) as g:
                step.enter(g, GT + 2 * GT + 2)
                scaled(g + 2)
                choose(g)
            step.leave(NG - 2)
            choose(NG - 2)
            choose(NG - 1)
            dve.memset(pause[:, 1:2], 0.0).then_inc(w_in, 1)

            for k in range(2):
                step.done(dve.tensor_tensor(hot[:, k, :, :], TF[:, :, k].unsqueeze(1).to_broadcast([P, NX, NT]),
                                            iota_x[:, :].unsqueeze(2).to_broadcast([P, NX, NT]), ALU.is_equal))
            step.settle()
            hot_f = [hot[:, k, :, :].rearrange("p e t -> p (e t)") for k in range(2)]
            step.done(dve.tensor_tensor(hot_sum, hot_f[0], hot_f[1], ALU.add))
            step.settle()
            step.done(dve.tensor_tensor_scan(hot_count, ones[:, 0:1].to_broadcast([P, NX * NT]), hot_sum, 0.0,
                                             ALU.mult, ALU.add))
            step.settle()
            hot_count3 = hot_count.rearrange("p (e t) -> p e t", t=NT)
            count_to_place(hot_count3, NX, NT, 3)
            for k in range(2):
                masked_places(hot[:, k, :, :], hot_count3, NX)
                step.done(dve.tensor_reduce(hot_sum[:, k * NT:(k + 1) * NT],
                                            hot[:, k, :, :].rearrange("p e t -> p t e"), AX, ALU.add))
                step.settle()
                last = dve.tensor_scalar(place_x[:, k, :], hot_sum[:, k * NT:(k + 1) * NT], -1.0, 0.0,
                                         ALU.add, ALU.max)
            last.then_inc(place_ok, 1)
            bucket_of_tiles(TE, NX, work[0:1, 9280:9280 + TE * (NX - 1)], work[0:1, 9700:9700 + TE],
                            expert_row[:, 0:TE])
            dve.memset(pause[:, 1:2], 0.0).then_inc(experts_ok, 1)
            dve.wait_ge(w_exp, 1)
            step.done(dve.tensor_scalar(D12[:, 0, :], D12[:, 1, :], 1.0, None, ALU.add))
            step.settle()
            step.done(dve.reciprocal(W12[:, :, 0], D12[:, 0, :]))
            step.settle()
            step.done(dve.tensor_tensor(W12[:, :, 1], W12[:, :, 0], D12[:, 1, :], ALU.mult))
            step.settle()

            dve.wait_ge(wg_in, 16)
            for k in range(KD):
                for j, a in enumerate((ar_b, al_b)):
                    step.done(dve.tensor_tensor(prod, Wg_sb[:, k, 0:D], a, ALU.mult))
                    step.settle()
                    step.done(dve.tensor_reduce(Wg_sb[:, k, D + j * NH:D + (j + 1) * NH],
                                                prod.rearrange("p (h d) -> p h d", d=DH), AX, ALU.add))
                    step.settle()
            dve.memset(pause[:, 1:2], 0.0).then_inc(wa_ok, 1)

            e_regs = [dve.alloc_register(f"dve_e{k}") for k in range(3)]

            def hidden_bias(i, b, e):
                dve.wait_ge(l1_mm, i + 1)
                wait_from(dve, h_tr, i - 1)
                dve.tensor_tensor(hp[b], bank[b][:, 0:H0], b1_b[:, ds(e * H0, H0)], ALU.add).then_inc(hb_ok, 1)

            def turned_hidden(i, b):
                dve.wait_ge(h_tr, i + 1)
                wait_from(dve, l2_mm, i - 1)
                dve.tensor_copy(hT[b], bank[2 + b][:, 0:H0]).then_inc(hT_ok, 1)

            def outputs(i, b, e, out_at):
                dve.wait_ge(l2_mm, i + 1)
                wait_from(dve, ys_out[b], out_at)
                dve.tensor_tensor(ys[b], bank[4 + b][:, 0:D], b2_b[:, ds(e * D, D)], ALU.add).then_inc(ye_ok, 1)

            def expert_round(j, last):
                dve.load(e_regs, expert_row[0:1, ds(j * 2, 3)])
                es = [dve.snap(r, min_val=0, max_val=NX - 1) for r in e_regs]
                for b in range(2):
                    i = j * 2 + b
                    turned_hidden(i, b)
                    if b == 0 or not last:
                        hidden_bias(i + 1, 1 - b, es[b + 1])
                    outputs(i, b, es[b], j * 16)

            dve.wait_ge(bias_in, 32)
            dve.load(e_regs, expert_row[0:1, 0:3])
            hidden_bias(0, 0, dve.snap(e_regs[0], min_val=0, max_val=NX - 1))
            expert_round(0, False)
            with dve.Fori(1, ER - 1) as j:
                expert_round(j, False)
            expert_round(ER - 1, True)

            for n in range(2 * NT):
                t, k = n // 2, n % 2
                dve.wait_ge(yg_in[n % RING], 16 * (n // RING + 1))
                if n:
                    dve.wait_ge(comb_ok, n)
                if k == 0 and t:
                    dve.bn_stats(stats[:, t - 1, :], X3[:, t - 1, :])
                dve.scalar_tensor_tensor(out=X3[:, t, :], in0=ring[n % RING], scalar=W12[:, t, k:k + 1],
                                         in1=X3[:, t, :], op0=ALU.mult, op1=ALU.add).then_inc(comb_ok, 1)
            dve.wait_ge(comb_ok, 2 * NT)
            step.done(dve.bn_stats(stats[:, NT - 1, :], X3[:, NT - 1, :]))
            step.settle()

            def experts():
                yslot = [bank[4 + t // 2][:, (t % 2) * D:(t % 2 + 1) * D] for t in range(GT)]

                def gates(g):
                    dve.wait_ge(logit_ok, g + (NG + 1))
                    logits = bank[7][:, 0:GT * NX].rearrange("p (t e) -> p t e", e=NX)
                    step.done(dve.tensor_tensor(lg[:, :, :], logits,
                                                br_b[1].unsqueeze(1).to_broadcast([P, GT, NX]), ALU.add))
                    step.settle()
                    step.done(dve.tensor_reduce(gsm[:, 0, :], lg[:, :, :], AX, ALU.max))
                    step.settle()
                    dve.tensor_tensor(lg[:, :, :], lg[:, :, :], gsm[:, 0, :].unsqueeze(2).to_broadcast([P, GT, NX]),
                                      ALU.subtract).then_inc(gate_in, 1)
                    dve.wait_ge(gate_exp, g + 1)
                    step.done(dve.tensor_reduce(gsm[:, 1, :], wf2[:, :, :], AX, ALU.add))
                    step.settle()
                    step.done(dve.reciprocal(gsm[:, 2, :], gsm[:, 1, :]))
                    step.settle()
                    dve.tensor_tensor(wf[:, :, :], wf2[:, :, :], gsm[:, 2, :].unsqueeze(2).to_broadcast([P, GT, NX]),
                                      ALU.mult).then_inc(gate_ok, 1)
                    dve.wait_ge(gate_ok, g + 1)

                def group(g, last):
                    gates(g)
                    for e in range(NX + 1):
                        for t in range(GT):
                            n = 5 * e + t
                            xt = X[:, ds((g * GT + t) * D, D)]
                            dve.wait_ge(y_mm, LEAD + g * YM + (len(UNITS) * e + t // 2 + 1))
                            if e:
                                dve.wait_ge(y_ok, LEAD + g * YT + (n - GT + 1))
                            if e < NX:
                                dve.scalar_tensor_tensor(out=xt, in0=yslot[t], scalar=wf[:, t, e:e + 1], in1=xt,
                                                         op0=ALU.mult, op1=ALU.add).then_inc(y_ok, 1)
                            else:
                                dve.tensor_tensor(xt, yslot[t], xt, ALU.add).then_inc(y_ok, 1)
                        if e == 3 and not last:
                            dve.wait_ge(xn_tr, g + (NG + 1))
                            ln(g + 1)

                ln(0)
                add_neighbours(GT, NT)
                with dve.Fori(0, NG - 1) as g:
                    step.enter(g, 4 + 2)
                    group(g, False)
                step.leave(NG - 1)
                group(NG - 1, True)

            deviations(4)

            def copy_hr(i, b):
                dve.wait_ge(t_ev[0], LEAD + i + (NT + 1))
                dve.tensor_copy(HRL[:, ds(i, 1), :], tb1[b][:, D:WG].unsqueeze(1)).then_inc(hrl_ok, 1)

            with dve.Fori(0, NT // 2) as i:
                copy_hr(i * 2, 0)
                copy_hr(i * 2 + 1, 1)
            copy_hr(NT - 1, 0)
            dve.wait_ge(hrl_ok, LEAD + NT)

            def others(i, b, fresh=False):
                if not fresh:
                    dve.wait_ge(m_mm[b], LEAD + i)
                dve.tensor_tensor(notS[b], iota_p[:, :].unsqueeze(1).to_broadcast([P, UG, P]),
                                  loc1[:, ds(i * (BUF * UG) + b * UG, UG)].unsqueeze(2).to_broadcast([P, UG, P]),
                                  ALU.not_equal).then_inc(nots_ok, 1)

            def reduce_tile(i, b, u):
                dve.tensor_reduce(tmx[:, b, u, :], bank[4 * (b % 2) + u][:, :].rearrange("p (h j) -> p h j", j=P),
                                  AX, ALU.max).then_inc(m_red[b], 1)

            def keep_maxima(i, b, u, bs):
                dve.wait_ge(m_red[b], LEAD + i * UG + u + 1)
                dve.wait_ge(m_ok, LEAD + i * (BUF * UG) + (b * UG + u))
                m = M[:, ds(bs[b * UG + u] * NH, NH)]
                dve.tensor_tensor(m, m, tmx[:, b, u, :], ALU.max).then_inc(m_ok, 1)

            def maxima_round(i, first, last):
                bs = buckets(1, i)
                for b in range(BUF):
                    dve.wait_ge(m_mm[b], LEAD + i + 1)
                    reduce_tile(i, b, 0)
                    for u in range(1, UG):
                        reduce_tile(i, b, u)
                        keep_maxima(i, b, u - 1, bs)
                    if b < 2 or not last:
                        others(i + (b + 2) // BUF, (b + 2) % BUF, first and b < 2)
                    keep_maxima(i, b, UG - 1, bs)

            for b in range(2):
                others(0, b, True)
            maxima_round(0, True, False)
            with dve.Fori(1, rounds4 - 1) as i:
                maxima_round(i, False, False)
            maxima_round(rounds4 - 1, False, True)
            dve.wait_ge(m_ok, LEAD + T)

            M3 = M[:, :].rearrange("p (t h) -> p t h", h=NH)
            R3 = R[:, :].rearrange("p (t h) -> p t h", h=2 * NH)
            step.done(dve.memset(ACC, 0.0))
            step.done(dve.tensor_copy(R3[:, :, 0:NH], HRL[:, :, NH:2 * NH]))
            step.settle()
            step.done(dve.tensor_tensor(M3, M3, HRL[:, :, NH:2 * NH], ALU.add))
            step.settle()
            dve.scalar_tensor_tensor(out=R3[:, :, NH:2 * NH], in0=M3, scalar=SLOPE, in1=M3, op0=ALU.mult,
                                     op1=ALU.max).then_inc(r_ready, 1)

            def targets(i, b):
                dve.tensor_tensor(S2[b], iota_p[:, :].unsqueeze(1).to_broadcast([P, UG, P]),
                                  loc1[:, ds(i * (BUF * UG) + b * UG, UG)].unsqueeze(2).to_broadcast([P, UG, P]),
                                  ALU.is_equal).then_inc(s2_ready[b], 1)

            def logit_steps(i, b):
                re = bank[6 + b % 2][:, 0:UG * 2 * NH].rearrange("p (u h) -> p u h", h=2 * NH)
                z, y = ez[:, 1, b, :, :], ez[:, 0, b, :, :]

                def plus():
                    dve.wait_ge(g2_in[b], i * 64 + 64)
                    dve.wait_ge(re_mm, i * BUF + (b + 1))
                    step.done(dve.tensor_tensor(z, re[:, :, 0:NH], G2[b][:, :, D:AGG], ALU.add))

                def leaky():
                    step.settle()
                    step.done(dve.scalar_tensor_tensor(out=y, in0=z, scalar=SLOPE, in1=z, op0=ALU.mult, op1=ALU.max))

                def less_max():
                    step.settle()
                    step.done(dve.tensor_tensor(z, y, re[:, :, NH:2 * NH], ALU.subtract))

                def bounded():
                    step.settle()
                    dve.tensor_scalar(y, z, 1.0, None, ALU.min).then_inc(e_in[b], 1)
                return plus, leaky, less_max, bounded

            def messages(i, b):
                dve.wait_ge(e_exp[b], LEAD + i + 1)
                g4 = G2[b][:, :, 0:D].rearrange("p u (h d) -> p u h d", d=DH)
                w4 = G2[b][:, :, D:AGG].unsqueeze(3).to_broadcast([P, UG, NH, DH])
                dve.tensor_tensor(g4, g4, w4, ALU.mult).then_inc(msg_ok, 1)

            def add_sum(i, b, u, bucket):
                dve.wait_ge(acc2_mm[b], LEAD + i * UG + (u + 1))
                if u:
                    dve.wait_ge(acc2_ok[b], LEAD + i * UG + u)
                else:
                    dve.wait_ge(acc2_ok[(b - 1) % BUF], LEAD + i * UG + (UG if b else 0))
                t = ACC[:, ds(bucket * AGG, AGG)]
                dve.tensor_tensor(t, t, bank[u][:, 0:AGG], ALU.add).then_inc(acc2_ok[b], 1)

            def sum_buckets(n, at):
                dve.load(regs[0:n], bucket_row[1][0:1, at])
                return [dve.snap(r, min_val=0, max_val=NB - 1) for r in regs[0:n]]

            for b in range(3):
                targets(0, b)
            for part in logit_steps(0, 0):
                part()

            def sum_round(i, bs, first, last):
                for b in range(BUF):
                    messages(i, b)
                    adds = not (first and b == 0)
                    parts = logit_steps(i + (b + 1) // BUF, (b + 1) % BUF) if b < 3 or not last else (None,) * UG
                    for u, part in enumerate(parts):
                        if adds:
                            add_sum(i if b else i + (-1), (b - 1) % BUF, u, bs[b * UG + u])
                        if part:
                            part()
                        if u == UG - 1 and (b < 1 or not last):
                            dve.wait_ge(acc2_mm[(b - 1) % BUF], LEAD + i * UG + (UG if b else 0))
                            targets(i + (b + 3) // BUF, (b + 3) % BUF)

            bs = sum_buckets(3 * UG, slice(0, 3 * UG))
            sum_round(0, [None] * UG + bs, True, False)
            with dve.Fori(1, rounds4 - 1) as i:
                step.enter(i + (-1), 3 * BUF)
                sum_round(i, sum_buckets(BUF * UG, ds(i * (BUF * UG) + (-UG), BUF * UG)), False, False)
            step.leave(rounds4 - 2)
            end = T - UG
            sum_round(rounds4 - 1, sum_buckets(BUF * UG, slice(end - BUF * UG, end)), False, True)
            bs = sum_buckets(UG, slice(end, T))
            for u in range(UG):
                add_sum(rounds4 - 1, BUF - 1, u, bs[u])
            for b in range(BUF):
                dve.wait_ge(acc2_ok[b], LEAD + rounds4 * UG)
            acc3 = ACC.rearrange("p (t r) -> p t r", r=AGG)
            step.done(dve.tensor_scalar(M3, acc3[:, :, D:AGG], 1e-30, None, ALU.max))
            step.settle()
            step.done(dve.reciprocal(M[:, :], M[:, :]))
            step.settle()

            def add_neighbours(a, b):
                for h in range(NH):
                    part = acc3[:, a:b, h * DH:(h + 1) * DH]
                    step.done(dve.tensor_tensor(part, part, M3[:, a:b, h:h + 1].to_broadcast([P, b - a, DH]),
                                                ALU.mult))
                step.settle()
                step.done(dve.tensor_tensor(X3[:, a:b, :], X3[:, a:b, :], acc3[:, a:b, 0:D], ALU.add))
                step.settle()

            add_neighbours(0, GT)
            experts()


_INS = ['x', 'src', 'dst', 'edge_type_8', 'edge_weight', 'L0_gnn_weight', 'L0_ffn_gamma', 'L0_ffn_beta',
        'L0_ffn_Wr', 'L0_ffn_br', 'L0_ffn_W1', 'L0_ffn_b1', 'L0_ffn_W2', 'L0_ffn_b2', 'L1_gnn_W', 'L1_gnn_a_l',
        'L1_gnn_a_r', 'L1_ffn_Wr', 'L1_ffn_br', 'L1_ffn_W1', 'L1_ffn_b1', 'L1_ffn_g1', 'L1_ffn_be1', 'L1_ffn_m1',
        'L1_ffn_v1', 'L1_ffn_W2', 'L1_ffn_b2', 'L1_ffn_g2', 'L1_ffn_be2', 'L1_ffn_m2', 'L1_ffn_v2', 'L1_ffn_Wo',
        'L1_ffn_bo']
_OUTS = [((3125, 256), 'float32')]


def kernel(**inputs):
    import numpy as _np
    import concourse.bacc as _bacc
    from concourse import mybir as _mybir
    from concourse.bass_utils import run_bass_kernel_spmd as _run

    nc = _bacc.Bacc("TRN2", target_bir_lowering=False, num_devices=1)
    arrays, args = {}, []
    for name in _INS:
        a = _np.ascontiguousarray(inputs[name])
        arrays[f"in_{name}_dram"] = a
        args.append(nc.dram_tensor(f"in_{name}_dram", a.shape, _mybir.dt.from_np(a.dtype), kind="ExternalInput").ap())
    for i, (shape, dtype) in enumerate(_OUTS):
        dt = _mybir.dt.from_np(_np.dtype(dtype))
        args.append(nc.dram_tensor(f"out_{i}_dram", shape, dt, kind="ExternalOutput").ap())
    program(nc, *args)
    r = _run(nc, [arrays], core_ids=[0])
    got = tuple(r.results[0][f"out_{i}_dram"] for i in range(len(_OUTS)))
    return got[0]
```
